# Optimizing a Trainium2 kernel written in Bass

```python
import numpy as np
import jax
import jax.numpy as jnp

def _softmax(x, axis=-1):
    return jax.nn.softmax(x, axis=axis)

def _gelu(x):
    return jax.nn.gelu(x, approximate=True)

def _silu(x):
    return jax.nn.silu(x)

def _sigmoid(x):
    return jax.nn.sigmoid(x)

def _layernorm(x, axis=-1, eps=1e-05):
    m = jnp.mean(x, axis=axis, keepdims=True)
    v = jnp.var(x, axis=axis, keepdims=True)
    return (x - m) / jnp.sqrt(v + eps)

def _scatter_add(tgt, idx, src, axis=0):
    return tgt.at[idx].add(src)

def _segment_sum(src, seg, n):
    return jax.ops.segment_sum(src, seg, n)
kernel_name = 'mk_xattn_seq_d4_seqx_r4_bdf79a'

def setup_inputs(seed: int=0):
    np.random.seed(seed)
    _w = jnp.asarray

    def _rec_inputs():
        import jax
        import jax.numpy as jnp
        _rk = jax.random.key(seed)
        x = -0.0002928 + 1 * jax.random.normal(jax.random.fold_in(_rk, 1), (32, 112, 256), jnp.float32)
        _lenS = 112 - jax.random.randint(jax.random.fold_in(_rk, 7), (32,), 0, max(1, 112 // 4) + 1, jnp.int32)
        _lenS2 = 375 - jax.random.randint(jax.random.fold_in(_rk, 8), (32,), 0, max(1, 375 // 4) + 1, jnp.int32)
        _ctx_1024P = jax.random.normal(jax.random.fold_in(_rk, 11), (32, 16, 256), jnp.float32)
        _ctx_1024c = jax.random.dirichlet(jax.random.fold_in(_rk, 511), 0.3 * jnp.ones((16,), jnp.float32), (32, 375))
        _ctx_1024t = jnp.einsum('bsk,bkd->bsd', _ctx_1024c, _ctx_1024P)
        _ctx_1024t = _ctx_1024t * jax.lax.rsqrt(jnp.mean(jnp.square(_ctx_1024t)) + 1e-12) * 0.953939
        ctx_1024 = 4.13588e-05 + 0.999923 * (_ctx_1024t + 0.3 * jax.random.normal(jax.random.fold_in(_rk, 611), (32, 375, 256), jnp.float32))
        _validS = jnp.arange(112)[None, :] < _lenS[:, None]
        _validS2 = jnp.arange(375)[None, :] < _lenS2[:, None]
        _causal = jnp.tril(jnp.ones((112, 112), dtype=bool))
        mask_BxSxS_ik0 = jnp.where(jnp.broadcast_to(_validS[:, None, :], (32, 112, 112)), 0, 1).astype(jnp.int32)
        mask_BxSxS2_if1 = jnp.where(jnp.ones((32, 112, 375), dtype=bool), 1, 0).astype(jnp.int32)
        return (x, ctx_1024, mask_BxSxS_ik0, mask_BxSxS2_if1)
    x, ctx_1024, mask_BxSxS_ik0, mask_BxSxS2_if1 = _rec_inputs()

    def _L0_xattn_setup():
        import jax, jax.numpy as jnp
        import numpy as np
        D_MODEL = 256
        NUM_HEADS = 16
        HEAD_DIM = D_MODEL // NUM_HEADS
        SCALE = HEAD_DIM ** (-0.5)
        LN_EPS = 1e-05
        Q_EPS = 1e-05

        def bit_quant(W):
            gamma = jnp.mean(jnp.abs(W))
            Wq = jnp.clip(jnp.round(W / (gamma + Q_EPS)), -1.0, 1.0) * gamma
            return W + jax.lax.stop_gradient(Wq - W)

        def layer_norm(x, gamma, beta):
            mu = jnp.mean(x, axis=-1, keepdims=True)
            var = jnp.mean(jnp.square(x - mu), axis=-1, keepdims=True)
            return (x - mu) * jax.lax.rsqrt(var + LN_EPS) * gamma + beta
        key = jax.random.key(seed)
        ks = jax.random.split(key, 8)
        B, T, T_ctx, C = (4, 256, 512, D_MODEL)
        w_std = C ** (-0.5)
        return {'x': jax.random.normal(ks[0], (B, T, C), jnp.float32), 'context': jax.random.normal(ks[1], (B, T_ctx, C), jnp.float32), 'Wq': jax.random.normal(ks[2], (C, C), jnp.float32) * w_std, 'bq': jnp.zeros((C,), jnp.float32), 'Wk': jax.random.normal(ks[3], (C, C), jnp.float32) * w_std, 'bk': jnp.zeros((C,), jnp.float32), 'Wv': jax.random.normal(ks[4], (C, C), jnp.float32) * w_std, 'bv': jnp.zeros((C,), jnp.float32), 'Wo': jax.random.normal(ks[5], (C, C), jnp.float32) * w_std, 'bo': jnp.zeros((C,), jnp.float32), 'ln_gamma': jnp.ones((C,), jnp.float32), 'ln_beta': jnp.zeros((C,), jnp.float32)}
    _L0_xattn_all = _L0_xattn_setup()
    _L0_xattn_in = {k: v for k, v in _L0_xattn_all.items() if k in ('Wq', 'bq', 'Wk', 'bk', 'Wv', 'bv', 'Wo', 'bo', 'ln_gamma', 'ln_beta')}
    del _L0_xattn_all

    def _L1_xattn_setup():
        import jax, jax.numpy as jnp
        import numpy as np
        B, T, S_ENC, D, H, E, K = (4, 256, 64, 256, 16, 8, 2)
        DK = D // H
        HID = 4 * D
        NEG = -65504.0
        EPS = 1e-05

        def rmsnorm(x, w):
            return w * (x * jax.lax.rsqrt(jnp.mean(x * x, axis=-1, keepdims=True) + EPS))

        def mha(xq, xk, xv, mask, wq, wk, wv, wo):
            q = jnp.einsum('bsd,ed->bse', xq, wq).reshape(xq.shape[0], -1, H, DK).transpose(0, 2, 1, 3)
            k = jnp.einsum('bsd,ed->bse', xk, wk).reshape(xk.shape[0], -1, H, DK).transpose(0, 2, 1, 3)
            v = jnp.einsum('bsd,ed->bse', xv, wv).reshape(xv.shape[0], -1, H, DK).transpose(0, 2, 1, 3)
            scores = jnp.einsum('bhqd,bhkd->bhqk', q, k) / jnp.sqrt(jnp.float32(DK))
            scores = jnp.where(mask[:, None, :, :] == 0, NEG, scores)
            attn = jax.nn.softmax(scores, axis=-1)
            out = jnp.einsum('bhqk,bhkd->bhqd', attn, v)
            out = out.transpose(0, 2, 1, 3).reshape(xq.shape[0], -1, D)
            return jnp.einsum('bsd,ed->bse', out, wo)

        def moe_ffn(x, gate_w, exp_w1, exp_w2, sh_w1, sh_w2):
            b, s, d = x.shape
            xf = x.reshape(-1, d)
            sh = jnp.einsum('nd,hd->nh', xf, sh_w1)
            sh = jax.nn.silu(sh)
            sh = jnp.einsum('nh,dh->nd', sh, sh_w2)
            logits = jnp.einsum('nd,ed->ne', xf, gate_w)
            topk_vals, topk_idx = jax.lax.top_k(logits, K)
            topk_gates = jax.nn.softmax(topk_vals, axis=-1)
            n = xf.shape[0]
            gates = jnp.zeros((n, E), dtype=xf.dtype).at[jnp.arange(n)[:, None], topk_idx].set(topk_gates)
            h = jnp.einsum('nd,ehd->neh', xf, exp_w1)
            h = jax.nn.silu(h)
            eo = jnp.einsum('neh,edh->ned', h, exp_w2)
            sel = jnp.einsum('ned,ne->nd', eo, gates)
            return (sh + sel).reshape(b, s, d)
        key = jax.random.key(seed)
        ks = jax.random.split(key, 16)
        sd = 1.0 / np.sqrt(D)
        inp = {'x': jax.random.normal(ks[0], (B, T, D), jnp.float32), 'encoder_output': jax.random.normal(ks[1], (B, S_ENC, D), jnp.float32), 'tgt_mask': jnp.tril(jnp.ones((T, T), jnp.int32))[None].repeat(B, 0), 'src_mask': jnp.ones((B, T, S_ENC), jnp.int32), 'norm1_w': jnp.ones((D,), jnp.float32), 'norm2_w': jnp.ones((D,), jnp.float32), 'norm3_w': jnp.ones((D,), jnp.float32), 'sa_wq': jax.random.normal(ks[2], (D, D), jnp.float32) * sd, 'sa_wk': jax.random.normal(ks[3], (D, D), jnp.float32) * sd, 'sa_wv': jax.random.normal(ks[4], (D, D), jnp.float32) * sd, 'sa_wo': jax.random.normal(ks[5], (D, D), jnp.float32) * sd, 'ca_wq': jax.random.normal(ks[6], (D, D), jnp.float32) * sd, 'ca_wk': jax.random.normal(ks[7], (D, D), jnp.float32) * sd, 'ca_wv': jax.random.normal(ks[8], (D, D), jnp.float32) * sd, 'ca_wo': jax.random.normal(ks[9], (D, D), jnp.float32) * sd, 'gate_w': jax.random.normal(ks[10], (E, D), jnp.float32) * 0.02, 'exp_w1': jax.random.normal(ks[11], (E, HID, D), jnp.float32) * sd, 'exp_w2': jax.random.normal(ks[12], (E, D, HID), jnp.float32) / np.sqrt(HID), 'sh_w1': jax.random.normal(ks[13], (HID, D), jnp.float32) * sd, 'sh_w2': jax.random.normal(ks[14], (D, HID), jnp.float32) / np.sqrt(HID)}
        return inp
    _L1_xattn_all = _L1_xattn_setup()
    _L1_xattn_in = {k: v for k, v in _L1_xattn_all.items() if k in ('norm1_w', 'norm2_w', 'norm3_w', 'sa_wq', 'sa_wk', 'sa_wv', 'sa_wo', 'ca_wq', 'ca_wk', 'ca_wv', 'ca_wo', 'gate_w', 'exp_w1', 'exp_w2', 'sh_w1', 'sh_w2')}
    del _L1_xattn_all

    def _L2_xattn_setup():
        import jax, jax.numpy as jnp
        import numpy as np
        E = 256
        H = 16
        HD = E // H
        EPS = 1e-05

        def _layer_norm(x, g, b):
            mu = jnp.mean(x, axis=-1, keepdims=True)
            var = jnp.var(x, axis=-1, keepdims=True)
            return (x - mu) * jax.lax.rsqrt(var + EPS) * g + b
        key = jax.random.key(seed)
        ks = jax.random.split(key, 16)
        s = 0.02
        inp = {'query': jax.random.normal(ks[0], (4, 256, E), jnp.float32), 'key': jax.random.normal(ks[1], (4, 512, E), jnp.float32), 'value': jax.random.normal(ks[2], (4, 512, E), jnp.float32), 'wq': jax.random.normal(ks[3], (E, E), jnp.float32) * s, 'bq': jnp.zeros((E,), jnp.float32), 'wk': jax.random.normal(ks[4], (E, E), jnp.float32) * s, 'bk': jnp.zeros((E,), jnp.float32), 'wv': jax.random.normal(ks[5], (E, E), jnp.float32) * s, 'bv': jnp.zeros((E,), jnp.float32), 'wo': jax.random.normal(ks[6], (E, E), jnp.float32) * s, 'bo': jnp.zeros((E,), jnp.float32), 'ln1_g': jnp.ones((E,), jnp.float32), 'ln1_b': jnp.zeros((E,), jnp.float32), 'ln2_g': jnp.ones((E,), jnp.float32), 'ln2_b': jnp.zeros((E,), jnp.float32), 'w1': jax.random.normal(ks[7], (E, 4 * E), jnp.float32) * s, 'b1': jnp.zeros((4 * E,), jnp.float32), 'w2': jax.random.normal(ks[8], (4 * E, E), jnp.float32) * s, 'b2': jnp.zeros((E,), jnp.float32)}
        return inp
    _L2_xattn_all = _L2_xattn_setup()
    _L2_xattn_in = {k: v for k, v in _L2_xattn_all.items() if k in ('wq', 'bq', 'wk', 'bk', 'wv', 'bv', 'wo', 'bo', 'ln1_g', 'ln1_b', 'ln2_g', 'ln2_b', 'w1', 'b1', 'w2', 'b2')}
    del _L2_xattn_all

    def _L3_xattn_setup():
        import jax, jax.numpy as jnp
        import numpy as np
        B, S, E, H, T, R = (8, 256, 256, 16, 196, 4)
        HD = E // H
        EPS = 1e-05

        def _ln(x, g, b):
            mu = jnp.mean(x, axis=-1, keepdims=True)
            var = jnp.mean(jnp.square(x - mu), axis=-1, keepdims=True)
            return (x - mu) * jax.lax.rsqrt(var + EPS) * g + b

        def _lin(x, w, b):
            return jnp.einsum('bse,oe->bso', x, w) + b

        def _heads(t):
            b, s, _ = t.shape
            return t.reshape(b, s, H, HD).transpose(0, 2, 1, 3)

        def _attend(q, k, v, causal):
            scale = HD ** (-0.5)
            scores = jnp.einsum('bhqd,bhkd->bhqk', q, k) * scale
            if causal:
                sq, sk = (scores.shape[-2], scores.shape[-1])
                mask = jnp.tril(jnp.ones((sq, sk), bool))
                scores = jnp.where(mask, scores, -jnp.inf)
            w = jax.nn.softmax(scores, axis=-1)
            out = jnp.einsum('bhqk,bhkd->bhqd', w, v)
            b, h, s, d = out.shape
            return out.transpose(0, 2, 1, 3).reshape(b, s, h * d)
        key = jax.random.key(seed)
        ks = jax.random.split(key, 12)
        w = lambda k, shape: jax.random.normal(k, shape, jnp.float32) * 0.02
        return {'x': jax.random.normal(ks[0], (B, S, E), jnp.float32), 'enc_out': jax.random.normal(ks[1], (B, T, E), jnp.float32), 'ln1_g': jnp.ones(E), 'ln1_b': jnp.zeros(E), 'attn_qkv_w': w(ks[2], (3 * E, E)), 'attn_qkv_b': jnp.zeros(3 * E), 'attn_proj_w': w(ks[3], (E, E)), 'attn_proj_b': jnp.zeros(E), 'ln2_g': jnp.ones(E), 'ln2_b': jnp.zeros(E), 'q_w': w(ks[4], (E, E)), 'q_b': jnp.zeros(E), 'k_w': w(ks[5], (E, E)), 'k_b': jnp.zeros(E), 'v_w': w(ks[6], (E, E)), 'v_b': jnp.zeros(E), 'ca_proj_w': w(ks[7], (E, E)), 'ca_proj_b': jnp.zeros(E), 'ln3_g': jnp.ones(E), 'ln3_b': jnp.zeros(E), 'fc_w': w(ks[8], (R * E, E)), 'fc_b': jnp.zeros(R * E), 'proj_w': w(ks[9], (E, R * E)), 'proj_b': jnp.zeros(E)}
    _L3_xattn_all = _L3_xattn_setup()
    _L3_xattn_in = {k: v for k, v in _L3_xattn_all.items() if k in ('ln1_g', 'ln1_b', 'attn_qkv_w', 'attn_qkv_b', 'attn_proj_w', 'attn_proj_b', 'ln2_g', 'ln2_b', 'q_w', 'q_b', 'k_w', 'k_b', 'v_w', 'v_b', 'ca_proj_w', 'ca_proj_b', 'ln3_g', 'ln3_b', 'fc_w', 'fc_b', 'proj_w', 'proj_b')}
    del _L3_xattn_all
    return {'x': x, 'ctx_1024': ctx_1024, 'mask_BxSxS_ik0': mask_BxSxS_ik0, 'mask_BxSxS2_if1': mask_BxSxS2_if1, 'L0_xattn_Wq': _L0_xattn_in['Wq'], 'L0_xattn_bq': _L0_xattn_in['bq'], 'L0_xattn_Wk': _L0_xattn_in['Wk'], 'L0_xattn_bk': _L0_xattn_in['bk'], 'L0_xattn_Wv': _L0_xattn_in['Wv'], 'L0_xattn_bv': _L0_xattn_in['bv'], 'L0_xattn_Wo': _L0_xattn_in['Wo'], 'L0_xattn_bo': _L0_xattn_in['bo'], 'L0_xattn_ln_gamma': _L0_xattn_in['ln_gamma'], 'L0_xattn_ln_beta': _L0_xattn_in['ln_beta'], 'L1_xattn_norm1_w': _L1_xattn_in['norm1_w'], 'L1_xattn_norm2_w': _L1_xattn_in['norm2_w'], 'L1_xattn_norm3_w': _L1_xattn_in['norm3_w'], 'L1_xattn_sa_wq': _L1_xattn_in['sa_wq'], 'L1_xattn_sa_wk': _L1_xattn_in['sa_wk'], 'L1_xattn_sa_wv': _L1_xattn_in['sa_wv'], 'L1_xattn_sa_wo': _L1_xattn_in['sa_wo'], 'L1_xattn_ca_wq': _L1_xattn_in['ca_wq'], 'L1_xattn_ca_wk': _L1_xattn_in['ca_wk'], 'L1_xattn_ca_wv': _L1_xattn_in['ca_wv'], 'L1_xattn_ca_wo': _L1_xattn_in['ca_wo'], 'L1_xattn_gate_w': _L1_xattn_in['gate_w'], 'L1_xattn_exp_w1': _L1_xattn_in['exp_w1'], 'L1_xattn_exp_w2': _L1_xattn_in['exp_w2'], 'L1_xattn_sh_w1': _L1_xattn_in['sh_w1'], 'L1_xattn_sh_w2': _L1_xattn_in['sh_w2'], 'L2_xattn_wq': _L2_xattn_in['wq'], 'L2_xattn_bq': _L2_xattn_in['bq'], 'L2_xattn_wk': _L2_xattn_in['wk'], 'L2_xattn_bk': _L2_xattn_in['bk'], 'L2_xattn_wv': _L2_xattn_in['wv'], 'L2_xattn_bv': _L2_xattn_in['bv'], 'L2_xattn_wo': _L2_xattn_in['wo'], 'L2_xattn_bo': _L2_xattn_in['bo'], 'L2_xattn_ln1_g': _L2_xattn_in['ln1_g'], 'L2_xattn_ln1_b': _L2_xattn_in['ln1_b'], 'L2_xattn_ln2_g': _L2_xattn_in['ln2_g'], 'L2_xattn_ln2_b': _L2_xattn_in['ln2_b'], 'L2_xattn_w1': _L2_xattn_in['w1'], 'L2_xattn_b1': _L2_xattn_in['b1'], 'L2_xattn_w2': _L2_xattn_in['w2'], 'L2_xattn_b2': _L2_xattn_in['b2'], 'L3_xattn_ln1_g': _L3_xattn_in['ln1_g'], 'L3_xattn_ln1_b': _L3_xattn_in['ln1_b'], 'L3_xattn_attn_qkv_w': _L3_xattn_in['attn_qkv_w'], 'L3_xattn_attn_qkv_b': _L3_xattn_in['attn_qkv_b'], 'L3_xattn_attn_proj_w': _L3_xattn_in['attn_proj_w'], 'L3_xattn_attn_proj_b': _L3_xattn_in['attn_proj_b'], 'L3_xattn_ln2_g': _L3_xattn_in['ln2_g'], 'L3_xattn_ln2_b': _L3_xattn_in['ln2_b'], 'L3_xattn_q_w': _L3_xattn_in['q_w'], 'L3_xattn_q_b': _L3_xattn_in['q_b'], 'L3_xattn_k_w': _L3_xattn_in['k_w'], 'L3_xattn_k_b': _L3_xattn_in['k_b'], 'L3_xattn_v_w': _L3_xattn_in['v_w'], 'L3_xattn_v_b': _L3_xattn_in['v_b'], 'L3_xattn_ca_proj_w': _L3_xattn_in['ca_proj_w'], 'L3_xattn_ca_proj_b': _L3_xattn_in['ca_proj_b'], 'L3_xattn_ln3_g': _L3_xattn_in['ln3_g'], 'L3_xattn_ln3_b': _L3_xattn_in['ln3_b'], 'L3_xattn_fc_w': _L3_xattn_in['fc_w'], 'L3_xattn_fc_b': _L3_xattn_in['fc_b'], 'L3_xattn_proj_w': _L3_xattn_in['proj_w'], 'L3_xattn_proj_b': _L3_xattn_in['proj_b']}

def reference(x, ctx_1024, mask_BxSxS_ik0, mask_BxSxS2_if1, L0_xattn_Wq, L0_xattn_bq, L0_xattn_Wk, L0_xattn_bk, L0_xattn_Wv, L0_xattn_bv, L0_xattn_Wo, L0_xattn_bo, L0_xattn_ln_gamma, L0_xattn_ln_beta, L1_xattn_norm1_w, L1_xattn_norm2_w, L1_xattn_norm3_w, L1_xattn_sa_wq, L1_xattn_sa_wk, L1_xattn_sa_wv, L1_xattn_sa_wo, L1_xattn_ca_wq, L1_xattn_ca_wk, L1_xattn_ca_wv, L1_xattn_ca_wo, L1_xattn_gate_w, L1_xattn_exp_w1, L1_xattn_exp_w2, L1_xattn_sh_w1, L1_xattn_sh_w2, L2_xattn_wq, L2_xattn_bq, L2_xattn_wk, L2_xattn_bk, L2_xattn_wv, L2_xattn_bv, L2_xattn_wo, L2_xattn_bo, L2_xattn_ln1_g, L2_xattn_ln1_b, L2_xattn_ln2_g, L2_xattn_ln2_b, L2_xattn_w1, L2_xattn_b1, L2_xattn_w2, L2_xattn_b2, L3_xattn_ln1_g, L3_xattn_ln1_b, L3_xattn_attn_qkv_w, L3_xattn_attn_qkv_b, L3_xattn_attn_proj_w, L3_xattn_attn_proj_b, L3_xattn_ln2_g, L3_xattn_ln2_b, L3_xattn_q_w, L3_xattn_q_b, L3_xattn_k_w, L3_xattn_k_b, L3_xattn_v_w, L3_xattn_v_b, L3_xattn_ca_proj_w, L3_xattn_ca_proj_b, L3_xattn_ln3_g, L3_xattn_ln3_b, L3_xattn_fc_w, L3_xattn_fc_b, L3_xattn_proj_w, L3_xattn_proj_b):
    import jax
    import jax.numpy as jnp

    def _L0_xattn_ref(x, context, Wq, bq, Wk, bk, Wv, bv, Wo, bo, ln_gamma, ln_beta):
        import jax, jax.numpy as jnp
        import numpy as np
        D_MODEL = 256
        NUM_HEADS = 16
        HEAD_DIM = D_MODEL // NUM_HEADS
        SCALE = HEAD_DIM ** (-0.5)
        LN_EPS = 1e-05
        Q_EPS = 1e-05

        def bit_quant(W):
            gamma = jnp.mean(jnp.abs(W))
            Wq = jnp.clip(jnp.round(W / (gamma + Q_EPS)), -1.0, 1.0) * gamma
            return W + jax.lax.stop_gradient(Wq - W)

        def layer_norm(x, gamma, beta):
            mu = jnp.mean(x, axis=-1, keepdims=True)
            var = jnp.mean(jnp.square(x - mu), axis=-1, keepdims=True)
            return (x - mu) * jax.lax.rsqrt(var + LN_EPS) * gamma + beta
        B, T, C = x.shape
        T_ctx = context.shape[1]
        residual = x
        xn = layer_norm(x, ln_gamma, ln_beta)
        q = xn @ bit_quant(Wq).T + bq
        k = context @ bit_quant(Wk).T + bk
        v = context @ bit_quant(Wv).T + bv
        q = q.reshape(B, T, NUM_HEADS, HEAD_DIM)
        k = k.reshape(B, T_ctx, NUM_HEADS, HEAD_DIM)
        v = v.reshape(B, T_ctx, NUM_HEADS, HEAD_DIM)
        scores = jnp.einsum('bqhd,bkhd->bhqk', q, k) * SCALE
        probs = jax.nn.softmax(scores, axis=-1)
        out = jnp.einsum('bhqk,bkhd->bqhd', probs, v).reshape(B, T, C)
        return residual + (out @ bit_quant(Wo).T + bo)

    def _L1_xattn_ref(x, encoder_output, tgt_mask, src_mask, norm1_w, norm2_w, norm3_w, sa_wq, sa_wk, sa_wv, sa_wo, ca_wq, ca_wk, ca_wv, ca_wo, gate_w, exp_w1, exp_w2, sh_w1, sh_w2):
        import jax, jax.numpy as jnp
        import numpy as np
        B, T, S_ENC, D, H, E, K = (4, 256, 64, 256, 16, 8, 2)
        DK = D // H
        HID = 4 * D
        NEG = -65504.0
        EPS = 1e-05

        def rmsnorm(x, w):
            return w * (x * jax.lax.rsqrt(jnp.mean(x * x, axis=-1, keepdims=True) + EPS))

        def mha(xq, xk, xv, mask, wq, wk, wv, wo):
            q = jnp.einsum('bsd,ed->bse', xq, wq).reshape(xq.shape[0], -1, H, DK).transpose(0, 2, 1, 3)
            k = jnp.einsum('bsd,ed->bse', xk, wk).reshape(xk.shape[0], -1, H, DK).transpose(0, 2, 1, 3)
            v = jnp.einsum('bsd,ed->bse', xv, wv).reshape(xv.shape[0], -1, H, DK).transpose(0, 2, 1, 3)
            scores = jnp.einsum('bhqd,bhkd->bhqk', q, k) / jnp.sqrt(jnp.float32(DK))
            scores = jnp.where(mask[:, None, :, :] == 0, NEG, scores)
            attn = jax.nn.softmax(scores, axis=-1)
            out = jnp.einsum('bhqk,bhkd->bhqd', attn, v)
            out = out.transpose(0, 2, 1, 3).reshape(xq.shape[0], -1, D)
            return jnp.einsum('bsd,ed->bse', out, wo)

        def moe_ffn(x, gate_w, exp_w1, exp_w2, sh_w1, sh_w2):
            b, s, d = x.shape
            xf = x.reshape(-1, d)
            sh = jnp.einsum('nd,hd->nh', xf, sh_w1)
            sh = jax.nn.silu(sh)
            sh = jnp.einsum('nh,dh->nd', sh, sh_w2)
            logits = jnp.einsum('nd,ed->ne', xf, gate_w)
            topk_vals, topk_idx = jax.lax.top_k(logits, K)
            topk_gates = jax.nn.softmax(topk_vals, axis=-1)
            n = xf.shape[0]
            gates = jnp.zeros((n, E), dtype=xf.dtype).at[jnp.arange(n)[:, None], topk_idx].set(topk_gates)
            h = jnp.einsum('nd,ehd->neh', xf, exp_w1)
            h = jax.nn.silu(h)
            eo = jnp.einsum('neh,edh->ned', h, exp_w2)
            sel = jnp.einsum('ned,ne->nd', eo, gates)
            return (sh + sel).reshape(b, s, d)
        xn = rmsnorm(x, norm1_w)
        h = x + mha(xn, xn, xn, tgt_mask, sa_wq, sa_wk, sa_wv, sa_wo)
        hn = rmsnorm(h, norm2_w)
        h = h + mha(hn, encoder_output, encoder_output, src_mask, ca_wq, ca_wk, ca_wv, ca_wo)
        hn = rmsnorm(h, norm3_w)
        return h + moe_ffn(hn, gate_w, exp_w1, exp_w2, sh_w1, sh_w2)

    def _L2_xattn_ref(query, key, value, wq, bq, wk, bk, wv, bv, wo, bo, ln1_g, ln1_b, ln2_g, ln2_b, w1, b1, w2, b2):
        import jax, jax.numpy as jnp
        import numpy as np
        E = 256
        H = 16
        HD = E // H
        EPS = 1e-05

        def _layer_norm(x, g, b):
            mu = jnp.mean(x, axis=-1, keepdims=True)
            var = jnp.var(x, axis=-1, keepdims=True)
            return (x - mu) * jax.lax.rsqrt(var + EPS) * g + b
        B, Sq, _ = query.shape
        Sk = key.shape[1]
        residual = query
        qn = _layer_norm(query, ln1_g, ln1_b)
        kn = _layer_norm(key, ln1_g, ln1_b)
        vn = _layer_norm(value, ln1_g, ln1_b)
        Q = (qn @ wq + bq).reshape(B, Sq, H, HD)
        K = (kn @ wk + bk).reshape(B, Sk, H, HD)
        V = (vn @ wv + bv).reshape(B, Sk, H, HD)
        scores = jnp.einsum('bqhd,bkhd->bhqk', Q, K) / jnp.sqrt(jnp.float32(HD))
        attn = jax.nn.softmax(scores, axis=-1)
        out = jnp.einsum('bhqk,bkhd->bqhd', attn, V).reshape(B, Sq, E)
        out = out @ wo + bo
        x = residual + out
        residual2 = x
        y = _layer_norm(x, ln2_g, ln2_b)
        y = jax.nn.gelu(y @ w1 + b1, approximate=False)
        y = y @ w2 + b2
        return residual2 + y

    def _L3_xattn_ref(x, enc_out, ln1_g, ln1_b, attn_qkv_w, attn_qkv_b, attn_proj_w, attn_proj_b, ln2_g, ln2_b, q_w, q_b, k_w, k_b, v_w, v_b, ca_proj_w, ca_proj_b, ln3_g, ln3_b, fc_w, fc_b, proj_w, proj_b):
        import jax, jax.numpy as jnp
        import numpy as np
        B, S, E, H, T, R = (8, 256, 256, 16, 196, 4)
        HD = E // H
        EPS = 1e-05

        def _ln(x, g, b):
            mu = jnp.mean(x, axis=-1, keepdims=True)
            var = jnp.mean(jnp.square(x - mu), axis=-1, keepdims=True)
            return (x - mu) * jax.lax.rsqrt(var + EPS) * g + b

        def _lin(x, w, b):
            return jnp.einsum('bse,oe->bso', x, w) + b

        def _heads(t):
            b, s, _ = t.shape
            return t.reshape(b, s, H, HD).transpose(0, 2, 1, 3)

        def _attend(q, k, v, causal):
            scale = HD ** (-0.5)
            scores = jnp.einsum('bhqd,bhkd->bhqk', q, k) * scale
            if causal:
                sq, sk = (scores.shape[-2], scores.shape[-1])
                mask = jnp.tril(jnp.ones((sq, sk), bool))
                scores = jnp.where(mask, scores, -jnp.inf)
            w = jax.nn.softmax(scores, axis=-1)
            out = jnp.einsum('bhqk,bhkd->bhqd', w, v)
            b, h, s, d = out.shape
            return out.transpose(0, 2, 1, 3).reshape(b, s, h * d)
        h = _ln(x, ln1_g, ln1_b)
        qkv = _lin(h, attn_qkv_w, attn_qkv_b)
        q, k, v = jnp.split(qkv, 3, axis=-1)
        a = _attend(_heads(q), _heads(k), _heads(v), causal=True)
        x = x + _lin(a, attn_proj_w, attn_proj_b)
        h = _ln(x, ln2_g, ln2_b)
        q = _heads(_lin(h, q_w, q_b))
        k = _heads(_lin(enc_out, k_w, k_b))
        v = _heads(_lin(enc_out, v_w, v_b))
        a = _attend(q, k, v, causal=False)
        x = x + _lin(a, ca_proj_w, ca_proj_b)
        h = _ln(x, ln3_g, ln3_b)
        h = jax.nn.gelu(_lin(h, fc_w, fc_b), approximate=False)
        x = x + _lin(h, proj_w, proj_b)
        return x
    x = _L0_xattn_ref(x, ctx_1024, L0_xattn_Wq, L0_xattn_bq, L0_xattn_Wk, L0_xattn_bk, L0_xattn_Wv, L0_xattn_bv, L0_xattn_Wo, L0_xattn_bo, L0_xattn_ln_gamma, L0_xattn_ln_beta)
    x = _L1_xattn_ref(x, ctx_1024, mask_BxSxS_ik0, mask_BxSxS2_if1, L1_xattn_norm1_w, L1_xattn_norm2_w, L1_xattn_norm3_w, L1_xattn_sa_wq, L1_xattn_sa_wk, L1_xattn_sa_wv, L1_xattn_sa_wo, L1_xattn_ca_wq, L1_xattn_ca_wk, L1_xattn_ca_wv, L1_xattn_ca_wo, L1_xattn_gate_w, L1_xattn_exp_w1, L1_xattn_exp_w2, L1_xattn_sh_w1, L1_xattn_sh_w2)
    x = _L2_xattn_ref(x, ctx_1024, ctx_1024, L2_xattn_wq, L2_xattn_bq, L2_xattn_wk, L2_xattn_bk, L2_xattn_wv, L2_xattn_bv, L2_xattn_wo, L2_xattn_bo, L2_xattn_ln1_g, L2_xattn_ln1_b, L2_xattn_ln2_g, L2_xattn_ln2_b, L2_xattn_w1, L2_xattn_b1, L2_xattn_w2, L2_xattn_b2)
    x = _L3_xattn_ref(x, ctx_1024, L3_xattn_ln1_g, L3_xattn_ln1_b, L3_xattn_attn_qkv_w, L3_xattn_attn_qkv_b, L3_xattn_attn_proj_w, L3_xattn_attn_proj_b, L3_xattn_ln2_g, L3_xattn_ln2_b, L3_xattn_q_w, L3_xattn_q_b, L3_xattn_k_w, L3_xattn_k_b, L3_xattn_v_w, L3_xattn_v_b, L3_xattn_ca_proj_w, L3_xattn_ca_proj_b, L3_xattn_ln3_g, L3_xattn_ln3_b, L3_xattn_fc_w, L3_xattn_fc_b, L3_xattn_proj_w, L3_xattn_proj_b)
    return x

_drawn_inputs = setup_inputs


def setup_inputs(seed=0):
    import zlib

    import numpy as np

    out = dict(_drawn_inputs(seed))
    spreads = {'L0_xattn_bq': (0.0, 0.309),
     'L0_xattn_bk': (0.0, 2.0),
     'L0_xattn_bv': (0.0, 0.1),
     'L0_xattn_bo': (0.0, 0.1),
     'L0_xattn_ln_gamma': (1.0, 0.567),
     'L0_xattn_ln_beta': (0.0, 0.405),
     'L1_xattn_norm1_w': (1.0, 0.2),
     'L1_xattn_norm2_w': (1.0, 0.2),
     'L1_xattn_norm3_w': (1.0, 0.2),
     'L2_xattn_bq': (0.0, 2.0),
     'L2_xattn_bk': (0.0, 2.0),
     'L2_xattn_bv': (0.0, 0.369),
     'L2_xattn_bo': (0.0, 0.1),
     'L2_xattn_ln1_g': (1.0, 0.6),
     'L2_xattn_ln1_b': (0.0, 0.8),
     'L2_xattn_ln2_g': (1.0, 0.6),
     'L2_xattn_ln2_b': (0.0, 0.8),
     'L2_xattn_b1': (0.0, 0.341),
     'L2_xattn_b2': (0.0, 0.1),
     'L3_xattn_ln1_g': (1.0, 0.6),
     'L3_xattn_ln1_b': (0.0, 0.8),
     'L3_xattn_attn_qkv_b': (0.0, 0.366),
     'L3_xattn_attn_proj_b': (0.0, 0.1),
     'L3_xattn_ln2_g': (1.0, 0.6),
     'L3_xattn_ln2_b': (0.0, 0.8),
     'L3_xattn_q_b': (0.0, 2.0),
     'L3_xattn_k_b': (0.0, 2.0),
     'L3_xattn_v_b': (0.0, 0.376),
     'L3_xattn_ca_proj_b': (0.0, 0.1),
     'L3_xattn_ln3_g': (1.0, 0.6),
     'L3_xattn_ln3_b': (0.0, 0.8),
     'L3_xattn_fc_b': (0.0, 0.359),
     'L3_xattn_proj_b': (0.0, 0.1)}
    factors = {'L2_xattn_wq': 8.0, 'L2_xattn_wk': 8.0, 'L3_xattn_q_w': 8.0, 'L3_xattn_k_w': 8.0}
    for name, (base, spread) in spreads.items():
        noise = np.random.default_rng([zlib.crc32(name.encode()), seed]).standard_normal(out[name].shape)
        drawn = base * np.exp(spread * noise) if base else spread * noise
        out[name] = jnp.asarray(drawn.astype(out[name].dtype))
    for name, factor in factors.items():
        out[name] = (out[name] * factor).astype(out[name].dtype)
    return out
```

```python
import numpy as np

import concourse.bass as bass
from concourse import mybir
from contextlib import ExitStack

F32 = mybir.dt.float32
BF16 = mybir.dt.bfloat16
I32 = mybir.dt.int32
U32 = mybir.dt.uint32
ALU = mybir.AluOpType
ACT = mybir.ActivationFunctionType
AX = mybir.AxisListType

B, S, SC, D = 32, 112, 375, 256
H, HD = 16, 16
C = D // 128
HID, HC = 1024, 8
E = 8
EPS = 1e-5
NEG = -65504.0
QK_SCALE = HD ** -0.5
KT_CTX = 125
TB = 4
NTILES = B // TB
TOK = TB * S

ATTN = {
    "L0": dict(cross=True, norm="ln", mask=None, ctx_ln=False),
    "L1S": dict(cross=False, norm="rms", mask="input", ctx_ln=False),
    "L1C": dict(cross=True, norm="rms", mask="input", ctx_ln=False),
    "L2": dict(cross=True, norm="ln", mask=None, ctx_ln=True),
    "L3S": dict(cross=False, norm="ln", mask="causal", ctx_ln=False),
    "L3C": dict(cross=True, norm="ln", mask=None, ctx_ln=False),
}
ORDER = ["L0", "L1S", "L1C", "MOE", "L2", "F2", "L3S", "L3C", "F3"]
ATTN_NAMES = list(ATTN)
COLS = {}
for _n in ATTN_NAMES:
    for _p in ("g", "b", "bq", "bk"):
        COLS[_n + _p] = (len(COLS)) * 2
for _n in ("MOE", "F2", "F3"):
    for _p in ("g", "b"):
        COLS[_n + _p] = (len(COLS)) * 2
NCOL = len(COLS) * 2
ROWS = {n: i for i, n in enumerate([a + p for a in ATTN_NAMES for p in ("bv", "bo")] + ["F2b2", "F3b2"])}


class Unit:

    def __init__(self, pair, k):
        self.pair, self.k = pair, k
        self.par = k % 2
        self.n = pair * 2 + k
        self.half = pair + k // 2

    def step(self, d):
        return Unit(self.pair, self.k + d)


def units(eng, count, body):
    u = Unit(0, 0)
    body(u, None, u.step(1))
    with eng.Fori(0, count // 2 - 1) as pair:
        for k in (1, 2):
            u = Unit(pair, k)
            body(u, u.step(-1), u.step(1))
    u = Unit(count // 2 - 1, 1)
    body(u, u.step(-1), None)


class Signals:

    def __init__(self, nc, stack):
        self.nc, self.stack = nc, stack
        self.sems, self.left, self.per = {}, {}, {}

    def phase(self, **per):
        self.per = per
        for name in per:
            if name not in self.sems:
                self.sems[name] = self.stack.enter_context(self.nc.semaphore(name))
                self.left[name] = 0

    def end(self, count, **once):
        for name, per in self.per.items():
            self.left[name] += per * count
        for name, n in once.items():
            self.left[name] += n

    def once(self, name, k):
        if name not in self.sems:
            self.sems[name] = self.stack.enter_context(self.nc.semaphore(name))
            self.left[name] = 0
        return self.sems[name], self.left[name] + k

    def __getitem__(self, name):
        return self.sems[name]

    def at(self, name, unit, k=None):
        n = unit.n if isinstance(unit, Unit) else unit
        return self.sems[name], n * self.per[name] + (self.left[name] + (self.per[name] if k is None else k))

    def loaded(self, name, unit):
        name = f"{name}{unit.par}"
        return self.sems[name], unit.half * (2 * self.per[name]) + (self.left[name] + 2 * self.per[name])


def head(s):
    i, par, j = s // 8, (s // 4) % 2, s % 4
    return 8 * i + 2 * j + par, i, j, par


def build(nc, t, out, order=tuple(ORDER)):
    stack = ExitStack()
    with stack:
        def sb(name, shape, dt=F32):
            return stack.enter_context(nc.sbuf_tensor(name, shape, dt))

        def pb(name, shape, dt=F32):
            return stack.enter_context(nc.psum_tensor(name, shape, dt))

        m = {}
        m["x"] = sb("x_all", [S, B, D])
        m["w"] = sb("attn_w", [128, 4 * len(ATTN), C, D])
        m["col"] = sb("col", [128, NCOL])
        m["fb1"] = sb("fb1", [128, 2, HC])
        m["row"] = sb("row", [128, len(ROWS), D])
        m["ident"] = sb("ident", [128, 128])
        m["qmask"] = sb("qmask", [128, 2])
        m["nmask"] = sb("nmask", [128, 4])
        m["causal"] = sb("causal", [S, S])
        m["causalT"] = sb("causalT", [S, 1, S])
        m["identb"] = sb("identb", [128, 128], BF16)
        m["onesb"] = sb("onesb", [128, 128], BF16)
        m["onesf"] = sb("onesf", [128, 128])
        m["iota"] = sb("iota", [128, E])
        m["mv"] = sb("mv", [S, B, 2])
        m["xst"] = sb("xst", [S, 6])
        m["xmv"] = sb("xmv", [S, 2])
        m["junk"] = sb("junk", [S, 2, SC])
        m["cmv"] = sb("cmv", [KT_CTX, B * 3, 2])
        m["rs"] = sb("rs", [S, B])
        m["crs"] = sb("crs", [KT_CTX, B * 3])
        m["psum"] = pb("psum", [128, 8, 512])
        sg = Signals(nc, stack)
        for name in ("rstd", "rstd_root", "c_rstd", "c_rstd_root", "v_const", "amb_zero", "msq", "apart"):
            sg.once(name, 0)

        kinds = ["rms" if name in ("L1S", "L1C", "MOE") else "ln" for name in order] + [None]
        prepare(nc, t, m, sg, kinds[0])
        for name, following in zip(order, kinds[1:]):
            if name in ATTN:
                attention(nc, t, m, sg, name, following)
            else:
                ffn(nc, t, m, sg, name, following)
        sg.phase(x_out=16)
        with nc.Block() as block:
            @block.sync
            def _(sp):
                sp.dma_start(out.rearrange("b s d -> s b d"), m["x"][:, :, :]).then_inc(sg["x_out"], 16)
                sp.wait_ge(sg["x_out"], 16)


def wait_apart(eng, sg, signal):
    eng.wait_ge(*signal)
    eng.sem_inc(sg["apart"], 1)


def token_stats(dve, sg, m, n, unit, k):
    dve.bn_stats(m["xst"][:, :], m["x"][:, n, :]).then_inc(sg["x_stats"], 1)
    wait_apart(dve, sg, sg.at("x_stats", unit, k))
    dve.bn_aggr(m["xmv"][:, :], m["xst"][:, :]).then_inc(sg["x_moments"], 1)
    wait_apart(dve, sg, sg.at("x_moments", unit, k))
    dve.tensor_copy(m["mv"][:, n, :], m["xmv"][:, :]).then_inc(sg["x_kept"], 1)


def mean_square(dve, sg, m, sq):
    dve.tensor_tensor(sq, m["mv"][:, :, 0], m["mv"][:, :, 0], ALU.mult).then_inc(sg["msq"], 1)
    dve.wait_ge(*sg.once("msq", 1))
    dve.tensor_tensor(sq, sq, m["mv"][:, :, 1], ALU.add).then_inc(sg["msq"], 1)
    dve.wait_ge(*sg.once("msq", 2))


def reciprocal_root(dve, act, sg, name, var, root, out, tmp):
    if act:
        act.wait_ge(*sg.once(name, 1))
        act.activation(root, tmp, ACT.Sqrt).then_inc(sg[name + "_root"], 1)
        return
    dve.tensor_scalar(tmp, var, EPS, None, ALU.add).then_inc(sg.once(name, 1)[0], 1)
    dve.wait_ge(*sg.once(name + "_root", 1))
    dve.reciprocal(out, root).then_inc(sg[name], 1)
    dve.wait_ge(*sg.once(name, 2))
    dve.tensor_tensor(root, tmp, out, ALU.mult).then_inc(sg[name], 1)
    dve.wait_ge(*sg.once(name, 3))
    dve.tensor_tensor(root, root, out, ALU.mult).then_inc(sg[name], 1)
    dve.wait_ge(*sg.once(name, 4))
    dve.tensor_scalar(root, root, -0.5, 1.5, ALU.mult, ALU.add).then_inc(sg[name], 1)
    dve.wait_ge(*sg.once(name, 5))
    dve.tensor_tensor(out, out, root, ALU.mult).then_inc(sg[name], 1)


def prepare(nc, t, m, sg, following):
    with ExitStack() as st:
        wq = m["w"]
        NW = 4
        absum = st.enter_context(nc.sbuf_tensor("absum", [128, NW], F32))
        gamma = st.enter_context(nc.sbuf_tensor("gamma", [128, NW], F32))
        geps = st.enter_context(nc.sbuf_tensor("geps", [128, 2, NW], F32))
        up = st.enter_context(nc.sbuf_tensor("up", [128, NW, C, D], F32))
        dn = st.enter_context(nc.sbuf_tensor("dn", [128, NW, C, D], F32))
        sg.phase(w_in=16, const_in=16 * 8, x_in=16, x_stats=B, x_moments=B, x_kept=B, ones_set=2, ident_cast=1, absum_set=NW, gsum_psum=1,
                 gamma_set=1, geps_set=2, tern_up=NW, tern_dn=NW, tern=NW, scaled=NW, quant_diff=NW, quantised=NW)
        block = st.enter_context(nc.Block())

        @block.sync
        def _(sp):
            sp.dma_start(m["w"][:, :, :, :], t["attn_w"]).then_inc(sg["w_in"], 16)
            for k in ("col", "fb1", "ident", "qmask", "nmask", "causal"):
                ap = m[k][:, :, :] if len(m[k].shape) == 3 else m[k][:, :]
                sp.dma_start(ap, t[k]).then_inc(sg["const_in"], 16)
            sp.dma_start(m["causalT"][:, 0, :], t["causalT"]).then_inc(sg["const_in"], 16)
            sp.dma_start(m["row"][:, :, :], t["row"].partition_broadcast(128)).then_inc(sg["const_in"], 16)
            sp.dma_start(m["x"][:, :, :], t["x"].rearrange("b s d -> s b d")).then_inc(sg["x_in"], 16)
            sp.wait_ge(sg["x_in"], 16)

        @block.gpsimd
        def _(pool):
            pool.memset(m["onesf"][:, :], 1.0).then_inc(sg["ones_set"], 1)
            pool.memset(m["onesb"][:, :], 1.0).then_inc(sg["ones_set"], 1)
            pool.iota(m["iota"][:, :], pattern=[[1, E]], base=0, channel_multiplier=0,
                      allow_small_or_imprecise_dtypes=True)
            pool.wait_ge(sg["const_in"], 16 * 8)
            pool.tensor_copy(m["identb"][:, :], m["ident"][:, :]).then_inc(sg["ident_cast"], 1)

        @block.tensor
        def _(pe):
            pe.wait_ge(sg["ones_set"], 2)
            pe.wait_ge(sg["absum_set"], NW)
            pe.matmul(m["psum"][:, 0, 0:NW], m["onesf"][:, :], absum[:, :], start=True, stop=True)\
              .then_inc(sg["gsum_psum"], 1)

        @block.vector
        def _(dve):
            dve.wait_ge(sg["w_in"], 16)
            for i in range(NW):
                dve.tensor_reduce(absum[:, i:i + 1], wq[:, i, :, :], axis=AX.XY, op=ALU.add,
                                  apply_absolute_value=True).then_inc(sg["absum_set"], 1)
            dve.wait_ge(sg["gsum_psum"], 1)
            dve.tensor_scalar(gamma[:, :], m["psum"][:, 0, 0:NW], 1.0 / (D * D), None, ALU.mult)\
               .then_inc(sg["gamma_set"], 1)
            dve.wait_ge(sg["gamma_set"], 1)
            dve.tensor_scalar(geps[:, 0, :], gamma[:, :], EPS, 0.5, ALU.add, ALU.mult).then_inc(sg["geps_set"], 1)
            dve.tensor_scalar(geps[:, 1, :], gamma[:, :], EPS, -0.5, ALU.add, ALU.mult).then_inc(sg["geps_set"], 1)
            dve.wait_ge(sg["geps_set"], 2)
            for i in range(NW):
                dve.tensor_scalar(up[:, i, :, :], wq[:, i, :, :], geps[:, 0, i:i + 1], None, ALU.is_gt)\
                   .then_inc(sg["tern_up"], 1)
                dve.tensor_scalar(dn[:, i, :, :], wq[:, i, :, :], geps[:, 1, i:i + 1], None, ALU.is_lt)\
                   .then_inc(sg["tern_dn"], 1)
            for i in range(NW):
                dve.wait_ge(sg["tern_dn"], i + 1)
                dve.tensor_tensor(up[:, i, :, :], up[:, i, :, :], dn[:, i, :, :], ALU.subtract)\
                   .then_inc(sg["tern"], 1)
            for i in range(NW):
                dve.wait_ge(sg["tern"], i + 1)
                dve.tensor_scalar(up[:, i, :, :], up[:, i, :, :], gamma[:, i:i + 1], None, ALU.mult)\
                   .then_inc(sg["scaled"], 1)
            for i in range(NW):
                dve.wait_ge(sg["scaled"], i + 1)
                dve.tensor_tensor(up[:, i, :, :], up[:, i, :, :], wq[:, i, :, :], ALU.subtract)\
                   .then_inc(sg["quant_diff"], 1)
            for i in range(NW):
                dve.wait_ge(sg["quant_diff"], i + 1)
                dve.tensor_tensor(wq[:, i, :, :], wq[:, i, :, :], up[:, i, :, :], ALU.add)\
                   .then_inc(sg["quantised"], 1)
            dve.wait_ge(sg["x_in"], 16)
            for n in range(B):
                if n:
                    dve.wait_ge(sg["x_kept"], n)
                token_stats(dve, sg, m, n, 0, n + 1)
    sg.end(1)


def attention(nc, t, m, sg, name, following):
    cfg = ATTN[name]
    cross, masked, ctx_ln, rms = cfg["cross"], cfg["mask"], cfg["ctx_ln"], cfg["norm"] == "rms"
    in_mask = masked == "input"
    a = ATTN_NAMES.index(name)
    NK, KS = (3, KT_CTX) if cross else (1, S)
    KEYS = NK * KS
    NT = 2 * NK
    bias = name not in ("L1S", "L1C")
    wq, wk, wv, wo = (m["w"][:, 4 * a + i, :, :] for i in range(4))
    x, ident, identb = m["x"], m["ident"], m["identb"]
    PS = m["psum"]
    NKE = 2 if cross else 1

    def col(p, c):
        at = COLS[name + p] + c
        return m["col"][:, at:at + 1]

    def row(p, n):
        return m["row"][0:n, ROWS[name + p], :]

    sg.phase(
        xn=1, xt_psum=1, xt_sb=1, k_psum=NKE, k_sb=NKE, v_psum=NK, v_sb=NK, q_psum=1, q_sb=1,
        s_psum=16, s_max=16, neg_max=1, neg_hi=1, neg_lo=1, nm_psum=1, nm_sb=1,
        t_psum=NT, p_exp=NT, av_psum=2, av_sb=1, t1_psum=1, rden=1, o_norm=1, ot_psum=1, ot_sb=1, o_psum=1, x_new=1,
        **(dict(x_stats=1, x_moments=1, x_kept=1) if following else {}),
        **(dict(xbias=1) if bias else {}),
        **(dict(ctx_in0=8, ctx_in1=8) if cross and not ctx_ln else {}),
        **(dict(tok_in0=8, tok_in1=8, cxn=NK, ct_psum=NK, ct_sb=NK) if ctx_ln else {}),
        **(dict(p_masked=NT) if masked else {}),
        **(dict(mask_in0=16, mask_in1=16, m_bias=1, m_max=1, m_two=1, any_psum=1, any_sb=1, any_off=1, m_ready=1)
           if in_mask else {}))

    FILL = ["T1"] + (["C0", "C1"] if ctx_ln else []) + ["OT"] + (["C2"] if ctx_ln else []) + ["O"] \
        + (["ANY"] if in_mask else []) + ["XT"]
    PROJ = ["K0", "K1", "V0", "V1", "V2", "Q"] if cross else ["K0", "V0", "Q"]
    BANK = {"T1": 6, "OT": 6, "O": 6, "K0": 6, "K1": 7, "V0": 7 if cross else 6, "V1": 6, "V2": 6, "C0": 7, "C1": 6, "C2": 7,
            "ANY": 7, "XT": 6, "Q": 6, "NM": 7, "AV": 7}
    READ_BY = {"T1": ("o_norm", 1), "OT": ("ot_sb", 1), "O": ("x_new", 1), "K0": ("k_sb", 1), "K1": ("k_sb", 2),
               "V0": ("v_sb", 1), "V1": ("v_sb", 2), "V2": ("v_sb", 3), "C0": ("ct_sb", 1), "C1": ("ct_sb", 2),
               "C2": ("ct_sb", 3), "ANY": ("any_sb", 1), "XT": ("xt_sb", 1), "Q": ("q_sb", 1),
               "NM": ("nm_sb", 1), "AV": ("av_sb", 1)}
    TAIL = ("T1", "OT", "O")
    steps = ["STAT"]
    fill = list(FILL)
    every = max(1, 16 // (len(fill) + 1))
    for s in range(16):
        steps.append(("S", s))
        if s % every == every - 1 and fill:
            steps.append(fill.pop(0))
    steps += fill + ["NM"]
    proj = list(PROJ)
    for tt in range(NT):
        steps.append(("T", tt))
        if tt == NK:
            steps.append(("AV", 0))
        steps.append(proj.pop(0))
    steps += proj + [("AV", 1)]
    first = ["STAT"] + (["ANY"] if in_mask else []) + ([] if cross else ["XT"]) \
        + (["C0", "C1", "C2"] if ctx_ln else []) + (["K0", "K1", "V0", "V1", "V2", "XT"] if cross else ["K0", "V0"]) + ["Q"]

    def walk(un, prev, nxt):
        for st in steps:
            if isinstance(st, tuple):
                yield st[0], st[1], un
            elif st == "NM":
                yield st, 0, un
            elif st in TAIL:
                if prev:
                    yield st, 0, prev
            elif nxt:
                yield (st, 0, nxt) if st[0] not in "KVC" else (st[0], int(st[1]), nxt)

    def opening(un):
        for st in first:
            yield (st, 0, un) if st[0] not in "KVC" else (st[0], int(st[1]), un)

    def closing(un):
        for st in TAIL:
            yield st, 0, un

    with ExitStack() as stk:
        def sb(nm, shape, dt=F32):
            return stk.enter_context(nc.sbuf_tensor(name + nm, shape, dt))
        ctxT = sb("ctxT", [128, 2, C, SC]) if cross else None
        ctok = sb("ctok", [KS, 2, NK, D]) if ctx_ln else None
        cxn = sb("cxn", [KS, NK, D]) if ctx_ln else None
        root, vare, sq = sb("root", [S, B]), sb("vare", [S, B]), sb("sq", [S, B])
        croot = sb("croot", [KS, B * NK]) if ctx_ln else None
        cvare = sb("cvare", [KS, B * NK]) if ctx_ln else None
        kT = sb("kT", [128, 2, C, KEYS])
        vA = sb("vA", [KS, 2, NK, H, 32])
        xn = sb("xn", [S, D])
        xT = sb("xT", [128, C, S])
        junk = m["junk"]
        qT = sb("qT", [128, 2, 4, S])
        mx = sb("mx", [S, H])
        amb = sb("amb", [S, 2, 1])
        nmx = sb("nmx", [S, H])
        nmb = sb("nmb", [S, 4, 2, H], BF16)
        nmT = sb("nmT", [128, 4, S], BF16)
        P = sb("P", [KS, 2, NK, 8, S])
        avT = sb("avT", [128, 4, S])
        rden = sb("rden", [S, 4, 4])
        on = sb("on", [S, D])
        oT = sb("oT", [128, C, S])
        mi = sb("mi", [S, 2, KEYS], I32) if in_mask else None
        miT = sb("miT", [KS, 2, NK, S], I32) if in_mask else None
        mb = sb("mb", [S, 2, KEYS]) if in_mask else None
        m2 = sb("m2", [KS, 2, NK, S], BF16) if in_mask else None
        anyB = sb("anyB", [128, 2, S]) if in_mask else None
        aoff = sb("aoff", [128, S], BF16) if in_mask else None
        block = stk.enter_context(nc.Block())

        keysT = (lambda un: (cxT if ctx_ln else ctxT)[:, 0 if ctx_ln else un.par]) if cross else None
        cxT = sb("cxT", [128, 1, C, SC]) if ctx_ln else None

        @block.sync
        def _(sp):
            def load(un, free):
                if cross and not ctx_ln:
                    if free:
                        sp.wait_ge(*sg.at("v_psum", free))
                    sp.dma_start(ctxT[:, un.par, :, :], t["ctxT"][un.n]).then_inc(sg[f"ctx_in{un.par}"], 16)
                if ctx_ln:
                    if free:
                        sp.wait_ge(*sg.at("cxn", free))
                    sp.dma_start(ctok[:, un.par, :, :], t["ctx"][un.n].rearrange("(k p) d -> p k d", p=KS))\
                      .then_inc(sg[f"tok_in{un.par}"], 16)
                if in_mask:
                    if free:
                        sp.wait_ge(*sg.at("m_two", free))
                        sp.wait_ge(*sg.at("m_bias", free))
                    sp.dma_start(mi[:, un.par, :], t["mask" + name][un.n]).then_inc(sg[f"mask_in{un.par}"], 16)
                    sp.dma_start(miT[:, un.par, :, :],
                                 t["maskT" + name][un.n].rearrange("(k p) q -> p k q", p=KS))\
                      .then_inc(sg[f"mask_in{un.par}"], 16)

            if cross or in_mask:
                load(Unit(0, 0), None)
                load(Unit(0, 1), None)
                with sp.Fori(0, B // 2 - 1) as pair:
                    load(Unit(pair, 2), Unit(pair, 0))
                    load(Unit(pair, 3), Unit(pair, 1))

        @block.gpsimd
        def _(pool):
            pool.memset(vA[:, :, :, :, HD + 1:32], 0.0).then_inc(sg["v_const"], 1)
            pool.memset(vA[:, :, :, :, HD:HD + 1], 1.0).then_inc(sg["v_const"], 1)

            def items(seq):
                for st, k, un in seq:
                    if st == "STAT":
                        if bias:
                            pool.wait_ge(*sg.at("xn", un))
                            pool.tensor_tensor(x[:, un.n, :], x[:, un.n, :], row("bo", S), ALU.add)\
                                .then_inc(sg["xbias"], 1)
                        if in_mask:
                            wait_apart(pool, sg, sg.loaded("mask_in", un))
                            if not (isinstance(un.pair, int) and un.pair * 2 + un.k <= 1):
                                wait_apart(pool, sg, sg.at("s_max", un.step(-2)))
                            pool.tensor_scalar(mb[:, un.par, :], mi[:, un.par, :], 0.0, NEG, ALU.is_equal,
                                               ALU.mult).then_inc(sg["m_bias"], 1)
            items(opening(Unit(0, 0)))
            units(pool, B, lambda un, prev, nxt: items(walk(un, prev, nxt)))

        @block.scalar
        def _(act):
            def items(seq):
                for st, k, un in seq:
                    later = not (isinstance(un.pair, int) and un.pair * 2 + un.k == 0)
                    if st == "XT":
                        act.wait_ge(*sg.at("xt_psum", un))
                        if later:
                            act.wait_ge(*sg.at("q_psum", un.step(-1)))
                            if not cross:
                                act.wait_ge(*sg.at("v_psum", un.step(-1)))
                        for c in range(C):
                            ins = act.activation(xT[:, c, :], PS[:, BANK["XT"], c * S:(c + 1) * S], ACT.Identity,
                                                 bias=0.0 if rms else col("b", c), scale=col("g", c))
                        ins.then_inc(sg["xt_sb"], 1)
                    elif st == "C":
                        act.wait_ge(*sg.at("ct_psum", un, k + 1))
                        if later and k == 0:
                            act.wait_ge(*sg.at("v_psum", un.step(-1)))
                        for c in range(C):
                            ins = act.activation(cxT[:, 0, c, k * KS:(k + 1) * KS],
                                                 PS[:, BANK[f"C{k}"], c * KS:(c + 1) * KS], ACT.Identity,
                                                 bias=col("b", c), scale=col("g", c))
                        ins.then_inc(sg["ct_sb"], 1)
                    elif st == "K":
                        act.wait_ge(*sg.at("k_psum", un, k + 1))
                        if cross:
                            act.activation(kT[:, un.par, k, :], PS[:, BANK[f"K{k}"], 0:SC], ACT.Identity,
                                           bias=col("bk", k) if bias else 0.0).then_inc(sg["k_sb"], 1)
                        else:
                            for c in range(C):
                                ins = act.activation(kT[:, un.par, c, :], PS[:, BANK["K0"], c * S:(c + 1) * S],
                                                     ACT.Identity, bias=col("bk", c) if bias else 0.0)
                            ins.then_inc(sg["k_sb"], 1)
                    elif st == "OT":
                        act.wait_ge(*sg.at("ot_psum", un))
                        if later:
                            act.wait_ge(*sg.at("o_psum", un.step(-1)))
                        act.activation(oT[:, :, :], PS[:, BANK["OT"], 0:C * S].rearrange("p (c s) -> p c s", c=C),
                                       ACT.Identity).then_inc(sg["ot_sb"], 1)
                    elif st == "NM":
                        act.wait_ge(*sg.at("nm_psum", un))
                        if later:
                            act.wait_ge(*sg.at("t_psum", un.step(-1)))
                        src = PS[:, BANK["NM"], 0:S // 2].bitcast(BF16)
                        for g in range(4):
                            ins = act.activation(nmT[:, g, :], src, ACT.Identity, scale=m["nmask"][:, g:g + 1])
                        ins.then_inc(sg["nm_sb"], 1)
                    elif st == "T":
                        i, kt = k // NK, k % NK
                        act.wait_ge(*sg.at("t_psum", un, k + 1))
                        if later and kt == 0:
                            act.wait_ge(*sg.at("av_psum", un.step(-1), i + 1))
                        act.activation(P[:, i, kt, :, :].rearrange("p (j e) s -> p j (e s)", j=4),
                                       PS[0:KS, 0:4, 0:2 * S], ACT.Exp)\
                            .then_inc(sg["p_exp"], 1)
                    elif st == "AV" and k == 1:
                        act.wait_ge(*sg.at("av_psum", un))
                        if later:
                            act.wait_ge(*sg.at("t1_psum", un.step(-1)))
                        act.activation(avT[:, :, :], PS[:, BANK["AV"], 0:4 * S].rearrange("p (g s) -> p g s", g=4),
                                       ACT.Identity).then_inc(sg["av_sb"], 1)

            reciprocal_root(None, act, sg, "rstd", None, root[:, :], None, vare[:, :])
            if ctx_ln:
                reciprocal_root(None, act, sg, "c_rstd", None, croot[:, :], None, cvare[:, :])
            items(opening(Unit(0, 0)))
            units(act, B, lambda un, prev, nxt: items(walk(un, prev, nxt)))
            items(closing(Unit(B // 2 - 1, 1)))

        @block.vector
        def _(dve):
            if not in_mask:
                dve.memset(amb[:, :, :], 0.0).then_inc(sg["amb_zero"], 1)

            def items(seq):
                for st, k, un in seq:
                    later = not (isinstance(un.pair, int) and un.pair * 2 + un.k == 0)
                    if st == "STAT":
                        if not later:
                            dve.wait_ge(*sg.once("rstd", 6))
                        else:
                            dve.wait_ge(*sg.at("xt_psum", un.step(-1)))
                        if rms:
                            dve.tensor_scalar(xn[:, :], x[:, un.n, :], m["rs"][:, bass.ds(un.n, 1)], None, ALU.mult)\
                               .then_inc(sg["xn"], 1)
                        else:
                            dve.tensor_scalar(xn[:, :], x[:, un.n, :], m["mv"][:, un.n, 0:1],
                                              m["rs"][:, bass.ds(un.n, 1)], ALU.subtract, ALU.mult)\
                               .then_inc(sg["xn"], 1)
                    if st == "STAT" and in_mask:
                        dve.wait_ge(*sg.loaded("mask_in", un))
                        if later and not (isinstance(un.pair, int) and un.pair * 2 + un.k == 1):
                            dve.wait_ge(*sg.at("p_masked", un.step(-2)))
                        dve.tensor_scalar(m2[:, un.par, :, :], miT[:, un.par, :, :], 0.0, 2.0,
                                          ALU.not_equal, ALU.mult).then_inc(sg["m_two"], 1)
                    elif st == "C":
                        if k == 0:
                            dve.wait_ge(*sg.loaded("tok_in", un))
                            if not later:
                                dve.wait_ge(*sg.once("c_rstd", 6))
                        if later:
                            dve.wait_ge(*sg.at("ct_psum", un.step(-1), k + 1))
                        dve.tensor_scalar(cxn[:, k, :], ctok[:, un.par, k, :], m["cmv"][:, un.n * NK + k, 0:1],
                                          m["crs"][:, bass.ds(un.n * NK + k, 1)], ALU.subtract, ALU.mult)\
                           .then_inc(sg["cxn"], 1)
                    elif st == "ANY":
                        dve.wait_ge(*sg.at("any_psum", un))
                        dve.tensor_scalar(anyB[:, un.par, :], PS[:, BANK["ANY"], 0:S], 1.0, None, ALU.min)\
                           .then_inc(sg["any_sb"], 1)
                        dve.wait_ge(*sg.at("any_sb", un))
                        dve.tensor_scalar(aoff[:, :], anyB[:, un.par, :], -2.0, 2.0, ALU.mult, ALU.add)\
                           .then_inc(sg["any_off"], 1)
                        dve.wait_ge(*sg.at("any_off", un))
                        dve.tensor_tensor(m2[:, un.par, :, :], m2[:, un.par, :, :],
                                          aoff[0:KS, :].unsqueeze(1).broadcast_to([KS, NK, S]), ALU.max)\
                           .then_inc(sg["m_ready"], 1)
                        dve.wait_ge(*sg.at("m_bias", un))
                        dve.tensor_reduce(amb[:, un.par, :], mb[:, un.par, :], axis=AX.X, op=ALU.max)\
                           .then_inc(sg["m_max"], 1)
                    elif st == "S":
                        h = head(k)[0]
                        wait = (lambda sig: wait_apart(dve, sg, sig)) if masked else (lambda sig: dve.wait_ge(*sig))
                        wait(sg.at("s_psum", un, k + 1))
                        if k == 0 and later:
                            wait(sg.at("neg_max", un.step(-1)))
                        sc = PS[0:S, 4 + k % 2, 0:KEYS]
                        if masked:
                            mask = mb[:, un.par, :] if in_mask else m["causal"][:, :]
                            if k == 0 and in_mask:
                                wait(sg.at("m_bias", un))
                            dve.tensor_tensor_reduce(out=junk[:, k % 2, 0:KEYS], in0=sc, in1=mask, scale=1.0, scalar=-3e38,
                                                     op0=ALU.add, op1=ALU.max, accum_out=mx[:, h:h + 1])\
                               .then_inc(sg["s_max"], 1)
                        else:
                            dve.reduce_max(mx[:, h:h + 1], sc, AX.X).then_inc(sg["s_max"], 1)
                    elif st == "NM":
                        dve.wait_ge(*sg.at("s_max", un))
                        if not in_mask and not later:
                            dve.wait_ge(*sg.once("amb_zero", 1))
                        dve.tensor_scalar(nmx[:, :], mx[:, :], amb[:, un.par, :], -1.0, ALU.subtract, ALU.mult)\
                           .then_inc(sg["neg_max"], 1)
                        dve.wait_ge(*sg.at("neg_max", un))
                        if later:
                            dve.wait_ge(*sg.at("nm_psum", un.step(-1)))
                        src = nmx[:, :].unsqueeze(1).broadcast_to([S, 4, H])
                        dve.tensor_copy(nmb[:, :, 0, :], src).then_inc(sg["neg_hi"], 1)
                        dve.wait_ge(*sg.at("neg_hi", un))
                        dve.tensor_tensor(nmb[:, :, 1, :], src, nmb[:, :, 0, :], ALU.subtract)\
                           .then_inc(sg["neg_lo"], 1)
                    elif st == "T" and masked:
                        i, kt = k // NK, k % NK
                        dve.wait_ge(*sg.at("p_exp", un, k + 1))
                        if in_mask and k == 0:
                            dve.wait_ge(*sg.at("m_ready", un))
                        mT = m2[:, un.par, kt, :] if in_mask else m["causalT"][:, 0, :]
                        dve.tensor_tensor(P[:, i, kt, :, :], P[:, i, kt, :, :],
                                          mT.unsqueeze(1).broadcast_to([KS, 8, S]), ALU.min)\
                           .then_inc(sg["p_masked"], 1)
                    elif st == "Q":
                        dve.wait_ge(*sg.at("q_psum", un))
                        if in_mask:
                            dve.wait_ge(*sg.at("any_sb", un))
                        for c in range(C):
                            src = PS[:, BANK["Q"], c * S:(c + 1) * S]
                            for e in range(2):
                                dst, qm = qT[:, un.par, 2 * c + e, :], m["qmask"][:, e:e + 1]
                                if in_mask:
                                    ins = dve.scalar_tensor_tensor(dst, src, qm, anyB[:, un.par, :], ALU.mult,
                                                                   ALU.mult)
                                elif bias:
                                    ins = dve.tensor_scalar(dst, src, col("bq", c), qm, ALU.add, ALU.mult)
                                else:
                                    ins = dve.tensor_scalar(dst, src, qm, None, ALU.mult)
                        ins.then_inc(sg["q_sb"], 1)
                    elif st == "V":
                        dve.wait_ge(*sg.at("v_psum", un, k + 1))
                        dst = vA[:, un.par, k, :, 0:HD]
                        src = PS[0:KS, BANK[f"V{k}"], 0:D].rearrange("p (h d) -> p h d", h=H)
                        if bias:
                            dve.tensor_tensor(dst, src, row("bv", KS).rearrange("p (h d) -> p h d", h=H), ALU.add)\
                               .then_inc(sg["v_sb"], 1)
                        else:
                            dve.tensor_copy(dst, src).then_inc(sg["v_sb"], 1)
                    elif st == "T1":
                        src = PS[0:S, BANK["T1"], :].rearrange("p (i e j c) -> p i e j c", i=2, e=2, j=4)
                        dve.wait_ge(*sg.at("t1_psum", un))
                        dve.reciprocal(rden[:, :, :], PS[0:S, BANK["T1"], :]
                                       .rearrange("p (g j c) -> p g j c", g=4, j=4)[:, :, :, HD])\
                           .then_inc(sg["rden"], 1)
                        dve.wait_ge(*sg.at("rden", un))
                        if later:
                            dve.wait_ge(*sg.at("ot_psum", un.step(-1)))
                        dst = on[:, :].rearrange("p (i j e d) -> p i e j d", i=2, j=4, e=2)
                        for i in range(2):
                            for e in range(2):
                                ins = dve.tensor_tensor(dst[:, i, e], src[:, i, e, :, 0:HD],
                                                        rden[:, 2 * i + e, :].unsqueeze(2).broadcast_to([S, 4, HD]),
                                                        ALU.mult)
                        ins.then_inc(sg["o_norm"], 1)
                    elif st == "O":
                        dve.wait_ge(*sg.at("o_psum", un))
                        if bias:
                            dve.wait_ge(*sg.at("xbias", un))
                        dve.tensor_tensor(x[:, un.n, :], PS[0:S, BANK["O"], 0:D], x[:, un.n, :], ALU.add)\
                           .then_inc(sg["x_new"], 1)
                        if following:
                            wait_apart(dve, sg, sg.at("x_new", un))
                            if later:
                                wait_apart(dve, sg, sg.at("x_kept", un.step(-1)))
                            token_stats(dve, sg, m, un.n, un, 1)

            if rms:
                mean_square(dve, sg, m, sq[:, :])
            reciprocal_root(dve, None, sg, "rstd", sq[:, :] if rms else m["mv"][:, :, 1], root[:, :], m["rs"][:, :], vare[:, :])
            if ctx_ln:
                reciprocal_root(dve, None, sg, "c_rstd", m["cmv"][:, :, 1], croot[:, :], m["crs"][:, :], cvare[:, :])
            items(opening(Unit(0, 0)))
            units(dve, B, lambda un, prev, nxt: items(walk(un, prev, nxt)))
            items(closing(Unit(B // 2 - 1, 1)))

        @block.tensor
        def _(pe):
            user = {6: None, 7: None}

            def take(st, un):
                b = BANK[st]
                if user[b]:
                    was, w = user[b]
                    sem, k = READ_BY[was]
                    pe.wait_ge(*sg.at(sem, w, k))
                user[b] = (st, un)

            def items(seq):
                for st, k, un in seq:
                    if st == "XT":
                        pe.wait_ge(*sg.at("xn", un))
                        take("XT", un)
                        for c in range(C):
                            ins = pe.transpose(PS[:, BANK["XT"], c * S:(c + 1) * S], xn[:, c * 128:(c + 1) * 128],
                                               ident[0:S, 0:S])
                        ins.then_inc(sg["xt_psum"], 1)
                    elif st == "C":
                        pe.wait_ge(*sg.at("cxn", un, k + 1))
                        take(f"C{k}", un)
                        for c in range(C):
                            ins = pe.transpose(PS[:, BANK[f"C{k}"], c * KS:(c + 1) * KS],
                                               cxn[:, k, c * 128:(c + 1) * 128], ident[0:KS, 0:KS])
                        ins.then_inc(sg["ct_psum"], 1)
                    elif st == "ANY":
                        pe.wait_ge(*sg.at("m_two", un))
                        take("ANY", un)
                        for kt in range(NK):
                            ins = pe.matmul(PS[:, BANK["ANY"], 0:S], m["onesb"][0:KS, :], m2[:, un.par, kt, :],
                                            start=kt == 0, stop=kt == NK - 1)
                        ins.then_inc(sg["any_psum"], 1)
                    elif st == "K":
                        if cross:
                            if k == 0:
                                pe.wait_ge(*(sg.at("ct_sb", un) if ctx_ln else sg.loaded("ctx_in", un)))
                            take(f"K{k}", un)
                            for c in range(C):
                                ins = pe.matmul(PS[:, BANK[f"K{k}"], 0:SC], wk[:, c, k * 128:(k + 1) * 128],
                                                keysT(un)[:, c, :], start=c == 0, stop=c == C - 1)
                        else:
                            pe.wait_ge(*sg.at("xt_sb", un))
                            take("K0", un)
                            for mo in range(C):
                                for c in range(C):
                                    ins = pe.matmul(PS[:, BANK["K0"], mo * S:(mo + 1) * S],
                                                    wk[:, c, mo * 128:(mo + 1) * 128], xT[:, c, :],
                                                    start=c == 0, stop=c == C - 1)
                        ins.then_inc(sg["k_psum"], 1)
                    elif st == "V":
                        take(f"V{k}", un)
                        src = keysT(un) if cross else xT
                        for c in range(C):
                            ins = pe.matmul(PS[0:KS, BANK[f"V{k}"], 0:D], src[:, c, k * KS:(k + 1) * KS],
                                            wv[:, c, :], start=c == 0, stop=c == C - 1)
                        ins.then_inc(sg["v_psum"], 1)
                    elif st == "Q":
                        pe.wait_ge(*sg.at("xt_sb", un))
                        take("Q", un)
                        for mo in range(C):
                            for c in range(C):
                                ins = pe.matmul(PS[:, BANK["Q"], mo * S:(mo + 1) * S],
                                                wq[:, c, mo * 128:(mo + 1) * 128], xT[:, c, :],
                                                start=c == 0, stop=c == C - 1)
                        ins.then_inc(sg["q_psum"], 1)
                    elif st == "S":
                        h, i, j, e = head(k)
                        later = not (isinstance(un.pair, int) and un.pair * 2 + un.k == 0)
                        if k == 0:
                            pe.wait_ge(*sg.at("q_sb", un))
                            pe.wait_ge(*sg.at("k_sb", un))
                        if k >= 2:
                            pe.wait_ge(*sg.at("s_max", un, k - 1))
                        elif later:
                            pe.wait_ge(*sg.at("s_max", un.step(-1), 15 + k))
                        r = slice(32 * j, 32 * j + 32)
                        pe.matmul(PS[0:S, 4 + k % 2, 0:KEYS], qT[r, un.par, 2 * i + e, :], kT[r, un.par, i, :],
                                  start=True, stop=True).then_inc(sg["s_psum"], 1)
                    elif st == "NM":
                        pe.wait_ge(*sg.at("neg_lo", un))
                        take("NM", un)
                        pe.transpose(PS[:, BANK["NM"], 0:S // 2].bitcast(BF16),
                                     nmb[:, :, :, :].rearrange("p a b c -> p (a b c)"), identb[0:S, 0:S])\
                          .then_inc(sg["nm_psum"], 1)
                    elif st == "T":
                        i, kt = k // NK, k % NK
                        later = not (isinstance(un.pair, int) and un.pair * 2 + un.k == 0)
                        if k == 0:
                            pe.wait_ge(*sg.at("nm_sb", un))
                        if k >= 1:
                            pe.wait_ge(*sg.at("p_exp", un, k))
                        elif later:
                            pe.wait_ge(*sg.at("p_exp", un.step(-1)))
                        for j in range(4):
                            r = slice(32 * j, 32 * j + 32)
                            pe.matmul(PS[0:KS, j, 0:2 * S], kT[r, un.par, i, kt * KS:(kt + 1) * KS],
                                      qT[r, un.par, 2 * i:2 * i + 2, :], start=True, stop=False)
                        for j in range(4):
                            r = slice(32 * j, 32 * j + 32)
                            ins = pe.matmul(PS[0:KS, j, 0:2 * S], m["onesb"][r, 0:KS],
                                            nmT[r, 2 * i:2 * i + 2, :], start=False, stop=True)
                        ins.then_inc(sg["t_psum"], 1)
                    elif st == "AV":
                        i = k
                        pe.wait_ge(*sg.at("p_masked" if masked else "p_exp", un, (i + 1) * NK))
                        if i == 0:
                            if not (isinstance(un.pair, int) and un.pair * 2 + un.k > 0):
                                pe.wait_ge(*sg.once("v_const", 2))
                            pe.wait_ge(*sg.at("v_sb", un))
                            take("AV", un)
                        for e in range(2):
                            g = 2 * i + e
                            for kt in range(NK):
                                for j in range(4):
                                    ins = pe.matmul(PS[32 * j:32 * j + 32, BANK["AV"], g * S:(g + 1) * S],
                                                    vA[:, un.par, kt, 8 * i + 2 * j + e, :], P[:, i, kt, 2 * j + e, :],
                                                    start=kt == 0, stop=kt == NK - 1)
                        ins.then_inc(sg["av_psum"], 1)
                    elif st == "T1":
                        pe.wait_ge(*sg.at("av_sb", un))
                        take("T1", un)
                        for g in range(4):
                            ins = pe.transpose(PS[0:S, BANK["T1"], g * 128:(g + 1) * 128], avT[:, g, :], ident[:, :])
                        ins.then_inc(sg["t1_psum"], 1)
                    elif st == "OT":
                        pe.wait_ge(*sg.at("o_norm", un))
                        take("OT", un)
                        for c in range(C):
                            ins = pe.transpose(PS[:, BANK["OT"], c * S:(c + 1) * S], on[:, c * 128:(c + 1) * 128],
                                               ident[0:S, 0:S])
                        ins.then_inc(sg["ot_psum"], 1)
                    elif st == "O":
                        pe.wait_ge(*sg.at("ot_sb", un))
                        take("O", un)
                        for c in range(C):
                            ins = pe.matmul(PS[0:S, BANK["O"], 0:D], oT[:, c, :], wo[:, c, :], start=c == 0,
                                            stop=c == C - 1)
                        ins.then_inc(sg["o_psum"], 1)

            def body(un, prev, nxt):
                if prev:
                    for b, (st, w) in list(user.items()):
                        user[b] = (st, un.step(w.k - body.at - 1))
                items(walk(un, prev, nxt))
                body.at = un.k

            items(opening(Unit(0, 0)))
            body.at = 0
            units(pe, B, body)
            items(closing(Unit(B // 2 - 1, 1)))
    sg.end(B, v_const=2, **(dict(msq=2) if rms else {}), **({} if in_mask else dict(amb_zero=1)), rstd=6, rstd_root=1, **(dict(c_rstd=6, c_rstd_root=1) if ctx_ln else {}))


def ffn(nc, t, m, sg, name, following):
    moe = name == "MOE"
    npass = 1 + E if moe else 1
    w0 = {"MOE": 0, "F2": 1 + E, "F3": 2 + E}[name]
    PS, x, ident = m["psum"], m["x"], m["ident"]
    act_fn = ACT.Silu if moe else ACT.Gelu

    def col(p, c):
        at = COLS[name + p] + c
        return m["col"][:, at:at + 1]

    steps = npass * NTILES
    sg.phase(c_in0=32, c_in1=32, c_stats=3 * TB, c_moments=TB, x_stats=TB, x_moments=TB, x_kept=TB, c_kept=TB, f_xn=TB, f_xbias=TB, f_xt_psum=TB, f_xt_sb=TB, f_copied=1,
             lg_psum=TB, top=TB, topi=TB, topf=TB, gdiff=1, gexp=1, gden=1, grec=1, gsec=1, lg_sb=1, gtwo=TB, gates_in=1,
             gates_set=TB)
    per_tile = dict(sg.per)
    sg.phase(h_psum=HC, h_sb=HC, y_psum=TB, y_acc=TB)
    per_step = dict(sg.per)
    sg.phase(w_in0=0, w_in1=0)
    sg.per = {**per_tile, **per_step}
    win = [sg.left["w_in0"], sg.left["w_in1"]]
    with ExitStack() as stk:
        def sb(nm, shape, dt=F32):
            return stk.enter_context(nc.sbuf_tensor(name + nm, shape, dt))
        NB = 2 if moe else 1
        w1 = [sb(f"w1{i}", [128, C, HID]) for i in range(NB)]
        w2 = [sb(f"w2{i}", [128, HC, D]) for i in range(NB)]
        xn = sb("xn", [S, 2, D])
        root, vare, sq = sb("root", [S, B]), sb("vare", [S, B]), sb("sq", [S, B])
        hnS = sb("hnS", [128, 2, C, TOK])
        hT = sb("hT", [128, HC, TOK])
        if moe:
            hn = sb("hn", [128, NTILES, C, TOK])
            gw = sb("gw", [128, C, E])
            gates = sb("gates", [S, B, E])
            top, topi, topf = sb("top", [S, TB, 8]), sb("topi", [S, TB, 8], U32), sb("topf", [S, TB, 2])
            gd, ge, gn, g1, g2 = (sb(f"g{k}", [S, TB]) for k in range(5))
            one, two = sb("one", [S, TB, E]), sb("two", [S, TB, E])
            lgs = sb("lgs", [S, TB, E])
            ctok, cst = sb("ctok", [KT_CTX, 2, 3, D]), sb("cst", [KT_CTX, 2, 3, 6])
            cmvs = sb("cmvs", [KT_CTX, 2, 3, 2])
        block = stk.enter_context(nc.Block())

        def nth(un):
            return un.n

        @block.sync
        def _(sp):
            if moe:
                sp.dma_start(gw[:, :, :], t["gate_w"]).then_inc(sg["gates_in"], 16)
            for p in range(npass):
                if p == 2:
                    for r in range(2):
                        sp.dma_start(ctok[:, r, :, :], t["ctx"][r].rearrange("(k p) d -> p k d", p=KT_CTX))\
                          .then_inc(sg[f"c_in{r}"], 16)
                    with sp.Fori(0, B // 2 - 1) as pair:
                        for r in range(2):
                            sp.wait_ge(sg["c_moments"], pair * 2 + (sg.left["c_moments"] + 1 + r))
                            sp.dma_start(ctok[:, r, :, :],
                                         t["ctx"][pair * 2 + (2 + r)].rearrange("(k p) d -> p k d", p=KT_CTX))\
                              .then_inc(sg[f"c_in{r}"], 16)
                if p >= 2:
                    sp.wait_ge(*sg.at("y_psum", (p - 2) * NTILES + NTILES - 1))
                sp.dma_start(w1[p % 2][:, :, :], t["ffn_w1"][w0 + p]).then_inc(sg[f"w_in{p % 2}"], 16)
                sp.dma_start(w2[p % 2][:, :, :], t["ffn_w2"][w0 + p]).then_inc(sg[f"w_in{p % 2}"], 16)

        def first_pass(eng, norm, main):
            norm(Unit(0, 0))

            def body(un, prev, nxt):
                main(un)
                if nxt:
                    norm(nxt)
            units(eng, NTILES, body)

        def other_passes(eng, main):
            if not moe:
                return
            def turn(pair):
                for k in (1, 2):
                    with eng.Fori(0, NTILES) as tile:
                        main(pair, k, tile)
            with eng.Fori(0, E // 2 - 1) as pair:
                turn(pair)
            turn(E // 2 - 1)

        def is_first(un):
            return isinstance(un.pair, int) and un.pair * 2 + un.k == 0

        @block.gpsimd
        def _(pool):
            def norm(un):
                if not moe:
                    for r in range(TB):
                        b = un.n * TB + r
                        pool.wait_ge(*sg.at("f_xn", un, r + 1))
                        pool.tensor_tensor(x[:, b, :], x[:, b, :], m["row"][0:S, ROWS[name + "b2"], :], ALU.add)\
                            .then_inc(sg["f_xbias"], 1)
                if moe:
                    pool.wait_ge(*sg.at("f_xt_sb", un))
                    pool.tensor_copy(hn[:, un.n, :, :], hnS[:, un.par, :, :]).then_inc(sg["f_copied"], 1)
            first_pass(pool, norm, lambda un: None)

        @block.scalar
        def _(act):
            def norm(un):
                for r in range(TB):
                    act.wait_ge(*sg.at("f_xt_psum", un, r + 1))
                    if r == 0 and not is_first(un):
                        if not is_first(un.step(-1)):
                            act.wait_ge(*sg.at("y_psum", un.step(-2)))
                            if moe:
                                act.wait_ge(*sg.at("f_copied", un.step(-2)))
                    for c in range(C):
                        ins = act.activation(hnS[:, un.par, c, r * S:(r + 1) * S], PS[:, 6, c * S:(c + 1) * S],
                                             ACT.Identity, bias=0.0 if moe else col("b", c), scale=col("g", c))
                    ins.then_inc(sg["f_xt_sb"], 1)
                if moe:
                    act.wait_ge(*sg.at("gdiff", un))
                    act.activation(ge[:, :], gd[:, :], ACT.Exp).then_inc(sg["gexp"], 1)

            def hidden(step):
                for hc in range(HC):
                    act.wait_ge(*sg.at("h_psum", step, hc + 1))
                    act.activation(hT[:, hc, :], PS[:, hc % 4, 0:TOK], act_fn,
                                   bias=0.0 if moe else m["fb1"][:, w0 - 1 - E, hc:hc + 1]).then_inc(sg["h_sb"], 1)
            reciprocal_root(None, act, sg, "rstd", None, root[:, :], None, vare[:, :])
            first_pass(act, norm, lambda un: hidden(un))
            other_passes(act, lambda pair, k, tile: hidden(pair * (2 * NTILES) + tile + k * NTILES))

        @block.vector
        def _(dve):
            def norm(un):
                for r in range(TB):
                    if is_first(un) and r == 0:
                        dve.wait_ge(*sg.once("rstd", 6))
                    if r >= 2:
                        dve.wait_ge(*sg.at("f_xt_psum", un, r - 1))
                    elif not is_first(un):
                        dve.wait_ge(*sg.at("f_xt_psum", un.step(-1), TB + r - 1))
                    b = un.n * TB + r
                    if moe:
                        dve.tensor_scalar(xn[:, r % 2, :], x[:, b, :], m["rs"][:, bass.ds(b, 1)], None, ALU.mult)\
                           .then_inc(sg["f_xn"], 1)
                    else:
                        dve.tensor_scalar(xn[:, r % 2, :], x[:, b, :], m["mv"][:, b, 0:1],
                                          m["rs"][:, bass.ds(b, 1)], ALU.subtract, ALU.mult)\
                           .then_inc(sg["f_xn"], 1)
                if not moe:
                    return
                for r in range(TB):
                    n = un.n * (TB * 3) + r * 3
                    sem = sg.sems[f"c_in{r % 2}"]
                    wait_apart(dve, sg, (sem, un.n * 32 + (sg.left[f"c_in{r % 2}"] + 16 * (r // 2 + 1))))
                    if r >= 2:
                        wait_apart(dve, sg, sg.at("c_kept", un, r - 1))
                    elif not is_first(un):
                        wait_apart(dve, sg, sg.at("c_kept", un.step(-1), TB + r - 1))
                    for kt in range(3):
                        dve.bn_stats(cst[:, r % 2, kt, :], ctok[:, r % 2, kt, :]).then_inc(sg["c_stats"], 1)
                    for kt in range(3):
                        wait_apart(dve, sg, sg.at("c_stats", un, 3 * r + kt + 1))
                        ins = dve.bn_aggr(cmvs[:, r % 2, kt, :], cst[:, r % 2, kt, :])
                    ins.then_inc(sg["c_moments"], 1)
                    wait_apart(dve, sg, sg.at("c_moments", un, r + 1))
                    dve.tensor_copy(m["cmv"][:, bass.ds(n, 3), :], cmvs[:, r % 2, :, :]).then_inc(sg["c_kept"], 1)
                dve.wait_ge(*sg.at("lg_psum", un))
                dve.tensor_copy(lgs[:, :, :].rearrange("p r e -> p (r e)"), PS[0:S, 7, 0:TB * E])\
                   .then_inc(sg["lg_sb"], 1)
                wait_apart(dve, sg, sg.at("lg_sb", un))
                for r in range(TB):
                    dve.max(top[:, r, :], lgs[:, r, :]).then_inc(sg["top"], 1)
                for r in range(TB):
                    wait_apart(dve, sg, sg.at("top", un, r + 1))
                    dve.max_index(topi[:, r, :], top[:, r, :], lgs[:, r, :]).then_inc(sg["topi"], 1)
                dve.tensor_tensor(gd[:, :], top[:, :, 1], top[:, :, 0], ALU.subtract).then_inc(sg["gdiff"], 1)
                for r in range(TB):
                    dve.wait_ge(*sg.at("topi", un, r + 1))
                    dve.tensor_copy(topf[:, r, :], topi[:, r, 0:2]).then_inc(sg["topf"], 1)
                dve.wait_ge(*sg.at("gexp", un))
                dve.tensor_scalar(gn[:, :], ge[:, :], 1.0, None, ALU.add).then_inc(sg["gden"], 1)
                dve.wait_ge(*sg.at("gden", un))
                dve.reciprocal(g1[:, :], gn[:, :]).then_inc(sg["grec"], 1)
                dve.wait_ge(*sg.at("grec", un))
                dve.tensor_tensor(g2[:, :], ge[:, :], g1[:, :], ALU.mult).then_inc(sg["gsec"], 1)
                dve.wait_ge(*sg.at("gsec", un))
                dve.wait_ge(*sg.at("topf", un))
                for r in range(TB):
                    dve.tensor_scalar(one[:, r, :], m["iota"][0:S, :], topf[:, r, 0:1], g1[:, r:r + 1], ALU.is_equal,
                                      ALU.mult)
                    dve.tensor_scalar(two[:, r, :], m["iota"][0:S, :], topf[:, r, 1:2], g2[:, r:r + 1], ALU.is_equal,
                                      ALU.mult).then_inc(sg["gtwo"], 1)
                for r in range(TB):
                    dve.wait_ge(*sg.at("gtwo", un, r + 1))
                    dve.tensor_tensor(gates[:, un.n * TB + r, :], one[:, r, :], two[:, r, :], ALU.add)\
                       .then_inc(sg["gates_set"], 1)

            def stats_after(step, tile, r, b, very_first):
                wait_apart(dve, sg, sg.at("y_acc", step, r + 1))
                if not very_first:
                    wait_apart(dve, sg, sg.at("x_kept", tile, r))
                token_stats(dve, sg, m, b, tile, r + 1)

            def shared(un):
                for r in range(TB):
                    b = un.n * TB + r
                    dve.wait_ge(*sg.at("y_psum", un, r + 1))
                    if not moe:
                        dve.wait_ge(*sg.at("f_xbias", un, r + 1))
                    dve.tensor_tensor(x[:, b, :], PS[0:S, 4 + r % 2, 0:D], x[:, b, :], ALU.add)\
                       .then_inc(sg["y_acc"], 1)
                    if following and not moe:
                        stats_after(un, un, r, b, is_first(un) and r == 0)

            def routed(pair, k, tile):
                step = pair * (2 * NTILES) + tile + k * NTILES
                last = following and isinstance(pair, int) and k == 2
                for r in range(TB):
                    b = tile * TB + r
                    dve.wait_ge(*sg.at("y_psum", step, r + 1))
                    if r == 0:
                        dve.wait_ge(*sg.at("gates_set", NTILES - 1))
                    e = pair * 2 + (k - 1)
                    dve.wait_ge(*sg.at("y_acc", step, r - TB * NTILES))
                    dve.scalar_tensor_tensor(x[:, b, :], PS[0:S, 4 + r % 2, 0:D],
                                             gates[:, b, bass.ds(e, 1)], x[:, b, :],
                                             ALU.mult, ALU.add).then_inc(sg["y_acc"], 1)
                    if last:
                        stats_after(step, tile, r, b, False)
            if moe:
                mean_square(dve, sg, m, sq[:, :])
            reciprocal_root(dve, None, sg, "rstd", sq[:, :] if moe else m["mv"][:, :, 1], root[:, :], m["rs"][:, :], vare[:, :])
            first_pass(dve, norm, shared)
            other_passes(dve, routed)

        @block.tensor
        def _(pe):
            def norm(un):
                for r in range(TB):
                    pe.wait_ge(*sg.at("f_xn", un, r + 1))
                    if r >= 1:
                        pe.wait_ge(*sg.at("f_xt_sb", un, r))
                    elif not is_first(un):
                        pe.wait_ge(*sg.at("f_xt_sb", un.step(-1)))
                    for c in range(C):
                        ins = pe.transpose(PS[:, 6, c * S:(c + 1) * S], xn[:, r % 2, c * 128:(c + 1) * 128],
                                           ident[0:S, 0:S])
                    ins.then_inc(sg["f_xt_psum"], 1)
                if moe:
                    if is_first(un):
                        pe.wait_ge(sg["gates_in"], 16)
                    else:
                        pe.wait_ge(*sg.at("lg_sb", un.step(-1)))
                    for r in range(TB):
                        pe.wait_ge(*sg.at("f_xt_sb", un, r + 1))
                        for c in range(C):
                            ins = pe.matmul(PS[0:S, 7, r * E:(r + 1) * E], hnS[:, un.par, c, r * S:(r + 1) * S],
                                            gw[:, c, :], start=c == 0, stop=c == C - 1)
                        ins.then_inc(sg["lg_psum"], 1)

            def products(step, w, src, first):
                for hc in range(HC):
                    if hc >= 4:
                        pe.wait_ge(*sg.at("h_sb", step, hc - 3))
                    elif not first:
                        pe.wait_ge(*sg.at("h_sb", step, hc - 3))
                    for c in range(C):
                        ins = pe.matmul(PS[:, hc % 4, 0:TOK], w1[w][:, c, hc * 128:(hc + 1) * 128], src(c),
                                        start=c == 0, stop=c == C - 1)
                    ins.then_inc(sg["h_psum"], 1)
                for r in range(TB):
                    if r >= 2:
                        pe.wait_ge(*sg.at("y_acc", step, r - 1))
                    elif not first:
                        pe.wait_ge(*sg.at("y_acc", step, r - 1))
                    for hc in range(HC):
                        if r == 0:
                            pe.wait_ge(*sg.at("h_sb", step, hc + 1))
                        ins = pe.matmul(PS[0:S, 4 + r % 2, 0:D], hT[:, hc, r * S:(r + 1) * S], w2[w][:, hc, :],
                                        start=hc == 0, stop=hc == HC - 1)
                    ins.then_inc(sg["y_psum"], 1)

            def shared(un):
                if is_first(un):
                    pe.wait_ge(sg["w_in0"], win[0] + 32)
                pe.wait_ge(*sg.at("f_xt_sb", un))
                products(un, 0, lambda c: hnS[:, un.par, c, :], is_first(un))

            def routed(pair, k, tile):
                pe.wait_ge(sg[f"w_in{k % 2}"], pair * 32 + (win[k % 2] + (32 if k == 1 else 64)))
                pe.wait_ge(*sg.at("f_copied", NTILES - 1)) if moe else None
                products(pair * (2 * NTILES) + tile + k * NTILES, k % 2, lambda c: hn[:, tile, c, :], False)
            first_pass(pe, norm, shared)
            other_passes(pe, routed)
    for p in range(npass):
        sg.left[f"w_in{p % 2}"] += 32
    sg.per = per_tile
    if not moe:
        for s in ("c_in0", "c_in1", "c_stats", "c_moments", "c_kept", "f_copied", "lg_psum", "top", "topi", "topf", "gdiff", "gexp",
                  "gden", "grec", "gsec", "lg_sb", "gtwo", "gates_in", "gates_set"):
            sg.per.pop(s)
    else:
        sg.per.pop("f_xbias")
    if not following:
        for s in ("x_stats", "x_moments", "x_kept"):
            sg.per.pop(s)
    sg.end(NTILES, rstd=6, rstd_root=1, **(dict(msq=2) if moe else {}))
    sg.per = per_step
    sg.end(steps)


def build_inputs(inputs):
    g = {k: np.asarray(v) for k, v in inputs.items()}
    f = np.float32

    def chunks(w):
        return w.reshape(-1, 128, w.shape[-1]).transpose(1, 0, 2)

    def cols(v):
        return v.reshape(-1, 128).T

    wt = {"L0": [g[f"L0_xattn_W{p}"].T for p in "qkvo"],
          "L1S": [g[f"L1_xattn_sa_w{p}"].T for p in "qkvo"],
          "L1C": [g[f"L1_xattn_ca_w{p}"].T for p in "qkvo"],
          "L2": [g[f"L2_xattn_w{p}"] for p in "qkvo"],
          "L3S": [g["L3_xattn_attn_qkv_w"][i * D:(i + 1) * D].T for i in range(3)] + [g["L3_xattn_attn_proj_w"].T],
          "L3C": [g[f"L3_xattn_{p}_w"].T for p in ("q", "k", "v", "ca_proj")]}
    qkv_b = g["L3_xattn_attn_qkv_b"]
    zero, one = np.zeros(D, f), np.ones(D, f)
    vec = {"L0g": g["L0_xattn_ln_gamma"], "L0b": g["L0_xattn_ln_beta"], "L0bq": g["L0_xattn_bq"],
           "L0bk": g["L0_xattn_bk"], "L1Sg": g["L1_xattn_norm1_w"], "L1Cg": g["L1_xattn_norm2_w"],
           "MOEg": g["L1_xattn_norm3_w"],
           "L2g": g["L2_xattn_ln1_g"], "L2b": g["L2_xattn_ln1_b"], "L2bq": g["L2_xattn_bq"], "L2bk": g["L2_xattn_bk"],
           "F2g": g["L2_xattn_ln2_g"], "F2b": g["L2_xattn_ln2_b"],
           "L3Sg": g["L3_xattn_ln1_g"], "L3Sb": g["L3_xattn_ln1_b"], "L3Sbq": qkv_b[0:D], "L3Sbk": qkv_b[D:2 * D],
           "L3Cg": g["L3_xattn_ln2_g"], "L3Cb": g["L3_xattn_ln2_b"], "L3Cbq": g["L3_xattn_q_b"],
           "L3Cbk": g["L3_xattn_k_b"], "F3g": g["L3_xattn_ln3_g"], "F3b": g["L3_xattn_ln3_b"]}
    rows = {"L0bv": g["L0_xattn_bv"], "L0bo": g["L0_xattn_bo"], "L2bv": g["L2_xattn_bv"], "L2bo": g["L2_xattn_bo"],
            "L3Sbv": qkv_b[2 * D:], "L3Sbo": g["L3_xattn_attn_proj_b"], "L3Cbv": g["L3_xattn_v_b"],
            "L3Cbo": g["L3_xattn_ca_proj_b"], "F2b2": g["L2_xattn_b2"], "F3b2": g["L3_xattn_proj_b"]}
    w1 = [g["L1_xattn_sh_w1"].T] + [w.T for w in g["L1_xattn_exp_w1"]] + [g["L2_xattn_w1"], g["L3_xattn_fc_w"].T]
    w2 = [g["L1_xattn_sh_w2"].T] + [w.T for w in g["L1_xattn_exp_w2"]] + [g["L2_xattn_w2"], g["L3_xattn_proj_w"].T]
    p = np.arange(128)
    qmask = np.stack([np.where((p // 16) % 2 == e, QK_SCALE, 0.0) for e in range(2)], 1)
    nmask = np.stack([(p % 16 == 8 * i + 2 * (p // 32) + e) * 1.0 for i in range(2) for e in range(2)], 1)
    tri = np.tril(np.ones((S, S)))
    a = {
        "x": g["x"],
        "ctx": g["ctx_1024"],
        "ctxT": g["ctx_1024"].transpose(0, 2, 1).reshape(B, C, 128, SC).transpose(0, 2, 1, 3),
        "maskL1S": g["mask_BxSxS_ik0"], "maskTL1S": g["mask_BxSxS_ik0"].transpose(0, 2, 1),
        "maskL1C": g["mask_BxSxS2_if1"], "maskTL1C": g["mask_BxSxS2_if1"].transpose(0, 2, 1),
        "attn_w": np.stack([chunks(w) for n in ATTN_NAMES for w in wt[n]], 1),
        "col": np.concatenate([cols(vec.get(n, zero)) for n in COLS], 1),
        "fb1": np.stack([cols(g["L2_xattn_b1"]), cols(g["L3_xattn_fc_b"])], 1),
        "row": np.stack([rows.get(n, zero) for n in ROWS], 0),
        "ident": np.eye(128, dtype=f), "qmask": qmask.astype(f), "nmask": nmask.astype(f),
        "causal": ((1 - tri) * NEG).astype(f), "causalT": (tri.T * 2).astype(f),
        "gate_w": chunks(g["L1_xattn_gate_w"].T),
        "ffn_w1": np.stack([chunks(w) for w in w1], 0),
        "ffn_w2": np.stack([chunks(w) for w in w2], 0),
    }
    return {k: np.ascontiguousarray(v) for k, v in a.items()}


def kernel(**inputs):
    import concourse.bacc as bacc
    from concourse.bass_utils import run_bass_kernel_spmd

    nc = bacc.Bacc("TRN2", target_bir_lowering=False, num_devices=1)
    arrays = build_inputs(inputs)
    t = {k: nc.dram_tensor(k + "_dram", v.shape, mybir.dt.from_np(v.dtype), kind="ExternalInput").ap()
         for k, v in arrays.items()}
    out = nc.dram_tensor("out_dram", (B, S, D), F32, kind="ExternalOutput").ap()
    build(nc, t, out)
    r = run_bass_kernel_spmd(nc, [{k + "_dram": v for k, v in arrays.items()}], core_ids=[0])
    return r.results[0]["out_dram"]
```

```python
import numpy as np

import concourse.bass as bass
from concourse import mybir
from contextlib import ExitStack

F32 = mybir.dt.float32
F32R = mybir.dt.float32r
BF16 = mybir.dt.bfloat16
I32 = mybir.dt.int32
U32 = mybir.dt.uint32
ALU = mybir.AluOpType
ACT = mybir.ActivationFunctionType
AX = mybir.AxisListType

B, S, SC, D = 32, 112, 375, 256
H, HD = 16, 16
C = D // 128
HID, HC = 1024, 8
E = 8
EPS = 1e-5
NEG = -65504.0
KEEP = 2.0 ** 100
QK_SCALE = HD ** -0.5
KT_CTX = 125
TB = 4
NTILES = B // TB
TOK = TB * S
SCP = SC + 1

ATTN = {
    "L0": dict(cross=True, norm="ln", mask=None, ctx_ln=False),
    "L1S": dict(cross=False, norm="rms", mask="input", ctx_ln=False),
    "L1C": dict(cross=True, norm="rms", mask="input", ctx_ln=False),
    "L2": dict(cross=True, norm="ln", mask=None, ctx_ln=True),
    "L3S": dict(cross=False, norm="ln", mask="causal", ctx_ln=False),
    "L3C": dict(cross=True, norm="ln", mask=None, ctx_ln=False),
}
ORDER = ["L0", "L1S", "L1C", "MOE", "L2", "F2", "L3S", "L3C", "F3"]
ATTN_NAMES = list(ATTN)
COLS = {}
for _n in ATTN_NAMES:
    for _p in ("g", "b", "bq", "bk"):
        COLS[_n + _p] = (len(COLS)) * 2
for _n in ("MOE", "F2", "F3"):
    for _p in ("g", "b"):
        COLS[_n + _p] = (len(COLS)) * 2
NCOL = len(COLS) * 2
ROWS = {n: i for i, n in enumerate([a + p for a in ATTN_NAMES for p in ("bv", "bo")] + ["F2b2", "F3b2"])}


class Unit:

    def __init__(self, pair, k):
        self.pair, self.k = pair, k
        self.par = k % 2
        self.n = pair * 2 + k
        self.half = pair + k // 2

    def step(self, d):
        return Unit(self.pair, self.k + d)


def units(eng, count, body):
    u = Unit(0, 0)
    body(u, None, u.step(1))
    with eng.Fori(0, count // 2 - 1) as pair:
        for k in (1, 2):
            u = Unit(pair, k)
            body(u, u.step(-1), u.step(1))
    u = Unit(count // 2 - 1, 1)
    body(u, u.step(-1), None)


class Signals:

    def __init__(self, nc, stack):
        self.nc, self.stack = nc, stack
        self.sems, self.left, self.per = {}, {}, {}

    def phase(self, **per):
        self.per = per
        for name in per:
            if name not in self.sems:
                self.sems[name] = self.stack.enter_context(self.nc.semaphore(name))
                self.left[name] = 0

    def end(self, count, **once):
        for name, per in self.per.items():
            self.left[name] += per * count
        for name, n in once.items():
            self.left[name] += n

    def once(self, name, k):
        if name not in self.sems:
            self.sems[name] = self.stack.enter_context(self.nc.semaphore(name))
            self.left[name] = 0
        return self.sems[name], self.left[name] + k

    def __getitem__(self, name):
        return self.sems[name]

    def at(self, name, unit, k=None):
        n = unit.n if isinstance(unit, Unit) else unit
        return self.sems[name], n * self.per[name] + (self.left[name] + (self.per[name] if k is None else k))

    def loaded(self, name, unit):
        name = f"{name}{unit.par}"
        return self.sems[name], unit.half * (2 * self.per[name]) + (self.left[name] + 2 * self.per[name])


def split_product(pe, out, lhsT, rhs, first, last):
    for n, (a, b) in enumerate(((0, 0), (0, 1), (1, 0))):
        ins = pe.matmul(out, lhsT[a], rhs[b], start=first and n == 0, stop=last and n == 2)
    return ins


def build(nc, t, out, order=tuple(ORDER)):
    stack = ExitStack()
    with stack:
        def sb(name, shape, dt=F32):
            return stack.enter_context(nc.sbuf_tensor(name, shape, dt))

        def pb(name, shape, dt=F32):
            return stack.enter_context(nc.psum_tensor(name, shape, dt))

        m = {}
        m["x"] = sb("x_all", [S, B, D])
        m["w"] = sb("attn_w", [128, 2, 4, C, D])
        m["wh"] = sb("attn_wh", [128, 4, C, D], F32R)
        m["wl"] = sb("attn_wl", [128, 4, C, D], F32R)
        m["col"] = sb("col", [128, NCOL])
        m["fb1"] = sb("fb1", [128, 2, HC])
        m["row"] = sb("row", [128, len(ROWS), D])
        m["ident"] = sb("ident", [128, 128])
        m["nmask"] = sb("nmask", [128, 8])
        m["hmask"] = sb("hmask", [128, 8])
        m["causal"] = sb("causal", [S, S])
        m["causalT"] = sb("causalT", [S, 1, S])
        m["identb"] = sb("identb", [128, 128], BF16)
        m["onesb"] = sb("onesb", [128, 128], BF16)
        m["onesf"] = sb("onesf", [128, 128])
        m["iota"] = sb("iota", [128, E])
        m["mv"] = sb("mv", [S, B, 2])
        m["xst"] = sb("xst", [S, 6])
        m["xmv"] = sb("xmv", [S, 2])
        m["junk"] = sb("junk", [S, 2, SC])
        m["cmv"] = sb("cmv", [KT_CTX, B * 3, 2])
        m["rs"] = sb("rs", [S, B])
        m["crs"] = sb("crs", [KT_CTX, B * 3])
        m["psum"] = pb("psum", [128, 8, 512])
        sg = Signals(nc, stack)
        for name in ("w_next", "w_hi", "w_lo", "ctx_pad", "rstd", "rstd_root", "c_rstd", "c_rstd_root", "v_const", "amb_zero", "msq", "apart"):
            sg.once(name, 0)

        kinds = ["rms" if name in ("L1S", "L1C", "MOE") else "ln" for name in order] + [None]
        prepare(nc, t, m, sg, kinds[0])
        for name, following in zip(order, kinds[1:]):
            if name in ATTN:
                attention(nc, t, m, sg, name, following)
            else:
                ffn(nc, t, m, sg, name, following)
        sg.phase(x_out=16)
        with nc.Block() as block:
            @block.sync
            def _(sp):
                sp.dma_start(out.rearrange("b s d -> s b d"), m["x"][:, :, :]).then_inc(sg["x_out"], 16)
                sp.wait_ge(sg["x_out"], 16)


def wait_apart(eng, sg, signal):
    eng.wait_ge(*signal)
    eng.sem_inc(sg["apart"], 1)


def token_stats(dve, sg, m, n, unit, k):
    dve.bn_stats(m["xst"][:, :], m["x"][:, n, :]).then_inc(sg["x_stats"], 1)
    wait_apart(dve, sg, sg.at("x_stats", unit, k))
    dve.bn_aggr(m["xmv"][:, :], m["xst"][:, :]).then_inc(sg["x_moments"], 1)
    wait_apart(dve, sg, sg.at("x_moments", unit, k))
    dve.tensor_copy(m["mv"][:, n, :], m["xmv"][:, :]).then_inc(sg["x_kept"], 1)


def mean_square(dve, sg, m, sq):
    dve.tensor_tensor(sq, m["mv"][:, :, 0], m["mv"][:, :, 0], ALU.mult).then_inc(sg["msq"], 1)
    dve.wait_ge(*sg.once("msq", 1))
    dve.tensor_tensor(sq, sq, m["mv"][:, :, 1], ALU.add).then_inc(sg["msq"], 1)
    dve.wait_ge(*sg.once("msq", 2))


def reciprocal_root(dve, act, sg, name, var, root, out, tmp):
    if act:
        act.wait_ge(*sg.once(name, 1))
        act.activation(root, tmp, ACT.Sqrt).then_inc(sg[name + "_root"], 1)
        return
    dve.tensor_scalar(tmp, var, EPS, None, ALU.add).then_inc(sg.once(name, 1)[0], 1)
    dve.wait_ge(*sg.once(name + "_root", 1))
    dve.reciprocal(out, root).then_inc(sg[name], 1)
    dve.wait_ge(*sg.once(name, 2))
    dve.tensor_tensor(root, tmp, out, ALU.mult).then_inc(sg[name], 1)
    dve.wait_ge(*sg.once(name, 3))
    dve.tensor_tensor(root, root, out, ALU.mult).then_inc(sg[name], 1)
    dve.wait_ge(*sg.once(name, 4))
    dve.tensor_scalar(root, root, -0.5, 1.5, ALU.mult, ALU.add).then_inc(sg[name], 1)
    dve.wait_ge(*sg.once(name, 5))
    dve.tensor_tensor(out, out, root, ALU.mult).then_inc(sg[name], 1)


def prepare(nc, t, m, sg, following):
    with ExitStack() as st:
        wq = m["w"][:, 0, :, :, :]
        NW = 4
        absum = st.enter_context(nc.sbuf_tensor("absum", [128, NW], F32))
        gamma = st.enter_context(nc.sbuf_tensor("gamma", [128, NW], F32))
        geps = st.enter_context(nc.sbuf_tensor("geps", [128, 2, NW], F32))
        up = st.enter_context(nc.sbuf_tensor("up", [128, NW, C, D], F32))
        dn = st.enter_context(nc.sbuf_tensor("dn", [128, NW, C, D], F32))
        sg.phase(w_in=16, const_in=16 * 8, x_in=16, x_stats=B, x_moments=B, x_kept=B, ones_set=2, ident_cast=1, absum_set=NW, gsum_psum=1,
                 gamma_set=1, geps_set=2, tern_up=NW, tern_dn=NW, tern=NW, scaled=NW, quant_diff=NW, quantised=NW)
        block = st.enter_context(nc.Block())

        @block.sync
        def _(sp):
            sp.dma_start(m["w"][:, 0, :, :, :], t["attn_w"][0]).then_inc(sg["w_in"], 16)
            for k in ("col", "fb1", "ident", "hmask", "nmask", "causal"):
                ap = m[k][:, :, :] if len(m[k].shape) == 3 else m[k][:, :]
                sp.dma_start(ap, t[k]).then_inc(sg["const_in"], 16)
            sp.dma_start(m["causalT"][:, 0, :], t["causalT"]).then_inc(sg["const_in"], 16)
            sp.dma_start(m["row"][:, :, :], t["row"].partition_broadcast(128)).then_inc(sg["const_in"], 16)
            sp.dma_start(m["x"][:, :, :], t["x"].rearrange("b s d -> s b d")).then_inc(sg["x_in"], 16)
            sp.wait_ge(sg["x_in"], 16)

        @block.gpsimd
        def _(pool):
            pool.memset(m["onesf"][:, :], 1.0).then_inc(sg["ones_set"], 1)
            pool.memset(m["onesb"][:, :], 1.0).then_inc(sg["ones_set"], 1)
            pool.iota(m["iota"][:, :], pattern=[[1, E]], base=0, channel_multiplier=0,
                      allow_small_or_imprecise_dtypes=True)
            pool.wait_ge(sg["const_in"], 16 * 8)
            pool.tensor_copy(m["identb"][:, :], m["ident"][:, :]).then_inc(sg["ident_cast"], 1)

        @block.tensor
        def _(pe):
            pe.wait_ge(sg["ones_set"], 2)
            pe.wait_ge(sg["absum_set"], NW)
            pe.matmul(m["psum"][:, 0, 0:NW], m["onesf"][:, :], absum[:, :], start=True, stop=True)\
              .then_inc(sg["gsum_psum"], 1)

        @block.vector
        def _(dve):
            dve.wait_ge(sg["w_in"], 16)
            for i in range(NW):
                dve.tensor_reduce(absum[:, i:i + 1], wq[:, i, :, :], axis=AX.XY, op=ALU.add,
                                  apply_absolute_value=True).then_inc(sg["absum_set"], 1)
            dve.wait_ge(sg["gsum_psum"], 1)
            dve.tensor_scalar(gamma[:, :], m["psum"][:, 0, 0:NW], 1.0 / (D * D), None, ALU.mult)\
               .then_inc(sg["gamma_set"], 1)
            dve.wait_ge(sg["gamma_set"], 1)
            dve.tensor_scalar(geps[:, 0, :], gamma[:, :], EPS, 0.5, ALU.add, ALU.mult).then_inc(sg["geps_set"], 1)
            dve.tensor_scalar(geps[:, 1, :], gamma[:, :], EPS, -0.5, ALU.add, ALU.mult).then_inc(sg["geps_set"], 1)
            dve.wait_ge(sg["geps_set"], 2)
            for i in range(NW):
                dve.tensor_scalar(up[:, i, :, :], wq[:, i, :, :], geps[:, 0, i:i + 1], None, ALU.is_gt)\
                   .then_inc(sg["tern_up"], 1)
                dve.tensor_scalar(dn[:, i, :, :], wq[:, i, :, :], geps[:, 1, i:i + 1], None, ALU.is_lt)\
                   .then_inc(sg["tern_dn"], 1)
            for i in range(NW):
                dve.wait_ge(sg["tern_dn"], i + 1)
                dve.tensor_tensor(up[:, i, :, :], up[:, i, :, :], dn[:, i, :, :], ALU.subtract)\
                   .then_inc(sg["tern"], 1)
            for i in range(NW):
                dve.wait_ge(sg["tern"], i + 1)
                dve.tensor_scalar(up[:, i, :, :], up[:, i, :, :], gamma[:, i:i + 1], None, ALU.mult)\
                   .then_inc(sg["scaled"], 1)
            for i in range(NW):
                dve.wait_ge(sg["scaled"], i + 1)
                dve.tensor_tensor(up[:, i, :, :], up[:, i, :, :], wq[:, i, :, :], ALU.subtract)\
                   .then_inc(sg["quant_diff"], 1)
            for i in range(NW):
                dve.wait_ge(sg["quant_diff"], i + 1)
                dve.tensor_tensor(wq[:, i, :, :], wq[:, i, :, :], up[:, i, :, :], ALU.add)\
                   .then_inc(sg["quantised"], 1)
            dve.wait_ge(sg["x_in"], 16)
            for n in range(B):
                if n:
                    dve.wait_ge(sg["x_kept"], n)
                token_stats(dve, sg, m, n, 0, n + 1)
    sg.end(1)


def attention(nc, t, m, sg, name, following):
    cfg = ATTN[name]
    cross, masked, ctx_ln, rms = cfg["cross"], cfg["mask"], cfg["ctx_ln"], cfg["norm"] == "rms"
    in_mask = masked == "input"
    a = ATTN_NAMES.index(name)
    NK, KS = (3, KT_CTX) if cross else (1, S)
    KEYS = NK * KS
    NT = 2 * NK
    bias = name not in ("L1S", "L1C")
    KP = SCP if cross else S
    Q_, K_, V_, O_ = range(4)

    def W(i, c, cols=slice(0, D)):
        return m["wh"][:, i, c, cols], m["wl"][:, i, c, cols]
    x, ident, identb = m["x"], m["ident"], m["identb"]
    PS = m["psum"]
    NKE = 2 if cross else 1

    def col(p, c):
        at = COLS[name + p] + c
        return m["col"][:, at:at + 1]

    def row(p, n):
        return m["row"][0:n, ROWS[name + p], :]

    sg.phase(
        xn=1, xt_psum=1, xt_sb=1, k_psum=NKE, k_sb=NKE, v_psum=NK, v_sb=NK, q_psum=1,
        xt_lo=1, k_lo=NKE, q_sum=1, q_hi=1, q_lo=1, qm_hi=1, qm_lo=1, ot_lo=1,
        s_psum=16, s_max=16, neg_max=2, neg_hi=2, neg_lo=2, nm_psum=2, nm_sb=2,
        t_psum=NT, p_exp=NT, av_psum=2, av_sb=2, t1_psum=1, rden=1, o_norm=1, ot_psum=1, ot_sb=1, o_psum=1, x_new=1,
        **(dict(x_stats=1, x_moments=1, x_kept=1) if following else {}),
        **(dict(xbias=1) if bias else {}),
        **(dict(ctx_in0=8, ctx_in1=8) if cross and not ctx_ln else {}),
        **(dict(c_hi=1, c_lo=1) if cross else {}),
        **(dict(tok_in0=8, tok_in1=8, cxn=NK, ct_psum=NK, ct_sb=NK) if ctx_ln else {}),
        **(dict(p_masked=NT) if masked else {}),
        **(dict(mask_in0=16, mask_in1=16, m_bias=1, m_max=1, m_two=1, any_psum=1, any_sb=1, any_off=1, m_ready=1)
           if in_mask else {}))

    TP = [("T", NK + i, "p") for i in range(NK)]
    TU = [("T", i, "u") for i in range(NK)]
    if cross:
        CX = [("C", i, "n") for i in range(3)] if ctx_ln else [None] * 3
        ANY = ("ANY", 0, "n") if in_mask else None
        steps = [("STAT", 0, "n"), ("NMD", 1, "p"), ("S", 0, "u"), ("NM", 1, "p"), ("XT", 0, "n"), ("S", 1, "u"), CX[0],
                 ("S", 2, "u"), CX[1], ANY, ("S", 3, "u"), TP[0], CX[2], ("CS", 0, "n"), ("S", 4, "u"), TP[1],
                 ("S", 5, "u"), ("Q", 0, "n"), TP[2], ("S", 6, "u"), ("AV", 1, "p"), ("K", 0, "n"), ("S", 7, "u"),
                 ("NMD", 0, "u"), ("S", 8, "u"), ("NM", 0, "u"), ("K", 1, "n"), ("S", 9, "u"), ("T1", 0, "p"),
                 ("S", 10, "u"), ("V", 0, "n"), ("S", 11, "u"), TU[0], ("OT", 0, "p"), ("S", 12, "u"), ("V", 1, "n"), TU[1],
                 ("S", 13, "u"), ("O", 0, "p"), TU[2], ("S", 14, "u"), ("AV", 0, "u"), ("V", 2, "n"), ("S", 15, "u")]
        BANK = {"T1": 6, "OT": 6, "O": 6, "K0": 7, "K1": 7, "V0": 7, "V1": 7, "V2": 6, "C0": 6, "C1": 7, "C2": 6,
                "ANY": 7, "XT": 6, "Q": 7, "NM0": 6, "NM1": 7, "AV0": 7, "AV1": 6}
    else:
        ANY = ("ANY", 0, "n") if in_mask else None
        steps = [("STAT", 0, "n"), ("NMD", 1, "p"), ("S", 0, "u"), ("NM", 1, "p"), ("XT", 0, "n"), ("S", 1, "u"), ANY,
                 ("S", 2, "u"), ("S", 3, "u"), TP[0], ("S", 4, "u"), ("Q", 0, "n"), ("S", 5, "u"), ("AV", 1, "p"),
                 ("S", 6, "u"), ("K", 0, "n"), ("S", 7, "u"), ("NMD", 0, "u"), ("S", 8, "u"), ("NM", 0, "u"),
                 ("S", 9, "u"), ("T1", 0, "p"), ("S", 10, "u"), ("S", 11, "u"), TU[0], ("OT", 0, "p"), ("S", 12, "u"),
                 ("S", 13, "u"), ("O", 0, "p"), ("AV", 0, "u"), ("S", 14, "u"), ("V", 0, "n"), ("S", 15, "u")]
        BANK = {"T1": 7, "OT": 6, "O": 7, "K0": 6, "V0": 6, "ANY": 7, "XT": 6, "Q": 6, "NM0": 7, "NM1": 7,
                "AV0": 7, "AV1": 7}
    if in_mask:
        steps = [st for st in steps if st and st[0] not in ("ANY", "Q")]
        for new, after in ((("M2", 0, "n"), TP[-1]), (("ANY", 0, "n"), ("AV", 1, "p")), (("Q", 0, "n"), ("S", 9, "u"))):
            steps.insert(steps.index(after) + 1, new)
    steps = [st for st in steps if st]
    opening_steps = [st for st in steps if st[2] == "n"]
    closing_steps = [("NMD", 1), ("NM", 1)] + [("T", NK + i) for i in range(NK)] \
        + [("AV", 1), ("T1", 0), ("OT", 0), ("O", 0)]
    READ_BY = {"T1": ("o_norm", 1), "OT": ("ot_sb", 1), "O": ("x_new", 1), "K0": ("k_lo", 1), "K1": ("k_lo", 2),
               "V0": ("v_sb", 1), "V1": ("v_sb", 2), "V2": ("v_sb", 3), "C0": ("ct_sb", 1), "C1": ("ct_sb", 2),
               "C2": ("ct_sb", 3), "ANY": ("any_sb", 1), "XT": ("xt_sb", 1), "Q": ("q_sum", 1),
               "NM0": ("nm_sb", 1), "NM1": ("nm_sb", 2), "AV0": ("av_sb", 1), "AV1": ("av_sb", 2)}

    def walk(un, prev, nxt):
        for st, k, whose in steps:
            w = {"u": un, "p": prev, "n": nxt}[whose]
            if w:
                yield st, k, w

    def opening(un):
        for st, k, _ in opening_steps:
            yield st, k, un

    def closing(un):
        for st, k in closing_steps:
            yield st, k, un

    with ExitStack() as stk:
        def sb(nm, shape, dt=F32):
            return stk.enter_context(nc.sbuf_tensor(name + nm, shape, dt))
        ctxT = sb("ctxT", [128, 2, C, SCP]) if cross and not ctx_ln else None
        cH = sb("cH", [128, C, SCP], F32R) if cross else None
        cL = sb("cL", [128, C, SCP], F32R) if cross else None
        ctok = sb("ctok", [KS, 2, NK, D]) if ctx_ln else None
        cxn = sb("cxn", [KS, NK, D]) if ctx_ln else None
        root, vare, sq = sb("root", [S, B]), sb("vare", [S, B]), sb("sq", [S, B])
        croot = sb("croot", [KS, B * NK]) if ctx_ln else None
        cvare = sb("cvare", [KS, B * NK]) if ctx_ln else None
        kH = sb("kH", [128, 2, C, KP], F32R)
        kL = sb("kL", [128, 2, C, KP], F32R)
        vA = sb("vA", [KS, 2, NK, H, 32])
        xn = sb("xn", [S, D])
        xT = sb("xT", [128, C, S])
        junk = m["junk"]
        xH, xL = sb("xH", [128, C, S], F32R), sb("xL", [128, C, S], F32R)
        qf = sb("qf", [128, C, S])
        qH, qL = sb("qH", [128, C, S], F32R), sb("qL", [128, C, S], F32R)
        qmH = sb("qmH", [128, 2, C, 8, S], F32R)
        qmL = sb("qmL", [128, 2, C, 8, S], F32R)
        oH, oL = sb("oH", [128, C, S], F32R), sb("oL", [128, C, S], F32R)
        mx = sb("mx", [S, H])
        amb = sb("amb", [S, 2, 1])
        nmx = sb("nmx", [S, 2, 8])
        nmb = sb("nmb", [S, 2, 2, 8], BF16)
        nmT = sb("nmT", [16, H, S], BF16)
        P = sb("P", [KS, 2, NK, 8, S])
        avT = sb("avT", [128, 4, S])
        rden = sb("rden", [S, H])
        on = sb("on", [S, D])
        oT = sb("oT", [128, C, S])
        mi = sb("mi", [S, 2, KEYS], I32) if in_mask else None
        miT = sb("miT", [KS, 2, NK, S], I32) if in_mask else None
        mb = sb("mb", [S, 2, KEYS]) if in_mask else None
        m2 = sb("m2", [KS, 2, NK, S], BF16) if in_mask else None
        anyB = sb("anyB", [128, 2, S]) if in_mask else None
        aoff = sb("aoff", [128, S], BF16) if in_mask else None
        block = stk.enter_context(nc.Block())

        cxT = sb("cxT", [128, 1, C, SCP]) if ctx_ln else None

        @block.sync
        def _(sp):
            def load(un, free):
                if cross and not ctx_ln:
                    if free:
                        sp.wait_ge(*sg.at("c_lo", free))
                    sp.dma_start(ctxT[:, un.par, :, 0:SC], t["ctxT"][un.n]).then_inc(sg[f"ctx_in{un.par}"], 16)
                if ctx_ln:
                    if free:
                        sp.wait_ge(*sg.at("cxn", free))
                    sp.dma_start(ctok[:, un.par, :, :], t["ctx"][un.n].rearrange("(k p) d -> p k d", p=KS))\
                      .then_inc(sg[f"tok_in{un.par}"], 16)
                if in_mask:
                    if free:
                        sp.wait_ge(*sg.at("m_two", free))
                        sp.wait_ge(*sg.at("m_bias", free))
                    sp.dma_start(mi[:, un.par, :], t["mask" + name][un.n]).then_inc(sg[f"mask_in{un.par}"], 16)
                    sp.dma_start(miT[:, un.par, :, :],
                                 t["maskT" + name][un.n].rearrange("(k p) q -> p k q", p=KS))\
                      .then_inc(sg[f"mask_in{un.par}"], 16)

            if a + 1 < len(ATTN):
                sp.dma_start(m["w"][:, (a + 1) % 2, :, :, :], t["attn_w"][a + 1]).then_inc(sg["w_next"], 16)
            if cross or in_mask:
                load(Unit(0, 0), None)
                load(Unit(0, 1), None)
                with sp.Fori(0, B // 2 - 1) as pair:
                    load(Unit(pair, 2), Unit(pair, 0))
                    load(Unit(pair, 3), Unit(pair, 1))

        @block.gpsimd
        def _(pool):
            if cross:
                src = (cxT if ctx_ln else ctxT)
                pool.memset(src[:, :, :, SC:SCP], 0.0).then_inc(sg["ctx_pad"], 1)
                pool.wait_ge(*sg.once("ctx_pad", 1))
            pool.memset(vA[:, :, :, :, HD + 1:32], 0.0).then_inc(sg["v_const"], 1)
            pool.memset(vA[:, :, :, :, HD:HD + 1], 1.0).then_inc(sg["v_const"], 1)

            def items(seq):
                for st, k, un in seq:
                    later = not (isinstance(un.pair, int) and un.pair * 2 + un.k == 0)
                    if st == "CS":
                        if ctx_ln:
                            wait_apart(pool, sg, sg.at("ct_sb", un))
                            src = cxT[:, 0, :, :]
                        else:
                            wait_apart(pool, sg, sg.loaded("ctx_in", un))
                            src = ctxT[:, un.par, :, :]
                        if later:
                            wait_apart(pool, sg, sg.at("v_psum", un.step(-1)))
                        pool.tensor_copy(cH[:, :, :], src).then_inc(sg["c_hi"], 1)
                        pool.wait_ge(*sg.at("c_hi", un))
                        pool.tensor_tensor(cL[:, :, :], src, cH[:, :, :].bitcast(F32), ALU.subtract)\
                            .then_inc(sg["c_lo"], 1)
                    elif st == "Q":
                        for half, mask_of, ready, done in ((qH, qmH, "q_hi", "qm_hi"), (qL, qmL, "q_lo", "qm_lo")):
                            pool.wait_ge(*sg.at(ready, un))
                            if later and half is qH and not (isinstance(un.pair, int) and un.pair * 2 + un.k == 1):
                                pool.wait_ge(*sg.at("t_psum", un.step(-2)))
                            pool.tensor_tensor(mask_of[:, un.par, :, :, :],
                                               half[:, :, :].bitcast(F32).unsqueeze(2).broadcast_to([128, C, 8, S]),
                                               m["hmask"][:, :].unsqueeze(1).unsqueeze(3)
                                               .broadcast_to([128, C, 8, S]), ALU.mult).then_inc(sg[done], 1)
                    elif st == "STAT":
                        if bias:
                            pool.wait_ge(*sg.at("xn", un))
                            pool.tensor_tensor(x[:, un.n, :], x[:, un.n, :], row("bo", S), ALU.add)\
                                .then_inc(sg["xbias"], 1)
                        if in_mask:
                            wait_apart(pool, sg, sg.loaded("mask_in", un))
                            if not (isinstance(un.pair, int) and un.pair * 2 + un.k <= 1):
                                wait_apart(pool, sg, sg.at("s_max", un.step(-2)))
                            pool.tensor_scalar(mb[:, un.par, :], mi[:, un.par, :], 0.0, NEG, ALU.is_equal,
                                               ALU.mult).then_inc(sg["m_bias"], 1)
            items(opening(Unit(0, 0)))
            units(pool, B, lambda un, prev, nxt: items(walk(un, prev, nxt)))

        @block.scalar
        def _(act):
            def items(seq):
                for st, k, un in seq:
                    later = not (isinstance(un.pair, int) and un.pair * 2 + un.k == 0)
                    if st == "XT":
                        act.wait_ge(*sg.at("xt_psum", un))
                        if later:
                            act.wait_ge(*sg.at("q_psum", un.step(-1)))
                            act.wait_ge(*sg.at("xt_lo", un.step(-1)))
                            if not cross:
                                act.wait_ge(*sg.at("v_psum", un.step(-1)))
                        for dst in (xT, xH):
                            for c in range(C):
                                ins = act.activation(dst[:, c, :], PS[:, BANK["XT"], c * S:(c + 1) * S],
                                                     ACT.Identity, bias=0.0 if rms else col("b", c),
                                                     scale=col("g", c))
                        ins.then_inc(sg["xt_sb"], 1)
                    elif st == "C":
                        act.wait_ge(*sg.at("ct_psum", un, k + 1))
                        if later and k == 0:
                            act.wait_ge(*sg.at("c_lo", un.step(-1)))
                        for c in range(C):
                            ins = act.activation(cxT[:, 0, c, k * KS:(k + 1) * KS],
                                                 PS[:, BANK[f"C{k}"], c * KS:(c + 1) * KS], ACT.Identity,
                                                 bias=col("b", c), scale=col("g", c))
                        ins.then_inc(sg["ct_sb"], 1)
                    elif st == "K":
                        act.wait_ge(*sg.at("k_psum", un, k + 1))
                        if cross:
                            act.activation(kH[:, un.par, k, :], PS[:, BANK[f"K{k}"], 0:SCP], ACT.Identity,
                                           bias=col("bk", k) if bias else 0.0).then_inc(sg["k_sb"], 1)
                        else:
                            for c in range(C):
                                ins = act.activation(kH[:, un.par, c, :], PS[:, BANK["K0"], c * S:(c + 1) * S],
                                                     ACT.Identity, bias=col("bk", c) if bias else 0.0)
                            ins.then_inc(sg["k_sb"], 1)
                    elif st == "OT":
                        act.wait_ge(*sg.at("ot_psum", un))
                        if later:
                            act.wait_ge(*sg.at("o_psum", un.step(-1)))
                        for dst in (oT, oH):
                            ins = act.activation(dst[:, :, :], PS[:, BANK["OT"], 0:C * S]
                                                 .rearrange("p (c s) -> p c s", c=C), ACT.Identity)
                        ins.then_inc(sg["ot_sb"], 1)
                    elif st == "NM":
                        act.wait_ge(*sg.at("nm_psum", un, k + 1))
                        if later:
                            act.wait_ge(*sg.at("t_psum", un.step(-1), (k + 1) * NK))
                        src = PS[0:16, BANK[f"NM{k}"], 0:S // 2].bitcast(BF16)
                        for h in range(8):
                            ins = act.activation(nmT[:, 8 * k + h, :], src, ACT.Identity,
                                                 scale=m["nmask"][0:16, h:h + 1])
                        ins.then_inc(sg["nm_sb"], 1)
                    elif st == "T":
                        i, kt = k // NK, k % NK
                        act.wait_ge(*sg.at("t_psum", un, k + 1))
                        if later and kt == 0:
                            act.wait_ge(*sg.at("av_psum", un.step(-1), i + 1))
                        b = 2 * (k % 2)
                        act.activation(P[:, i, kt, :, :].rearrange("p (b j) s -> p b (j s)", b=2),
                                       PS[0:KS, b:b + 2, 0:4 * S], ACT.Exp)\
                            .then_inc(sg["p_exp"], 1)
                    elif st == "AV":
                        act.wait_ge(*sg.at("av_psum", un, k + 1))
                        if later:
                            act.wait_ge(*sg.at("t1_psum", un.step(-1)))
                        act.activation(avT[:, 2 * k:2 * k + 2, :],
                                       PS[:, BANK[f"AV{k}"], 0:2 * S].rearrange("p (g s) -> p g s", g=2),
                                       ACT.Identity).then_inc(sg["av_sb"], 1)

            reciprocal_root(None, act, sg, "rstd", None, root[:, :], None, vare[:, :])
            if ctx_ln:
                reciprocal_root(None, act, sg, "c_rstd", None, croot[:, :], None, cvare[:, :])
            items(opening(Unit(0, 0)))
            units(act, B, lambda un, prev, nxt: items(walk(un, prev, nxt)))
            items(closing(Unit(B // 2 - 1, 1)))

        @block.vector
        def _(dve):
            if a:
                dve.wait_ge(*sg.once("w_next", 0))
            w = m["w"][:, a % 2, :, :, :]
            for i in (K_, V_, Q_, O_):
                dve.tensor_copy(m["wh"][:, i, :, :], w[:, i, :, :]).then_inc(sg["w_hi"], 1)
            for n, i in enumerate((K_, V_, Q_, O_)):
                dve.wait_ge(*sg.once("w_hi", n + 1))
                dve.tensor_tensor(m["wl"][:, i, :, :], w[:, i, :, :], m["wh"][:, i, :, :].bitcast(F32),
                                  ALU.subtract).then_inc(sg["w_lo"], 1)
            if not in_mask:
                dve.memset(amb[:, :, :], 0.0).then_inc(sg["amb_zero"], 1)

            def items(seq):
                for st, k, un in seq:
                    later = not (isinstance(un.pair, int) and un.pair * 2 + un.k == 0)
                    if st == "STAT":
                        if not later:
                            dve.wait_ge(*sg.once("rstd", 6))
                        else:
                            dve.wait_ge(*sg.at("xt_psum", un.step(-1)))
                        if rms:
                            dve.tensor_scalar(xn[:, :], x[:, un.n, :], m["rs"][:, bass.ds(un.n, 1)], None, ALU.mult)\
                               .then_inc(sg["xn"], 1)
                        else:
                            dve.tensor_scalar(xn[:, :], x[:, un.n, :], m["mv"][:, un.n, 0:1],
                                              m["rs"][:, bass.ds(un.n, 1)], ALU.subtract, ALU.mult)\
                               .then_inc(sg["xn"], 1)
                    elif st == "M2":
                        dve.wait_ge(*sg.loaded("mask_in", un))
                        if later and not (isinstance(un.pair, int) and un.pair * 2 + un.k == 1):
                            dve.wait_ge(*sg.at("p_masked", un.step(-2)))
                        dve.tensor_scalar(m2[:, un.par, :, :], miT[:, un.par, :, :], 0.0, KEEP,
                                          ALU.not_equal, ALU.mult).then_inc(sg["m_two"], 1)
                    elif st == "C":
                        if k == 0:
                            dve.wait_ge(*sg.loaded("tok_in", un))
                            if not later:
                                dve.wait_ge(*sg.once("c_rstd", 6))
                        if later:
                            dve.wait_ge(*sg.at("ct_psum", un.step(-1), k + 1))
                        dve.tensor_scalar(cxn[:, k, :], ctok[:, un.par, k, :], m["cmv"][:, un.n * NK + k, 0:1],
                                          m["crs"][:, bass.ds(un.n * NK + k, 1)], ALU.subtract, ALU.mult)\
                           .then_inc(sg["cxn"], 1)
                    elif st == "ANY":
                        dve.wait_ge(*sg.at("any_psum", un))
                        dve.tensor_scalar(anyB[:, un.par, :], PS[:, BANK["ANY"], 0:S], 1.0, None, ALU.min)\
                           .then_inc(sg["any_sb"], 1)
                        dve.wait_ge(*sg.at("any_sb", un))
                        dve.tensor_scalar(aoff[:, :], anyB[:, un.par, :], -KEEP, KEEP, ALU.mult, ALU.add)\
                           .then_inc(sg["any_off"], 1)
                        dve.wait_ge(*sg.at("any_off", un))
                        dve.tensor_tensor(m2[:, un.par, :, :], m2[:, un.par, :, :],
                                          aoff[0:KS, :].unsqueeze(1).broadcast_to([KS, NK, S]), ALU.max)\
                           .then_inc(sg["m_ready"], 1)
                        dve.wait_ge(*sg.at("m_bias", un))
                        dve.tensor_reduce(amb[:, un.par, :], mb[:, un.par, :], axis=AX.X, op=ALU.max)\
                           .then_inc(sg["m_max"], 1)
                    elif st == "S":
                        h = k
                        wait = (lambda sig: wait_apart(dve, sg, sig)) if masked else (lambda sig: dve.wait_ge(*sig))
                        wait(sg.at("s_psum", un, k + 1))
                        if k % 8 == 0 and later:
                            wait(sg.at("neg_max", un.step(-1), k // 8 + 1))
                        sc = PS[0:S, 4 + k % 2, 0:KEYS]
                        if masked:
                            mask = mb[:, un.par, :] if in_mask else m["causal"][:, :]
                            if k == 0 and in_mask:
                                wait(sg.at("m_bias", un))
                            dve.tensor_tensor_reduce(out=junk[:, k % 2, 0:KEYS], in0=sc, in1=mask, scale=1.0, scalar=-3e38,
                                                     op0=ALU.add, op1=ALU.max, accum_out=mx[:, h:h + 1])\
                               .then_inc(sg["s_max"], 1)
                        else:
                            dve.reduce_max(mx[:, h:h + 1], sc, AX.X).then_inc(sg["s_max"], 1)
                    elif st == "NMD":
                        dve.wait_ge(*sg.at("s_max", un, 8 * k + 8))
                        if not in_mask and not later and k == 0:
                            dve.wait_ge(*sg.once("amb_zero", 1))
                        if in_mask and k == 0:
                            dve.wait_ge(*sg.at("m_max", un))
                        dve.tensor_scalar(nmx[:, k, :], mx[:, 8 * k:8 * k + 8], amb[:, un.par, :], -1.0,
                                          ALU.subtract, ALU.mult).then_inc(sg["neg_max"], 1)
                        dve.wait_ge(*sg.at("neg_max", un, k + 1))
                        if later:
                            dve.wait_ge(*sg.at("nm_psum", un.step(-1), k + 1))
                        dve.tensor_copy(nmb[:, k, 0, :], nmx[:, k, :]).then_inc(sg["neg_hi"], 1)
                        dve.wait_ge(*sg.at("neg_hi", un, k + 1))
                        dve.tensor_tensor(nmb[:, k, 1, :], nmx[:, k, :], nmb[:, k, 0, :], ALU.subtract)\
                           .then_inc(sg["neg_lo"], 1)
                    elif st == "T" and masked:
                        i, kt = k // NK, k % NK
                        dve.wait_ge(*sg.at("p_exp", un, k + 1))
                        if in_mask and k == 0:
                            dve.wait_ge(*sg.at("m_ready", un))
                        mT = m2[:, un.par, kt, :] if in_mask else m["causalT"][:, 0, :]
                        dve.tensor_tensor(P[:, i, kt, :, :], P[:, i, kt, :, :],
                                          mT.unsqueeze(1).broadcast_to([KS, 8, S]), ALU.min)\
                           .then_inc(sg["p_masked"], 1)
                    elif st == "Q":
                        dve.wait_ge(*sg.at("q_psum", un))
                        if in_mask:
                            dve.wait_ge(*sg.at("any_sb", un))
                        if later:
                            dve.wait_ge(*sg.at("qm_lo", un.step(-1)))
                        for c in range(C):
                            src = PS[:, BANK["Q"], c * S:(c + 1) * S]
                            if in_mask:
                                ins = dve.scalar_tensor_tensor(qf[:, c, :], src, QK_SCALE, anyB[:, un.par, :],
                                                               ALU.mult, ALU.mult)
                            elif bias:
                                ins = dve.tensor_scalar(qf[:, c, :], src, col("bq", c), QK_SCALE, ALU.add, ALU.mult)
                            else:
                                ins = dve.tensor_scalar(qf[:, c, :], src, QK_SCALE, None, ALU.mult)
                        ins.then_inc(sg["q_sum"], 1)
                        dve.wait_ge(*sg.at("q_sum", un))
                        dve.tensor_copy(qH[:, :, :], qf[:, :, :]).then_inc(sg["q_hi"], 1)
                        dve.wait_ge(*sg.at("q_hi", un))
                        dve.tensor_tensor(qL[:, :, :], qf[:, :, :], qH[:, :, :].bitcast(F32), ALU.subtract)\
                           .then_inc(sg["q_lo"], 1)
                    elif st == "XT":
                        dve.wait_ge(*sg.at("xt_sb", un))
                        if later:
                            dve.wait_ge(*sg.at("q_psum", un.step(-1)))
                            if not cross:
                                dve.wait_ge(*sg.at("v_psum", un.step(-1)))
                        dve.tensor_tensor(xL[:, :, :], xT[:, :, :], xH[:, :, :].bitcast(F32), ALU.subtract)\
                           .then_inc(sg["xt_lo"], 1)
                    elif st == "OT":
                        dve.wait_ge(*sg.at("ot_sb", un))
                        if later:
                            dve.wait_ge(*sg.at("o_psum", un.step(-1)))
                        dve.tensor_tensor(oL[:, :, :], oT[:, :, :], oH[:, :, :].bitcast(F32), ALU.subtract)\
                           .then_inc(sg["ot_lo"], 1)
                    elif st == "K":
                        dve.wait_ge(*sg.at("k_sb", un, k + 1))
                        n, w = (1, SCP) if cross else (C, S)
                        for c in range(n):
                            at = k + c
                            src = PS[:, BANK[f"K{k}"], c * S:c * S + w]
                            ins = dve.scalar_tensor_tensor(kL[:, un.par, at, :], src, col("bk", at),
                                                           kH[:, un.par, at, :].bitcast(F32), ALU.add, ALU.subtract)
                        ins.then_inc(sg["k_lo"], 1)
                    elif st == "V":
                        dve.wait_ge(*sg.at("v_psum", un, k + 1))
                        dst = vA[:, un.par, k, :, 0:HD]
                        src = PS[0:KS, BANK[f"V{k}"], 0:D].rearrange("p (h d) -> p h d", h=H)
                        if bias:
                            dve.tensor_tensor(dst, src, row("bv", KS).rearrange("p (h d) -> p h d", h=H), ALU.add)\
                               .then_inc(sg["v_sb"], 1)
                        else:
                            dve.tensor_copy(dst, src).then_inc(sg["v_sb"], 1)
                    elif st == "T1":
                        dve.wait_ge(*sg.at("t1_psum", un))
                        dve.reciprocal(rden[:, :], PS[0:S, BANK["T1"], :]
                                       .rearrange("p (h c) -> p h c", h=H)[:, :, HD])\
                           .then_inc(sg["rden"], 1)
                        dve.wait_ge(*sg.at("rden", un))
                        if later:
                            dve.wait_ge(*sg.at("ot_psum", un.step(-1)))
                        dve.tensor_tensor(on[:, :].rearrange("p (h d) -> p h d", h=H),
                                          PS[0:S, BANK["T1"], :].rearrange("p (h c) -> p h c", h=H)[:, :, 0:HD],
                                          rden[:, :].unsqueeze(2).broadcast_to([S, H, HD]), ALU.mult)\
                           .then_inc(sg["o_norm"], 1)
                    elif st == "O":
                        dve.wait_ge(*sg.at("o_psum", un))
                        if bias:
                            dve.wait_ge(*sg.at("xbias", un))
                        dve.tensor_tensor(x[:, un.n, :], PS[0:S, BANK["O"], 0:D], x[:, un.n, :], ALU.add)\
                           .then_inc(sg["x_new"], 1)
                        if following:
                            wait_apart(dve, sg, sg.at("x_new", un))
                            if later:
                                wait_apart(dve, sg, sg.at("x_kept", un.step(-1)))
                            token_stats(dve, sg, m, un.n, un, 1)

            if rms:
                mean_square(dve, sg, m, sq[:, :])
            reciprocal_root(dve, None, sg, "rstd", sq[:, :] if rms else m["mv"][:, :, 1], root[:, :], m["rs"][:, :], vare[:, :])
            if ctx_ln:
                reciprocal_root(dve, None, sg, "c_rstd", m["cmv"][:, :, 1], croot[:, :], m["crs"][:, :], cvare[:, :])
            items(opening(Unit(0, 0)))
            units(dve, B, lambda un, prev, nxt: items(walk(un, prev, nxt)))
            items(closing(Unit(B // 2 - 1, 1)))

        @block.tensor
        def _(pe):
            user = {6: None, 7: None}

            def take(st, un):
                b = BANK[st]
                if user[b]:
                    was, w = user[b]
                    sem, k = READ_BY[was]
                    pe.wait_ge(*sg.at(sem, w, k))
                user[b] = (st, un)

            def items(seq):
                for st, k, un in seq:
                    if st == "XT":
                        pe.wait_ge(*sg.at("xn", un))
                        take("XT", un)
                        for c in range(C):
                            ins = pe.transpose(PS[:, BANK["XT"], c * S:(c + 1) * S], xn[:, c * 128:(c + 1) * 128],
                                               ident[0:S, 0:S])
                        ins.then_inc(sg["xt_psum"], 1)
                    elif st == "C":
                        pe.wait_ge(*sg.at("cxn", un, k + 1))
                        take(f"C{k}", un)
                        for c in range(C):
                            ins = pe.transpose(PS[:, BANK[f"C{k}"], c * KS:(c + 1) * KS],
                                               cxn[:, k, c * 128:(c + 1) * 128], ident[0:KS, 0:KS])
                        ins.then_inc(sg["ct_psum"], 1)
                    elif st == "ANY":
                        pe.wait_ge(*sg.at("m_two", un))
                        take("ANY", un)
                        for kt in range(NK):
                            ins = pe.matmul(PS[:, BANK["ANY"], 0:S], m["onesb"][0:KS, :], m2[:, un.par, kt, :],
                                            start=kt == 0, stop=kt == NK - 1)
                        ins.then_inc(sg["any_psum"], 1)
                    elif st == "K":
                        if cross:
                            if k == 0:
                                pe.wait_ge(*sg.at("c_lo", un))
                            take(f"K{k}", un)
                            for c in range(C):
                                ins = split_product(pe, PS[:, BANK[f"K{k}"], 0:SCP],
                                                    W(K_, c, slice(k * 128, (k + 1) * 128)),
                                                    (cH[:, c, :], cL[:, c, :]), c == 0, c == C - 1)
                        else:
                            pe.wait_ge(*sg.at("xt_lo", un))
                            take("K0", un)
                            for mo in range(C):
                                for c in range(C):
                                    ins = split_product(pe, PS[:, BANK["K0"], mo * S:(mo + 1) * S],
                                                        W(K_, c, slice(mo * 128, (mo + 1) * 128)),
                                                        (xH[:, c, :], xL[:, c, :]), c == 0, c == C - 1)
                        ins.then_inc(sg["k_psum"], 1)
                    elif st == "V":
                        take(f"V{k}", un)
                        hi, lo = (cH, cL) if cross else (xH, xL)
                        for c in range(C):
                            ks = slice(k * KS, (k + 1) * KS)
                            ins = split_product(pe, PS[0:KS, BANK[f"V{k}"], 0:D], (hi[:, c, ks], lo[:, c, ks]),
                                                W(V_, c), c == 0, c == C - 1)
                        ins.then_inc(sg["v_psum"], 1)
                    elif st == "Q":
                        pe.wait_ge(*sg.at("xt_lo", un))
                        take("Q", un)
                        for mo in range(C):
                            for c in range(C):
                                ins = split_product(pe, PS[:, BANK["Q"], mo * S:(mo + 1) * S],
                                                    W(Q_, c, slice(mo * 128, (mo + 1) * 128)),
                                                    (xH[:, c, :], xL[:, c, :]), c == 0, c == C - 1)
                        ins.then_inc(sg["q_psum"], 1)
                    elif st == "S":
                        i = k // 8
                        later = not (isinstance(un.pair, int) and un.pair * 2 + un.k == 0)
                        if k == 0:
                            pe.wait_ge(*sg.at("qm_hi", un))
                            pe.wait_ge(*sg.at("k_sb", un))
                        if k >= 2:
                            pe.wait_ge(*sg.at("s_max", un, k - 1))
                        elif later:
                            pe.wait_ge(*sg.at("s_max", un.step(-1), 15 + k))
                        pe.matmul(PS[0:S, 4 + k % 2, 0:KP], qmH[:, un.par, i, k % 8, :], kH[:, un.par, i, :],
                                  start=True, stop=True).then_inc(sg["s_psum"], 1)
                    elif st == "NM":
                        pe.wait_ge(*sg.at("neg_lo", un, k + 1))
                        take(f"NM{k}", un)
                        pe.transpose(PS[0:16, BANK[f"NM{k}"], 0:S // 2].bitcast(BF16),
                                     nmb[:, k, :, :].rearrange("p a b -> p (a b)"), identb[0:S, 0:S])\
                          .then_inc(sg["nm_psum"], 1)
                    elif st == "T":
                        i, kt = k // NK, k % NK
                        later = not (isinstance(un.pair, int) and un.pair * 2 + un.k == 0)
                        if kt == 0:
                            pe.wait_ge(*sg.at("nm_sb", un, i + 1))
                        if k == 0:
                            pe.wait_ge(*sg.at("qm_lo", un))
                            pe.wait_ge(*sg.at("k_lo", un))
                        if k >= 2:
                            pe.wait_ge(*sg.at("p_exp", un, k - 1))
                        elif later:
                            pe.wait_ge(*sg.at("p_exp", un.step(-1), NT - 1 + k))
                        ks = slice(kt * KS, (kt + 1) * KS)
                        for e in range(2):
                            o = PS[0:KS, 2 * (k % 2) + e, 0:4 * S]
                            split_product(pe, o, (kH[:, un.par, i, ks], kL[:, un.par, i, ks]),
                                          (qmH[:, un.par, i, 4 * e:4 * e + 4, :], qmL[:, un.par, i, 4 * e:4 * e + 4, :]),
                                          True, False)
                            ins = pe.matmul(o, m["onesb"][0:16, 0:KS],
                                            nmT[:, 8 * i + 4 * e:8 * i + 4 * e + 4, :], start=False, stop=True)
                        ins.then_inc(sg["t_psum"], 1)
                    elif st == "AV":
                        i = k
                        pe.wait_ge(*sg.at("p_masked" if masked else "p_exp", un, (i + 1) * NK))
                        if i == 0:
                            if not (isinstance(un.pair, int) and un.pair * 2 + un.k > 0):
                                pe.wait_ge(*sg.once("v_const", 2))
                            pe.wait_ge(*sg.at("v_sb", un))
                        take(f"AV{i}", un)
                        for e in range(2):
                            for kt in range(NK):
                                for j in range(4):
                                    ins = pe.matmul(PS[32 * j:32 * j + 32, BANK[f"AV{i}"], e * S:(e + 1) * S],
                                                    vA[:, un.par, kt, 8 * i + 4 * e + j, :], P[:, i, kt, 4 * e + j, :],
                                                    start=kt == 0, stop=kt == NK - 1)
                        ins.then_inc(sg["av_psum"], 1)
                    elif st == "T1":
                        pe.wait_ge(*sg.at("av_sb", un))
                        take("T1", un)
                        for g in range(4):
                            ins = pe.transpose(PS[0:S, BANK["T1"], g * 128:(g + 1) * 128], avT[:, g, :], ident[:, :])
                        ins.then_inc(sg["t1_psum"], 1)
                    elif st == "OT":
                        pe.wait_ge(*sg.at("o_norm", un))
                        take("OT", un)
                        for c in range(C):
                            ins = pe.transpose(PS[:, BANK["OT"], c * S:(c + 1) * S], on[:, c * 128:(c + 1) * 128],
                                               ident[0:S, 0:S])
                        ins.then_inc(sg["ot_psum"], 1)
                    elif st == "O":
                        pe.wait_ge(*sg.at("ot_lo", un))
                        take("O", un)
                        for c in range(C):
                            ins = split_product(pe, PS[0:S, BANK["O"], 0:D], (oH[:, c, :], oL[:, c, :]), W(O_, c),
                                                c == 0, c == C - 1)
                        ins.then_inc(sg["o_psum"], 1)

            def body(un, prev, nxt):
                if prev:
                    for b, (st, w) in list(user.items()):
                        user[b] = (st, un.step(w.k - body.at - 1))
                items(walk(un, prev, nxt))
                body.at = un.k

            pe.wait_ge(*sg.once("w_lo", 4))
            items(opening(Unit(0, 0)))
            body.at = 0
            units(pe, B, body)
            items(closing(Unit(B // 2 - 1, 1)))
    sg.end(B, w_hi=4, w_lo=4, w_next=16 if a + 1 < len(ATTN) else 0, ctx_pad=1 if cross else 0, v_const=2, **(dict(msq=2) if rms else {}), **({} if in_mask else dict(amb_zero=1)), rstd=6, rstd_root=1, **(dict(c_rstd=6, c_rstd_root=1) if ctx_ln else {}))


def ffn(nc, t, m, sg, name, following):
    moe = name == "MOE"
    npass = 1 + E if moe else 1
    w0 = {"MOE": 0, "F2": 1 + E, "F3": 2 + E}[name]
    PS, x, ident = m["psum"], m["x"], m["ident"]
    act_fn = ACT.Silu if moe else ACT.Gelu

    def col(p, c):
        at = COLS[name + p] + c
        return m["col"][:, at:at + 1]

    steps = npass * NTILES
    sg.phase(c_in0=32, c_in1=32, c_stats=3 * TB, c_moments=TB, x_stats=TB, x_moments=TB, x_kept=TB, c_kept=TB, f_xn=TB, f_xbias=TB, f_xt_psum=TB, f_xt_sb=TB, f_copied=1,
             lg_psum=TB, top=TB, topi=TB, topf=TB, gdiff=1, gexp=1, gden=1, grec=1, gsec=1, lg_sb=1, gtwo=TB, gates_in=1,
             gates_set=TB)
    per_tile = dict(sg.per)
    sg.phase(h_psum=HC, h_sb=HC, y_psum=TB, y_acc=TB)
    per_step = dict(sg.per)
    sg.phase(w_in0=0, w_in1=0)
    sg.per = {**per_tile, **per_step}
    win = [sg.left["w_in0"], sg.left["w_in1"]]
    with ExitStack() as stk:
        def sb(nm, shape, dt=F32):
            return stk.enter_context(nc.sbuf_tensor(name + nm, shape, dt))
        NB = 2 if moe else 1
        w1 = [sb(f"w1{i}", [128, C, HID]) for i in range(NB)]
        w2 = [sb(f"w2{i}", [128, HC, D]) for i in range(NB)]
        xn = sb("xn", [S, 2, D])
        root, vare, sq = sb("root", [S, B]), sb("vare", [S, B]), sb("sq", [S, B])
        hnS = sb("hnS", [128, 2, C, TOK])
        hT = sb("hT", [128, HC, TOK])
        if moe:
            hn = sb("hn", [128, NTILES, C, TOK])
            gw = sb("gw", [128, C, E])
            gates = sb("gates", [S, B, E])
            top, topi, topf = sb("top", [S, TB, 8]), sb("topi", [S, TB, 8], U32), sb("topf", [S, TB, 2])
            gd, ge, gn, g1, g2 = (sb(f"g{k}", [S, TB]) for k in range(5))
            one, two = sb("one", [S, TB, E]), sb("two", [S, TB, E])
            lgs = sb("lgs", [S, TB, E])
            ctok, cst = sb("ctok", [KT_CTX, 2, 3, D]), sb("cst", [KT_CTX, 2, 3, 6])
            cmvs = sb("cmvs", [KT_CTX, 2, 3, 2])
        block = stk.enter_context(nc.Block())

        def nth(un):
            return un.n

        @block.sync
        def _(sp):
            if moe:
                sp.dma_start(gw[:, :, :], t["gate_w"]).then_inc(sg["gates_in"], 16)
            for p in range(npass):
                if p == 2:
                    for r in range(2):
                        sp.dma_start(ctok[:, r, :, :], t["ctx"][r].rearrange("(k p) d -> p k d", p=KT_CTX))\
                          .then_inc(sg[f"c_in{r}"], 16)
                    with sp.Fori(0, B // 2 - 1) as pair:
                        for r in range(2):
                            sp.wait_ge(sg["c_moments"], pair * 2 + (sg.left["c_moments"] + 1 + r))
                            sp.dma_start(ctok[:, r, :, :],
                                         t["ctx"][pair * 2 + (2 + r)].rearrange("(k p) d -> p k d", p=KT_CTX))\
                              .then_inc(sg[f"c_in{r}"], 16)
                if p >= 2:
                    sp.wait_ge(*sg.at("y_psum", (p - 2) * NTILES + NTILES - 1))
                sp.dma_start(w1[p % 2][:, :, :], t["ffn_w1"][w0 + p]).then_inc(sg[f"w_in{p % 2}"], 16)
                sp.dma_start(w2[p % 2][:, :, :], t["ffn_w2"][w0 + p]).then_inc(sg[f"w_in{p % 2}"], 16)

        def first_pass(eng, norm, main):
            norm(Unit(0, 0))

            def body(un, prev, nxt):
                main(un)
                if nxt:
                    norm(nxt)
            units(eng, NTILES, body)

        def other_passes(eng, main):
            if not moe:
                return
            def turn(pair):
                for k in (1, 2):
                    with eng.Fori(0, NTILES) as tile:
                        main(pair, k, tile)
            with eng.Fori(0, E // 2 - 1) as pair:
                turn(pair)
            turn(E // 2 - 1)

        def is_first(un):
            return isinstance(un.pair, int) and un.pair * 2 + un.k == 0

        @block.gpsimd
        def _(pool):
            def norm(un):
                if not moe:
                    for r in range(TB):
                        b = un.n * TB + r
                        pool.wait_ge(*sg.at("f_xn", un, r + 1))
                        pool.tensor_tensor(x[:, b, :], x[:, b, :], m["row"][0:S, ROWS[name + "b2"], :], ALU.add)\
                            .then_inc(sg["f_xbias"], 1)
                if moe:
                    pool.wait_ge(*sg.at("f_xt_sb", un))
                    pool.tensor_copy(hn[:, un.n, :, :], hnS[:, un.par, :, :]).then_inc(sg["f_copied"], 1)
            first_pass(pool, norm, lambda un: None)

        @block.scalar
        def _(act):
            def norm(un):
                for r in range(TB):
                    act.wait_ge(*sg.at("f_xt_psum", un, r + 1))
                    if r == 0 and not is_first(un):
                        if not is_first(un.step(-1)):
                            act.wait_ge(*sg.at("y_psum", un.step(-2)))
                            if moe:
                                act.wait_ge(*sg.at("f_copied", un.step(-2)))
                    for c in range(C):
                        ins = act.activation(hnS[:, un.par, c, r * S:(r + 1) * S], PS[:, 6, c * S:(c + 1) * S],
                                             ACT.Identity, bias=0.0 if moe else col("b", c), scale=col("g", c))
                    ins.then_inc(sg["f_xt_sb"], 1)
                if moe:
                    act.wait_ge(*sg.at("gdiff", un))
                    act.activation(ge[:, :], gd[:, :], ACT.Exp).then_inc(sg["gexp"], 1)

            def hidden(step):
                for hc in range(HC):
                    act.wait_ge(*sg.at("h_psum", step, hc + 1))
                    act.activation(hT[:, hc, :], PS[:, hc % 4, 0:TOK], act_fn,
                                   bias=0.0 if moe else m["fb1"][:, w0 - 1 - E, hc:hc + 1]).then_inc(sg["h_sb"], 1)
            reciprocal_root(None, act, sg, "rstd", None, root[:, :], None, vare[:, :])
            first_pass(act, norm, lambda un: hidden(un))
            other_passes(act, lambda pair, k, tile: hidden(pair * (2 * NTILES) + tile + k * NTILES))

        @block.vector
        def _(dve):
            def norm(un):
                for r in range(TB):
                    if is_first(un) and r == 0:
                        dve.wait_ge(*sg.once("rstd", 6))
                    if r >= 2:
                        dve.wait_ge(*sg.at("f_xt_psum", un, r - 1))
                    elif not is_first(un):
                        dve.wait_ge(*sg.at("f_xt_psum", un.step(-1), TB + r - 1))
                    b = un.n * TB + r
                    if moe:
                        dve.tensor_scalar(xn[:, r % 2, :], x[:, b, :], m["rs"][:, bass.ds(b, 1)], None, ALU.mult)\
                           .then_inc(sg["f_xn"], 1)
                    else:
                        dve.tensor_scalar(xn[:, r % 2, :], x[:, b, :], m["mv"][:, b, 0:1],
                                          m["rs"][:, bass.ds(b, 1)], ALU.subtract, ALU.mult)\
                           .then_inc(sg["f_xn"], 1)
                if not moe:
                    return
                for r in range(TB):
                    n = un.n * (TB * 3) + r * 3
                    sem = sg.sems[f"c_in{r % 2}"]
                    wait_apart(dve, sg, (sem, un.n * 32 + (sg.left[f"c_in{r % 2}"] + 16 * (r // 2 + 1))))
                    if r >= 2:
                        wait_apart(dve, sg, sg.at("c_kept", un, r - 1))
                    elif not is_first(un):
                        wait_apart(dve, sg, sg.at("c_kept", un.step(-1), TB + r - 1))
                    for kt in range(3):
                        dve.bn_stats(cst[:, r % 2, kt, :], ctok[:, r % 2, kt, :]).then_inc(sg["c_stats"], 1)
                    for kt in range(3):
                        wait_apart(dve, sg, sg.at("c_stats", un, 3 * r + kt + 1))
                        ins = dve.bn_aggr(cmvs[:, r % 2, kt, :], cst[:, r % 2, kt, :])
                    ins.then_inc(sg["c_moments"], 1)
                    wait_apart(dve, sg, sg.at("c_moments", un, r + 1))
                    dve.tensor_copy(m["cmv"][:, bass.ds(n, 3), :], cmvs[:, r % 2, :, :]).then_inc(sg["c_kept"], 1)
                dve.wait_ge(*sg.at("lg_psum", un))
                dve.tensor_copy(lgs[:, :, :].rearrange("p r e -> p (r e)"), PS[0:S, 7, 0:TB * E])\
                   .then_inc(sg["lg_sb"], 1)
                wait_apart(dve, sg, sg.at("lg_sb", un))
                for r in range(TB):
                    dve.max(top[:, r, :], lgs[:, r, :]).then_inc(sg["top"], 1)
                for r in range(TB):
                    wait_apart(dve, sg, sg.at("top", un, r + 1))
                    dve.max_index(topi[:, r, :], top[:, r, :], lgs[:, r, :]).then_inc(sg["topi"], 1)
                dve.tensor_tensor(gd[:, :], top[:, :, 1], top[:, :, 0], ALU.subtract).then_inc(sg["gdiff"], 1)
                for r in range(TB):
                    dve.wait_ge(*sg.at("topi", un, r + 1))
                    dve.tensor_copy(topf[:, r, :], topi[:, r, 0:2]).then_inc(sg["topf"], 1)
                dve.wait_ge(*sg.at("gexp", un))
                dve.tensor_scalar(gn[:, :], ge[:, :], 1.0, None, ALU.add).then_inc(sg["gden"], 1)
                dve.wait_ge(*sg.at("gden", un))
                dve.reciprocal(g1[:, :], gn[:, :]).then_inc(sg["grec"], 1)
                dve.wait_ge(*sg.at("grec", un))
                dve.tensor_tensor(g2[:, :], ge[:, :], g1[:, :], ALU.mult).then_inc(sg["gsec"], 1)
                dve.wait_ge(*sg.at("gsec", un))
                dve.wait_ge(*sg.at("topf", un))
                for r in range(TB):
                    dve.tensor_scalar(one[:, r, :], m["iota"][0:S, :], topf[:, r, 0:1], g1[:, r:r + 1], ALU.is_equal,
                                      ALU.mult)
                    dve.tensor_scalar(two[:, r, :], m["iota"][0:S, :], topf[:, r, 1:2], g2[:, r:r + 1], ALU.is_equal,
                                      ALU.mult).then_inc(sg["gtwo"], 1)
                for r in range(TB):
                    dve.wait_ge(*sg.at("gtwo", un, r + 1))
                    dve.tensor_tensor(gates[:, un.n * TB + r, :], one[:, r, :], two[:, r, :], ALU.add)\
                       .then_inc(sg["gates_set"], 1)

            def stats_after(step, tile, r, b, very_first):
                wait_apart(dve, sg, sg.at("y_acc", step, r + 1))
                if not very_first:
                    wait_apart(dve, sg, sg.at("x_kept", tile, r))
                token_stats(dve, sg, m, b, tile, r + 1)

            def shared(un):
                for r in range(TB):
                    b = un.n * TB + r
                    dve.wait_ge(*sg.at("y_psum", un, r + 1))
                    if not moe:
                        dve.wait_ge(*sg.at("f_xbias", un, r + 1))
                    dve.tensor_tensor(x[:, b, :], PS[0:S, 4 + r % 2, 0:D], x[:, b, :], ALU.add)\
                       .then_inc(sg["y_acc"], 1)
                    if following and not moe:
                        stats_after(un, un, r, b, is_first(un) and r == 0)

            def routed(pair, k, tile):
                step = pair * (2 * NTILES) + tile + k * NTILES
                last = following and isinstance(pair, int) and k == 2
                for r in range(TB):
                    b = tile * TB + r
                    dve.wait_ge(*sg.at("y_psum", step, r + 1))
                    if r == 0:
                        dve.wait_ge(*sg.at("gates_set", NTILES - 1))
                    e = pair * 2 + (k - 1)
                    dve.wait_ge(*sg.at("y_acc", step, r - TB * NTILES))
                    dve.scalar_tensor_tensor(x[:, b, :], PS[0:S, 4 + r % 2, 0:D],
                                             gates[:, b, bass.ds(e, 1)], x[:, b, :],
                                             ALU.mult, ALU.add).then_inc(sg["y_acc"], 1)
                    if last:
                        stats_after(step, tile, r, b, False)
            if moe:
                mean_square(dve, sg, m, sq[:, :])
            reciprocal_root(dve, None, sg, "rstd", sq[:, :] if moe else m["mv"][:, :, 1], root[:, :], m["rs"][:, :], vare[:, :])
            first_pass(dve, norm, shared)
            other_passes(dve, routed)

        @block.tensor
        def _(pe):
            def norm(un):
                for r in range(TB):
                    pe.wait_ge(*sg.at("f_xn", un, r + 1))
                    if r >= 1:
                        pe.wait_ge(*sg.at("f_xt_sb", un, r))
                    elif not is_first(un):
                        pe.wait_ge(*sg.at("f_xt_sb", un.step(-1)))
                    for c in range(C):
                        ins = pe.transpose(PS[:, 6, c * S:(c + 1) * S], xn[:, r % 2, c * 128:(c + 1) * 128],
                                           ident[0:S, 0:S])
                    ins.then_inc(sg["f_xt_psum"], 1)
                if moe:
                    if is_first(un):
                        pe.wait_ge(sg["gates_in"], 16)
                    else:
                        pe.wait_ge(*sg.at("lg_sb", un.step(-1)))
                    for r in range(TB):
                        pe.wait_ge(*sg.at("f_xt_sb", un, r + 1))
                        for c in range(C):
                            ins = pe.matmul(PS[0:S, 7, r * E:(r + 1) * E], hnS[:, un.par, c, r * S:(r + 1) * S],
                                            gw[:, c, :], start=c == 0, stop=c == C - 1)
                        ins.then_inc(sg["lg_psum"], 1)

            def products(step, w, src, first):
                for hc in range(HC):
                    if hc >= 4:
                        pe.wait_ge(*sg.at("h_sb", step, hc - 3))
                    elif not first:
                        pe.wait_ge(*sg.at("h_sb", step, hc - 3))
                    for c in range(C):
                        ins = pe.matmul(PS[:, hc % 4, 0:TOK], w1[w][:, c, hc * 128:(hc + 1) * 128], src(c),
                                        start=c == 0, stop=c == C - 1)
                    ins.then_inc(sg["h_psum"], 1)
                for r in range(TB):
                    if r >= 2:
                        pe.wait_ge(*sg.at("y_acc", step, r - 1))
                    elif not first:
                        pe.wait_ge(*sg.at("y_acc", step, r - 1))
                    for hc in range(HC):
                        if r == 0:
                            pe.wait_ge(*sg.at("h_sb", step, hc + 1))
                        ins = pe.matmul(PS[0:S, 4 + r % 2, 0:D], hT[:, hc, r * S:(r + 1) * S], w2[w][:, hc, :],
                                        start=hc == 0, stop=hc == HC - 1)
                    ins.then_inc(sg["y_psum"], 1)

            def shared(un):
                if is_first(un):
                    pe.wait_ge(sg["w_in0"], win[0] + 32)
                pe.wait_ge(*sg.at("f_xt_sb", un))
                products(un, 0, lambda c: hnS[:, un.par, c, :], is_first(un))

            def routed(pair, k, tile):
                pe.wait_ge(sg[f"w_in{k % 2}"], pair * 32 + (win[k % 2] + (32 if k == 1 else 64)))
                pe.wait_ge(*sg.at("f_copied", NTILES - 1)) if moe else None
                products(pair * (2 * NTILES) + tile + k * NTILES, k % 2, lambda c: hn[:, tile, c, :], False)
            first_pass(pe, norm, shared)
            other_passes(pe, routed)
    for p in range(npass):
        sg.left[f"w_in{p % 2}"] += 32
    sg.per = per_tile
    if not moe:
        for s in ("c_in0", "c_in1", "c_stats", "c_moments", "c_kept", "f_copied", "lg_psum", "top", "topi", "topf", "gdiff", "gexp",
                  "gden", "grec", "gsec", "lg_sb", "gtwo", "gates_in", "gates_set"):
            sg.per.pop(s)
    else:
        sg.per.pop("f_xbias")
    if not following:
        for s in ("x_stats", "x_moments", "x_kept"):
            sg.per.pop(s)
    sg.end(NTILES, rstd=6, rstd_root=1, **(dict(msq=2) if moe else {}))
    sg.per = per_step
    sg.end(steps)


def build_inputs(inputs):
    g = {k: np.asarray(v) for k, v in inputs.items()}
    f = np.float32

    def chunks(w):
        return w.reshape(-1, 128, w.shape[-1]).transpose(1, 0, 2)

    def cols(v):
        return v.reshape(-1, 128).T

    wt = {"L0": [g[f"L0_xattn_W{p}"].T for p in "qkvo"],
          "L1S": [g[f"L1_xattn_sa_w{p}"].T for p in "qkvo"],
          "L1C": [g[f"L1_xattn_ca_w{p}"].T for p in "qkvo"],
          "L2": [g[f"L2_xattn_w{p}"] for p in "qkvo"],
          "L3S": [g["L3_xattn_attn_qkv_w"][i * D:(i + 1) * D].T for i in range(3)] + [g["L3_xattn_attn_proj_w"].T],
          "L3C": [g[f"L3_xattn_{p}_w"].T for p in ("q", "k", "v", "ca_proj")]}
    qkv_b = g["L3_xattn_attn_qkv_b"]
    zero, one = np.zeros(D, f), np.ones(D, f)
    vec = {"L0g": g["L0_xattn_ln_gamma"], "L0b": g["L0_xattn_ln_beta"], "L0bq": g["L0_xattn_bq"],
           "L0bk": g["L0_xattn_bk"], "L1Sg": g["L1_xattn_norm1_w"], "L1Cg": g["L1_xattn_norm2_w"],
           "MOEg": g["L1_xattn_norm3_w"],
           "L2g": g["L2_xattn_ln1_g"], "L2b": g["L2_xattn_ln1_b"], "L2bq": g["L2_xattn_bq"], "L2bk": g["L2_xattn_bk"],
           "F2g": g["L2_xattn_ln2_g"], "F2b": g["L2_xattn_ln2_b"],
           "L3Sg": g["L3_xattn_ln1_g"], "L3Sb": g["L3_xattn_ln1_b"], "L3Sbq": qkv_b[0:D], "L3Sbk": qkv_b[D:2 * D],
           "L3Cg": g["L3_xattn_ln2_g"], "L3Cb": g["L3_xattn_ln2_b"], "L3Cbq": g["L3_xattn_q_b"],
           "L3Cbk": g["L3_xattn_k_b"], "F3g": g["L3_xattn_ln3_g"], "F3b": g["L3_xattn_ln3_b"]}
    rows = {"L0bv": g["L0_xattn_bv"], "L0bo": g["L0_xattn_bo"], "L2bv": g["L2_xattn_bv"], "L2bo": g["L2_xattn_bo"],
            "L3Sbv": qkv_b[2 * D:], "L3Sbo": g["L3_xattn_attn_proj_b"], "L3Cbv": g["L3_xattn_v_b"],
            "L3Cbo": g["L3_xattn_ca_proj_b"], "F2b2": g["L2_xattn_b2"], "F3b2": g["L3_xattn_proj_b"]}
    w1 = [g["L1_xattn_sh_w1"].T] + [w.T for w in g["L1_xattn_exp_w1"]] + [g["L2_xattn_w1"], g["L3_xattn_fc_w"].T]
    w2 = [g["L1_xattn_sh_w2"].T] + [w.T for w in g["L1_xattn_exp_w2"]] + [g["L2_xattn_w2"], g["L3_xattn_proj_w"].T]
    p = np.arange(128)
    hmask = np.stack([(p // 16 == e) * 1.0 for e in range(8)], 1)
    nmask = np.stack([((p == e) | (p == 8 + e)) * 1.0 for e in range(8)], 1)
    tri = np.tril(np.ones((S, S)))
    a = {
        "x": g["x"],
        "ctx": g["ctx_1024"],
        "ctxT": g["ctx_1024"].transpose(0, 2, 1).reshape(B, C, 128, SC).transpose(0, 2, 1, 3),
        "maskL1S": g["mask_BxSxS_ik0"], "maskTL1S": g["mask_BxSxS_ik0"].transpose(0, 2, 1),
        "maskL1C": g["mask_BxSxS2_if1"], "maskTL1C": g["mask_BxSxS2_if1"].transpose(0, 2, 1),
        "attn_w": np.stack([np.stack([chunks(w) for w in wt[n]], 1) for n in ATTN_NAMES], 0),
        "col": np.concatenate([cols(vec.get(n, zero)) for n in COLS], 1),
        "fb1": np.stack([cols(g["L2_xattn_b1"]), cols(g["L3_xattn_fc_b"])], 1),
        "row": np.stack([rows.get(n, zero) for n in ROWS], 0),
        "ident": np.eye(128, dtype=f), "hmask": hmask.astype(f), "nmask": nmask.astype(f),
        "causal": ((1 - tri) * NEG).astype(f), "causalT": (tri.T * KEEP).astype(f),
        "gate_w": chunks(g["L1_xattn_gate_w"].T),
        "ffn_w1": np.stack([chunks(w) for w in w1], 0),
        "ffn_w2": np.stack([chunks(w) for w in w2], 0),
    }
    return {k: np.ascontiguousarray(v) for k, v in a.items()}


def kernel(**inputs):
    import concourse.bacc as bacc
    from concourse.bass_utils import run_bass_kernel_spmd

    nc = bacc.Bacc("TRN2", target_bir_lowering=False, num_devices=1)
    arrays = build_inputs(inputs)
    t = {k: nc.dram_tensor(k + "_dram", v.shape, mybir.dt.from_np(v.dtype), kind="ExternalInput").ap()
         for k, v in arrays.items()}
    out = nc.dram_tensor("out_dram", (B, S, D), F32, kind="ExternalOutput").ap()
    build(nc, t, out)
    r = run_bass_kernel_spmd(nc, [{k + "_dram": v for k, v in arrays.items()}], core_ids=[0])
    return r.results[0]["out_dram"]
```

```python
import numpy as np

import concourse.bass as bass
from concourse import mybir
from contextlib import ExitStack

F32 = mybir.dt.float32
F32R = mybir.dt.float32r
BF16 = mybir.dt.bfloat16
I32 = mybir.dt.int32
U32 = mybir.dt.uint32
ALU = mybir.AluOpType
ACT = mybir.ActivationFunctionType
AX = mybir.AxisListType

B, S, SC, D = 32, 112, 375, 256
H, HD = 16, 16
C = D // 128
HID, HC = 1024, 8
E = 8
EPS = 1e-5
NEG = -65504.0
KEEP = 2.0 ** 100
QK_SCALE = HD ** -0.5
KT_CTX = 125
TB = 4
NTILES = B // TB
TOK = TB * S
SCP = SC + 1

ATTN = {
    "L0": dict(cross=True, norm="ln", mask=None, ctx_ln=False),
    "L1S": dict(cross=False, norm="rms", mask="input", ctx_ln=False),
    "L1C": dict(cross=True, norm="rms", mask="input", ctx_ln=False),
    "L2": dict(cross=True, norm="ln", mask=None, ctx_ln=True),
    "L3S": dict(cross=False, norm="ln", mask="causal", ctx_ln=False),
    "L3C": dict(cross=True, norm="ln", mask=None, ctx_ln=False),
}
ORDER = ["L0", "L1S", "L1C", "MOE", "L2", "F2", "L3S", "L3C", "F3"]
ATTN_NAMES = list(ATTN)
COLS = {}
for _n in ATTN_NAMES:
    for _p in ("g", "b", "bq", "bk"):
        COLS[_n + _p] = (len(COLS)) * 2
for _n in ("MOE", "F2", "F3"):
    for _p in ("g", "b"):
        COLS[_n + _p] = (len(COLS)) * 2
NCOL = len(COLS) * 2
ROWS = {n: i for i, n in enumerate([a + p for a in ATTN_NAMES if a not in ("L1S", "L1C") for p in ("bv", "bo")] + ["F2b2", "F3b2"])}


class Unit:

    def __init__(self, pair, k):
        self.pair, self.k = pair, k
        self.par = k % 2
        self.n = pair * 2 + k
        self.half = pair + k // 2

    def step(self, d):
        return Unit(self.pair, self.k + d)


def units(eng, count, body):
    u = Unit(0, 0)
    body(u, None, u.step(1))
    with eng.Fori(0, count // 2 - 1) as pair:
        for k in (1, 2):
            u = Unit(pair, k)
            body(u, u.step(-1), u.step(1))
    u = Unit(count // 2 - 1, 1)
    body(u, u.step(-1), None)


class Signals:

    def __init__(self, nc, stack):
        self.nc, self.stack = nc, stack
        self.sems, self.left, self.per = {}, {}, {}

    def phase(self, **per):
        self.per = per
        for name in per:
            if name not in self.sems:
                self.sems[name] = self.stack.enter_context(self.nc.semaphore(name))
                self.left[name] = 0

    def end(self, count, **once):
        for name, per in self.per.items():
            self.left[name] += per * count
        for name, n in once.items():
            self.left[name] += n

    def once(self, name, k):
        if name not in self.sems:
            self.sems[name] = self.stack.enter_context(self.nc.semaphore(name))
            self.left[name] = 0
        return self.sems[name], self.left[name] + k

    def __getitem__(self, name):
        return self.sems[name]

    def at(self, name, unit, k=None):
        n = unit.n if isinstance(unit, Unit) else unit
        return self.sems[name], n * self.per[name] + (self.left[name] + (self.per[name] if k is None else k))

    def loaded(self, name, unit):
        name = f"{name}{unit.par}"
        return self.sems[name], unit.half * (2 * self.per[name]) + (self.left[name] + 2 * self.per[name])


def split_product(pe, out, lhsT, rhs, first, last):
    for n, (a, b) in enumerate(((0, 0), (0, 1), (1, 0))):
        ins = pe.matmul(out, lhsT[a], rhs[b], start=first and n == 0, stop=last and n == 2)
    return ins


def build(nc, t, out, order=tuple(ORDER)):
    stack = ExitStack()
    with stack:
        def sb(name, shape, dt=F32):
            return stack.enter_context(nc.sbuf_tensor(name, shape, dt))

        def pb(name, shape, dt=F32):
            return stack.enter_context(nc.psum_tensor(name, shape, dt))

        m = {}
        m["x"] = sb("x_all", [S, B, D])
        m["w"] = sb("attn_w", [128, 4, C, D])
        m["col"] = sb("col", [128, NCOL])
        m["fb1"] = sb("fb1", [128, 2, HC])
        m["row"] = sb("row", [128, len(ROWS), D])
        m["ident"] = sb("ident", [128, 128])
        m["nmask"] = sb("nmask", [128, 8])
        m["hmask"] = sb("hmask", [128, 8])
        m["causal"] = sb("causal", [S, S])
        m["causalT"] = sb("causalT", [S, 1, S])
        m["identb"] = sb("identb", [128, 128], BF16)
        m["onesb"] = sb("onesb", [128, 128], BF16)
        m["onesf"] = sb("onesf", [128, 128])
        m["iota"] = sb("iota", [128, E])
        m["mv"] = sb("mv", [S, B, 2])
        m["xst"] = sb("xst", [S, 6])
        m["xmv"] = sb("xmv", [S, 2])
        m["cmv"] = sb("cmv", [KT_CTX, B * 3, 2])
        m["rs"] = sb("rs", [S, B])
        m["crs"] = sb("crs", [KT_CTX, B * 3])
        m["psum"] = pb("psum", [128, 8, 512])
        sg = Signals(nc, stack)
        for name in ("w_next", "w_hi", "w_lo", "ctx_pad", "rstd", "rstd_root", "c_rstd", "c_rstd_root", "v_const", "amb_zero", "msq", "apart"):
            sg.once(name, 0)

        kinds = ["rms" if name in ("L1S", "L1C", "MOE") else "ln" for name in order] + [None]
        prepare(nc, t, m, sg, kinds[0])
        for name, following in zip(order, kinds[1:]):
            if name in ATTN:
                attention(nc, t, m, sg, name, following)
            else:
                ffn(nc, t, m, sg, name, following)
        sg.phase(x_out=16)
        with nc.Block() as block:
            @block.sync
            def _(sp):
                sp.dma_start(out.rearrange("b s d -> s b d"), m["x"][:, :, :]).then_inc(sg["x_out"], 16)
                sp.wait_ge(sg["x_out"], 16)


def wait_apart(eng, sg, signal):
    eng.wait_ge(*signal)
    eng.sem_inc(sg["apart"], 1)


def token_stats(dve, sg, m, n, unit, k):
    dve.bn_stats(m["xst"][:, :], m["x"][:, n, :]).then_inc(sg["x_stats"], 1)
    wait_apart(dve, sg, sg.at("x_stats", unit, k))
    dve.bn_aggr(m["xmv"][:, :], m["xst"][:, :]).then_inc(sg["x_moments"], 1)
    wait_apart(dve, sg, sg.at("x_moments", unit, k))
    dve.tensor_copy(m["mv"][:, n, :], m["xmv"][:, :]).then_inc(sg["x_kept"], 1)


def mean_square(dve, sg, m, sq):
    dve.tensor_tensor(sq, m["mv"][:, :, 0], m["mv"][:, :, 0], ALU.mult).then_inc(sg["msq"], 1)
    dve.wait_ge(*sg.once("msq", 1))
    dve.tensor_tensor(sq, sq, m["mv"][:, :, 1], ALU.add).then_inc(sg["msq"], 1)
    dve.wait_ge(*sg.once("msq", 2))


def reciprocal_root(dve, act, sg, name, var, root, out, tmp):
    if act:
        act.wait_ge(*sg.once(name, 1))
        act.activation(root, tmp, ACT.Sqrt).then_inc(sg[name + "_root"], 1)
        return
    dve.tensor_scalar(tmp, var, EPS, None, ALU.add).then_inc(sg.once(name, 1)[0], 1)
    dve.wait_ge(*sg.once(name + "_root", 1))
    dve.reciprocal(out, root).then_inc(sg[name], 1)
    dve.wait_ge(*sg.once(name, 2))
    dve.tensor_tensor(root, tmp, out, ALU.mult).then_inc(sg[name], 1)
    dve.wait_ge(*sg.once(name, 3))
    dve.tensor_tensor(root, root, out, ALU.mult).then_inc(sg[name], 1)
    dve.wait_ge(*sg.once(name, 4))
    dve.tensor_scalar(root, root, -0.5, 1.5, ALU.mult, ALU.add).then_inc(sg[name], 1)
    dve.wait_ge(*sg.once(name, 5))
    dve.tensor_tensor(out, out, root, ALU.mult).then_inc(sg[name], 1)


def prepare(nc, t, m, sg, following):
    with ExitStack() as st:
        wq = m["w"][:, :, :, :]
        NW = 4
        absum = st.enter_context(nc.sbuf_tensor("absum", [128, NW], F32))
        gamma = st.enter_context(nc.sbuf_tensor("gamma", [128, NW], F32))
        geps = st.enter_context(nc.sbuf_tensor("geps", [128, 2, NW], F32))
        up = st.enter_context(nc.sbuf_tensor("up", [128, NW, C, D], F32))
        dn = st.enter_context(nc.sbuf_tensor("dn", [128, NW, C, D], F32))
        sg.phase(w_in=16, const_in=16 * 8, x_in=16, x_stats=B, x_moments=B, x_kept=B, ones_set=2, ident_cast=1, absum_set=NW, gsum_psum=1,
                 gamma_set=1, geps_set=2, tern_up=NW, tern_dn=NW, tern=NW, scaled=NW, quant_diff=NW, quantised=NW)
        block = st.enter_context(nc.Block())

        @block.sync
        def _(sp):
            sp.dma_start(m["w"][:, :, :, :], t["attn_w"][0]).then_inc(sg["w_in"], 16)
            for k in ("col", "fb1", "ident", "hmask", "nmask", "causal"):
                ap = m[k][:, :, :] if len(m[k].shape) == 3 else m[k][:, :]
                sp.dma_start(ap, t[k]).then_inc(sg["const_in"], 16)
            sp.dma_start(m["causalT"][:, 0, :], t["causalT"]).then_inc(sg["const_in"], 16)
            sp.dma_start(m["row"][:, :, :], t["row"].partition_broadcast(128)).then_inc(sg["const_in"], 16)
            sp.dma_start(m["x"][:, :, :], t["x"].rearrange("b s d -> s b d")).then_inc(sg["x_in"], 16)
            sp.wait_ge(sg["x_in"], 16)

        @block.gpsimd
        def _(pool):
            pool.memset(m["onesf"][:, :], 1.0).then_inc(sg["ones_set"], 1)
            pool.memset(m["onesb"][:, :], 1.0).then_inc(sg["ones_set"], 1)
            pool.iota(m["iota"][:, :], pattern=[[1, E]], base=0, channel_multiplier=0,
                      allow_small_or_imprecise_dtypes=True)
            pool.wait_ge(sg["const_in"], 16 * 8)
            pool.tensor_copy(m["identb"][:, :], m["ident"][:, :]).then_inc(sg["ident_cast"], 1)

        @block.tensor
        def _(pe):
            pe.wait_ge(sg["ones_set"], 2)
            pe.wait_ge(sg["absum_set"], NW)
            pe.matmul(m["psum"][:, 0, 0:NW], m["onesf"][:, :], absum[:, :], start=True, stop=True)\
              .then_inc(sg["gsum_psum"], 1)

        @block.vector
        def _(dve):
            dve.wait_ge(sg["w_in"], 16)
            for i in range(NW):
                dve.tensor_reduce(absum[:, i:i + 1], wq[:, i, :, :], axis=AX.XY, op=ALU.add,
                                  apply_absolute_value=True).then_inc(sg["absum_set"], 1)
            dve.wait_ge(sg["gsum_psum"], 1)
            dve.tensor_scalar(gamma[:, :], m["psum"][:, 0, 0:NW], 1.0 / (D * D), None, ALU.mult)\
               .then_inc(sg["gamma_set"], 1)
            dve.wait_ge(sg["gamma_set"], 1)
            dve.tensor_scalar(geps[:, 0, :], gamma[:, :], EPS, 0.5, ALU.add, ALU.mult).then_inc(sg["geps_set"], 1)
            dve.tensor_scalar(geps[:, 1, :], gamma[:, :], EPS, -0.5, ALU.add, ALU.mult).then_inc(sg["geps_set"], 1)
            dve.wait_ge(sg["geps_set"], 2)
            for i in range(NW):
                dve.tensor_scalar(up[:, i, :, :], wq[:, i, :, :], geps[:, 0, i:i + 1], None, ALU.is_gt)\
                   .then_inc(sg["tern_up"], 1)
                dve.tensor_scalar(dn[:, i, :, :], wq[:, i, :, :], geps[:, 1, i:i + 1], None, ALU.is_lt)\
                   .then_inc(sg["tern_dn"], 1)
            for i in range(NW):
                dve.wait_ge(sg["tern_dn"], i + 1)
                dve.tensor_tensor(up[:, i, :, :], up[:, i, :, :], dn[:, i, :, :], ALU.subtract)\
                   .then_inc(sg["tern"], 1)
            for i in range(NW):
                dve.wait_ge(sg["tern"], i + 1)
                dve.tensor_scalar(up[:, i, :, :], up[:, i, :, :], gamma[:, i:i + 1], None, ALU.mult)\
                   .then_inc(sg["scaled"], 1)
            for i in range(NW):
                dve.wait_ge(sg["scaled"], i + 1)
                dve.tensor_tensor(up[:, i, :, :], up[:, i, :, :], wq[:, i, :, :], ALU.subtract)\
                   .then_inc(sg["quant_diff"], 1)
            for i in range(NW):
                dve.wait_ge(sg["quant_diff"], i + 1)
                dve.tensor_tensor(wq[:, i, :, :], wq[:, i, :, :], up[:, i, :, :], ALU.add)\
                   .then_inc(sg["quantised"], 1)
            dve.wait_ge(sg["x_in"], 16)
            for n in range(B):
                if n:
                    dve.wait_ge(sg["x_kept"], n)
                token_stats(dve, sg, m, n, 0, n + 1)
    sg.end(1)


def attention(nc, t, m, sg, name, following):
    cfg = ATTN[name]
    cross, masked, ctx_ln, rms = cfg["cross"], cfg["mask"], cfg["ctx_ln"], cfg["norm"] == "rms"
    in_mask = masked == "input"
    a = ATTN_NAMES.index(name)
    NK, KS = (3, KT_CTX) if cross else (1, S)
    KEYS = NK * KS
    NT = 2 * NK
    bias = name not in ("L1S", "L1C")
    KP = SCP if cross else S
    Q_, K_, V_, O_ = range(4)

    def W(i, c, cols=slice(0, D)):
        return wh[:, i, c, cols], wl[:, i, c, cols]
    x, ident, identb = m["x"], m["ident"], m["identb"]
    PS = m["psum"]
    NKE = 2 if cross else 1

    def col(p, c):
        at = COLS[name + p] + c
        return m["col"][:, at:at + 1]

    def row(p, n):
        return m["row"][0:n, ROWS[name + p], :]

    sg.phase(
        xn=1, xt_psum=1, xt_sb=1, k_psum=NKE, k_sb=NKE, v_psum=NK, v_sb=NK, q_psum=1,
        xt_lo=1, k_lo=NKE, q_sum=1, q_hi=1, q_lo=1, qm_hi=1, qm_lo=1, ot_lo=1,
        s_psum=16, s_max=16, neg_max=2, neg_hi=2, neg_lo=2, nm_psum=2, nm_sb=2,
        t_psum=NT, p_exp=NT, av_psum=2, av_sb=2, t1_psum=1, rden=1, o_norm=1, ot_psum=1, ot_sb=1, o_psum=1, x_new=1,
        **(dict(x_stats=1, x_moments=1, x_kept=1) if following else {}),
        **(dict(xbias=1) if bias else {}),
        **(dict(ctx_in0=8, ctx_in1=8) if cross and not ctx_ln else {}),
        **(dict(c_hi=1, c_lo=1) if cross else {}),
        **(dict(tok_in0=8, tok_in1=8, cxn=NK, ct_psum=NK, ct_sb=NK) if ctx_ln else {}),
        **(dict(p_masked=NT) if masked else {}),
        **(dict(mask_in0=16, mask_in1=16, m_bias=1, m_max=1, m_two=1, any_psum=1, any_sb=1, any_off=1, m_ready=1)
           if in_mask else {}))

    if cross and in_mask:
        order = """NMD1p S0u AV0p NM1p STAT0n S1u NMS1p XT0n T3p S2u XL0n TM3p T4p S3u TM4p CS0n T5p S4u TM5p
            M20n S5u K0n S6u KL0n S7u NMD0u K1n AV1p KL1n ANY0n S8u ANS0n NM0u NMS0u BT0p S9u Q0n BN0p T0u
            QS0n OT0p S10u TM0u V0n S11u OL0p T1u VS0n S12u O0p TM1u V1n S13u OX0p T2u VS1n S14u TM2u V2n
            S15u VS2n"""
    elif cross:
        order = """NMD1p S0u AV0p NM1p STAT0n S1u NMS1p CN0n XT0n C0n CN1n T3p S2u XL0n C1n CN2n T4p S3u C2n
            Q0n CS0n S4u QS0n T5p S5u S6u K0n KL0n S7u NMD0u AV1p S8u K1n NM0u NMS0u KL1n BT0p S9u V0n BN0p
            VS0n T0u OT0p S10u OL0p T1u S11u O0p OX0p V1n S12u VS1n T2u S13u V2n S14u VS2n S15u"""
    else:
        order = """NMD1p S0u AV0p NM1p STAT0n S1u NMS1p XT0n S2u XL0n T1p S3u Q0n S4u TM1p QS0n K0n S5u KL0n
            S6u S7u NMD0u AV1p S8u NM0u S9u NMS0u BT0p S10u BN0p OT0p S11u T0u OL0p S12u O0p TM0u S13u OX0p
            S14u V0n S15u VS0n"""
        if in_mask:
            order = """NMD1p S0u AV0p NM1p STAT0n S1u NMS1p XT0n S2u XL0n T1p S3u K0n S4u TM1p M20n KL0n ANY0n S5u
                S6u ANS0n Q0n S7u QS0n NMD0u AV1p S8u NM0u S9u NMS0u BT0p S10u BN0p OT0p S11u T0u OL0p S12u O0p
                TM0u S13u OX0p S14u V0n S15u VS0n"""
    steps = [(st[:-2], int(st[-2]), st[-1]) if not st[-3:-1].isdigit() else (st[:-3], int(st[-3:-1]), st[-1])
             for st in order.replace("M20n", "MM0n").split()]
    absent = (() if ctx_ln else ("C", "CN")) + (() if masked else ("TM",))
    steps = [st for st in steps if st[0] not in absent]
    opening_steps = [st for st in steps if st[2] == "n"]
    closing_steps = [(st, k) for st, k, whose in steps if whose == "p"]
    SHARED = ("AV", "NM", "XT", "C", "Q", "K", "BT", "OT", "O", "V", "ANY")
    BANK = {f"{st}{k}": 6 + n % 2 for n, (st, k, _) in enumerate(st for st in steps if st[0] in SHARED)}
    READ_BY = {"BT0": ("o_norm", 1), "OT0": ("ot_sb", 1), "O0": ("x_new", 1), "K0": ("k_lo", 1), "K1": ("k_lo", 2),
               "V0": ("v_sb", 1), "V1": ("v_sb", 2), "V2": ("v_sb", 3), "C0": ("ct_sb", 1), "C1": ("ct_sb", 2),
               "C2": ("ct_sb", 3), "ANY0": ("any_sb", 1), "XT0": ("xt_sb", 1), "Q0": ("q_sum", 1),
               "NM0": ("nm_sb", 1), "NM1": ("nm_sb", 2), "AV0": ("av_sb", 1), "AV1": ("av_sb", 2)}

    def walk(un, prev, nxt):
        for st, k, whose in steps:
            w = {"u": un, "p": prev, "n": nxt}[whose]
            if w:
                yield st, k, w

    def opening(un):
        for st, k, _ in opening_steps:
            yield st, k, un

    def closing(un):
        for st, k in closing_steps:
            yield st, k, un

    with ExitStack() as stk:
        def sb(nm, shape, dt=F32):
            return stk.enter_context(nc.sbuf_tensor(name + nm, shape, dt))
        ctxT = sb("ctxT", [128, 2, C, SCP]) if cross and not ctx_ln else None
        cH = sb("cH", [128, C, SCP], F32R) if cross else None
        cL = sb("cL", [128, C, SCP], F32R) if cross else None
        ctok = sb("ctok", [KS, 2, NK, D]) if ctx_ln else None
        cxn = sb("cxn", [KS, NK, D]) if ctx_ln else None
        root, vare, sq = sb("root", [S, B]), sb("vare", [S, B]), sb("sq", [S, B])
        croot = sb("croot", [KS, B * NK]) if ctx_ln else None
        cvare = sb("cvare", [KS, B * NK]) if ctx_ln else None
        kH = sb("kH", [128, 2, C, KP], F32R)
        kL = sb("kL", [128, 2, C, KP], F32R)
        vA = sb("vA", [KS, 2, NK, H, 32])
        xn = sb("xn", [S, D])
        xT = sb("xT", [128, C, S])
        junk = sb("junk", [S, 2, KEYS]) if masked else None
        wh, wl = sb("wh", [128, 4, C, D], F32R), sb("wl", [128, 4, C, D], F32R)
        xH, xL = sb("xH", [128, C, S], F32R), sb("xL", [128, C, S], F32R)
        qf = sb("qf", [128, C, S])
        qH, qL = sb("qH", [128, C, S], F32R), sb("qL", [128, C, S], F32R)
        qmH = sb("qmH", [128, 2, C, 8, S], F32R)
        qmL = sb("qmL", [128, 2, C, 8, S], F32R)
        oH, oL = sb("oH", [128, C, S], F32R), sb("oL", [128, C, S], F32R)
        mx = sb("mx", [S, H])
        amb = sb("amb", [S, 2, 1])
        nmx = sb("nmx", [S, 2, 8])
        nmb = sb("nmb", [S, 2, 2, 8], BF16)
        nmT = sb("nmT", [16, H, S], BF16)
        P = sb("P", [KS, 2, NK, 8, S])
        avT = sb("avT", [128, 4, S])
        rden = sb("rden", [S, H])
        on = sb("on", [S, D])
        oT = sb("oT", [128, C, S])
        mi = sb("mi", [S, 2, KEYS], I32) if in_mask else None
        miT = sb("miT", [KS, 2, NK, S], I32) if in_mask else None
        mb = sb("mb", [S, 2, KEYS]) if in_mask else None
        m2 = sb("m2", [KS, 2, NK, S], BF16) if in_mask else None
        anyB = sb("anyB", [128, 2, S]) if in_mask else None
        aoff = sb("aoff", [128, S], BF16) if in_mask else None
        block = stk.enter_context(nc.Block())

        cxT = sb("cxT", [128, 1, C, SCP]) if ctx_ln else None

        @block.sync
        def _(sp):
            def load(un, free):
                if cross and not ctx_ln:
                    if free:
                        sp.wait_ge(*sg.at("c_lo", free))
                    sp.dma_start(ctxT[:, un.par, :, 0:SC], t["ctxT"][un.n]).then_inc(sg[f"ctx_in{un.par}"], 16)
                if ctx_ln:
                    if free:
                        sp.wait_ge(*sg.at("cxn", free))
                    sp.dma_start(ctok[:, un.par, :, :], t["ctx"][un.n].rearrange("(k p) d -> p k d", p=KS))\
                      .then_inc(sg[f"tok_in{un.par}"], 16)
                if in_mask:
                    if free:
                        sp.wait_ge(*sg.at("m_two", free))
                        sp.wait_ge(*sg.at("m_bias", free))
                    sp.dma_start(mi[:, un.par, :], t["mask" + name][un.n]).then_inc(sg[f"mask_in{un.par}"], 16)
                    sp.dma_start(miT[:, un.par, :, :],
                                 t["maskT" + name][un.n].rearrange("(k p) q -> p k q", p=KS))\
                      .then_inc(sg[f"mask_in{un.par}"], 16)

            if cross or in_mask:
                load(Unit(0, 0), None)
                load(Unit(0, 1), None)
            if a + 1 < len(ATTN):
                sp.wait_ge(*sg.once("w_lo", 4))
                sp.dma_start(m["w"][:, :, :, :], t["attn_w"][a + 1]).then_inc(sg["w_next"], 16)
            if cross or in_mask:
                with sp.Fori(0, B // 2 - 1) as pair:
                    load(Unit(pair, 2), Unit(pair, 0))
                    load(Unit(pair, 3), Unit(pair, 1))

        @block.gpsimd
        def _(pool):
            if cross:
                src = (cxT if ctx_ln else ctxT)
                pool.memset(src[:, :, :, SC:SCP], 0.0).then_inc(sg["ctx_pad"], 1)
                pool.wait_ge(*sg.once("ctx_pad", 1))
            pool.memset(vA[:, :, :, :, HD + 1:32], 0.0).then_inc(sg["v_const"], 1)
            pool.memset(vA[:, :, :, :, HD:HD + 1], 1.0).then_inc(sg["v_const"], 1)

            def items(seq):
                for st, k, un in seq:
                    later = not (isinstance(un.pair, int) and un.pair * 2 + un.k == 0)
                    if st == "CS":
                        if ctx_ln:
                            wait_apart(pool, sg, sg.at("ct_sb", un))
                            src = cxT[:, 0, :, :]
                        else:
                            wait_apart(pool, sg, sg.loaded("ctx_in", un))
                            src = ctxT[:, un.par, :, :]
                        if later:
                            wait_apart(pool, sg, sg.at("v_psum", un.step(-1)))
                        pool.tensor_copy(cH[:, :, :], src).then_inc(sg["c_hi"], 1)
                        pool.wait_ge(*sg.at("c_hi", un))
                        pool.tensor_tensor(cL[:, :, :], src, cH[:, :, :].bitcast(F32), ALU.subtract)\
                            .then_inc(sg["c_lo"], 1)
                    elif st == "QS":
                        for half, mask_of, ready, done in ((qH, qmH, "q_hi", "qm_hi"), (qL, qmL, "q_lo", "qm_lo")):
                            pool.wait_ge(*sg.at(ready, un))
                            if later and half is qH and not (isinstance(un.pair, int) and un.pair * 2 + un.k == 1):
                                pool.wait_ge(*sg.at("t_psum", un.step(-2)))
                            pool.tensor_tensor(mask_of[:, un.par, :, :, :],
                                               half[:, :, :].bitcast(F32).unsqueeze(2).broadcast_to([128, C, 8, S]),
                                               m["hmask"][:, :].unsqueeze(1).unsqueeze(3)
                                               .broadcast_to([128, C, 8, S]), ALU.mult).then_inc(sg[done], 1)
                    elif st == "STAT":
                        if bias:
                            pool.wait_ge(*sg.at("xn", un))
                            pool.tensor_tensor(x[:, un.n, :], x[:, un.n, :], row("bo", S), ALU.add)\
                                .then_inc(sg["xbias"], 1)
                        if in_mask:
                            wait_apart(pool, sg, sg.loaded("mask_in", un))
                            if not (isinstance(un.pair, int) and un.pair * 2 + un.k <= 1):
                                wait_apart(pool, sg, sg.at("s_max", un.step(-2)))
                            pool.tensor_scalar(mb[:, un.par, :], mi[:, un.par, :], 0.0, NEG, ALU.is_equal,
                                               ALU.mult).then_inc(sg["m_bias"], 1)
            items(opening(Unit(0, 0)))
            units(pool, B, lambda un, prev, nxt: items(walk(un, prev, nxt)))

        @block.scalar
        def _(act):
            def items(seq):
                for st, k, un in seq:
                    later = not (isinstance(un.pair, int) and un.pair * 2 + un.k == 0)
                    if st == "XT":
                        act.wait_ge(*sg.at("xt_psum", un))
                        if later:
                            act.wait_ge(*sg.at("q_psum", un.step(-1)))
                            act.wait_ge(*sg.at("xt_lo", un.step(-1)))
                            if not cross:
                                act.wait_ge(*sg.at("v_psum", un.step(-1)))
                        for dst in (xT, xH):
                            for c in range(C):
                                ins = act.activation(dst[:, c, :], PS[:, BANK["XT0"], c * S:(c + 1) * S],
                                                     ACT.Identity, bias=0.0 if rms else col("b", c),
                                                     scale=col("g", c))
                        ins.then_inc(sg["xt_sb"], 1)
                    elif st == "C":
                        act.wait_ge(*sg.at("ct_psum", un, k + 1))
                        if later and k == 0:
                            act.wait_ge(*sg.at("c_lo", un.step(-1)))
                        for c in range(C):
                            ins = act.activation(cxT[:, 0, c, k * KS:(k + 1) * KS],
                                                 PS[:, BANK[f"C{k}"], c * KS:(c + 1) * KS], ACT.Identity,
                                                 bias=col("b", c), scale=col("g", c))
                        ins.then_inc(sg["ct_sb"], 1)
                    elif st == "K":
                        act.wait_ge(*sg.at("k_psum", un, k + 1))
                        if cross:
                            act.activation(kH[:, un.par, k, :], PS[:, BANK[f"K{k}"], 0:SCP], ACT.Identity,
                                           bias=col("bk", k) if bias else 0.0).then_inc(sg["k_sb"], 1)
                        else:
                            for c in range(C):
                                ins = act.activation(kH[:, un.par, c, :], PS[:, BANK["K0"], c * S:(c + 1) * S],
                                                     ACT.Identity, bias=col("bk", c) if bias else 0.0)
                            ins.then_inc(sg["k_sb"], 1)
                    elif st == "OT":
                        act.wait_ge(*sg.at("ot_psum", un))
                        if later:
                            act.wait_ge(*sg.at("o_psum", un.step(-1)))
                        for dst in (oT, oH):
                            ins = act.activation(dst[:, :, :], PS[:, BANK["OT0"], 0:C * S]
                                                 .rearrange("p (c s) -> p c s", c=C), ACT.Identity)
                        ins.then_inc(sg["ot_sb"], 1)
                    elif st == "T":
                        i, kt = k // NK, k % NK
                        act.wait_ge(*sg.at("t_psum", un, k + 1))
                        if later and kt == 0:
                            act.wait_ge(*sg.at("av_psum", un.step(-1), i + 1))
                        b = 2 * (k % 2)
                        act.activation(P[:, i, kt, :, :].rearrange("p (b j) s -> p b (j s)", b=2),
                                       PS[0:KS, b:b + 2, 0:4 * S], ACT.Exp)\
                            .then_inc(sg["p_exp"], 1)
                    elif st == "AV":
                        act.wait_ge(*sg.at("av_psum", un, k + 1))
                        if later:
                            act.wait_ge(*sg.at("t1_psum", un.step(-1)))
                        act.activation(avT[:, 2 * k:2 * k + 2, :],
                                       PS[:, BANK[f"AV{k}"], 0:2 * S].rearrange("p (g s) -> p g s", g=2),
                                       ACT.Identity).then_inc(sg["av_sb"], 1)

            reciprocal_root(None, act, sg, "rstd", None, root[:, :], None, vare[:, :])
            if ctx_ln:
                reciprocal_root(None, act, sg, "c_rstd", None, croot[:, :], None, cvare[:, :])
            items(opening(Unit(0, 0)))
            units(act, B, lambda un, prev, nxt: items(walk(un, prev, nxt)))
            items(closing(Unit(B // 2 - 1, 1)))

        @block.vector
        def _(dve):
            if a:
                dve.wait_ge(*sg.once("w_next", 0))
            w = m["w"][:, :, :, :]
            for i in (K_, V_, Q_, O_):
                dve.tensor_copy(wh[:, i, :, :], w[:, i, :, :]).then_inc(sg["w_hi"], 1)
            for n, i in enumerate((K_, V_, Q_, O_)):
                dve.wait_ge(*sg.once("w_hi", n + 1))
                dve.tensor_tensor(wl[:, i, :, :], w[:, i, :, :], wh[:, i, :, :].bitcast(F32),
                                  ALU.subtract).then_inc(sg["w_lo"], 1)
            if not in_mask:
                dve.memset(amb[:, :, :], 0.0).then_inc(sg["amb_zero"], 1)

            def items(seq):
                for st, k, un in seq:
                    later = not (isinstance(un.pair, int) and un.pair * 2 + un.k == 0)
                    if st == "STAT":
                        if not later:
                            dve.wait_ge(*sg.once("rstd", 6))
                        else:
                            dve.wait_ge(*sg.at("xt_psum", un.step(-1)))
                        if rms:
                            dve.tensor_scalar(xn[:, :], x[:, un.n, :], m["rs"][:, bass.ds(un.n, 1)], None, ALU.mult)\
                               .then_inc(sg["xn"], 1)
                        else:
                            dve.tensor_scalar(xn[:, :], x[:, un.n, :], m["mv"][:, un.n, 0:1],
                                              m["rs"][:, bass.ds(un.n, 1)], ALU.subtract, ALU.mult)\
                               .then_inc(sg["xn"], 1)
                    elif st == "MM":
                        dve.wait_ge(*sg.loaded("mask_in", un))
                        if later and not (isinstance(un.pair, int) and un.pair * 2 + un.k == 1):
                            dve.wait_ge(*sg.at("p_masked", un.step(-2)))
                        dve.tensor_scalar(m2[:, un.par, :, :], miT[:, un.par, :, :], 0.0, KEEP,
                                          ALU.not_equal, ALU.mult).then_inc(sg["m_two"], 1)
                    elif st == "CN":
                        if k == 0:
                            dve.wait_ge(*sg.loaded("tok_in", un))
                            if not later:
                                dve.wait_ge(*sg.once("c_rstd", 6))
                        if later:
                            dve.wait_ge(*sg.at("ct_psum", un.step(-1), k + 1))
                        dve.tensor_scalar(cxn[:, k, :], ctok[:, un.par, k, :], m["cmv"][:, un.n * NK + k, 0:1],
                                          m["crs"][:, bass.ds(un.n * NK + k, 1)], ALU.subtract, ALU.mult)\
                           .then_inc(sg["cxn"], 1)
                    elif st == "ANS":
                        dve.wait_ge(*sg.at("any_psum", un))
                        dve.tensor_scalar(anyB[:, un.par, :], PS[:, BANK["ANY0"], 0:S], 1.0, None, ALU.min)\
                           .then_inc(sg["any_sb"], 1)
                        dve.wait_ge(*sg.at("any_sb", un))
                        dve.tensor_scalar(aoff[:, :], anyB[:, un.par, :], -KEEP, KEEP, ALU.mult, ALU.add)\
                           .then_inc(sg["any_off"], 1)
                        dve.wait_ge(*sg.at("any_off", un))
                        dve.tensor_tensor(m2[:, un.par, :, :], m2[:, un.par, :, :],
                                          aoff[0:KS, :].unsqueeze(1).broadcast_to([KS, NK, S]), ALU.max)\
                           .then_inc(sg["m_ready"], 1)
                        dve.wait_ge(*sg.at("m_bias", un))
                        dve.tensor_reduce(amb[:, un.par, :], mb[:, un.par, :], axis=AX.X, op=ALU.max)\
                           .then_inc(sg["m_max"], 1)
                    elif st == "S":
                        h = k
                        wait = (lambda sig: wait_apart(dve, sg, sig)) if masked else (lambda sig: dve.wait_ge(*sig))
                        wait(sg.at("s_psum", un, k + 1))
                        if k % 8 == 0 and later:
                            wait(sg.at("neg_max", un.step(-1), k // 8 + 1))
                        sc = PS[0:S, 4 + k % 2, 0:KEYS]
                        if masked:
                            mask = mb[:, un.par, :] if in_mask else m["causal"][:, :]
                            if k == 0 and in_mask:
                                wait(sg.at("m_bias", un))
                            dve.tensor_tensor_reduce(out=junk[:, k % 2, 0:KEYS], in0=sc, in1=mask, scale=1.0, scalar=-3e38,
                                                     op0=ALU.add, op1=ALU.max, accum_out=mx[:, h:h + 1])\
                               .then_inc(sg["s_max"], 1)
                        else:
                            dve.reduce_max(mx[:, h:h + 1], sc, AX.X).then_inc(sg["s_max"], 1)
                    elif st == "NMD":
                        dve.wait_ge(*sg.at("s_max", un, 8 * k + 8))
                        if not in_mask and not later and k == 0:
                            dve.wait_ge(*sg.once("amb_zero", 1))
                        if in_mask and k == 0:
                            dve.wait_ge(*sg.at("m_max", un))
                        dve.tensor_scalar(nmx[:, k, :], mx[:, 8 * k:8 * k + 8], amb[:, un.par, :], -1.0,
                                          ALU.subtract, ALU.mult).then_inc(sg["neg_max"], 1)
                        dve.wait_ge(*sg.at("neg_max", un, k + 1))
                        if later:
                            dve.wait_ge(*sg.at("nm_psum", un.step(-1), k + 1))
                        dve.tensor_copy(nmb[:, k, 0, :], nmx[:, k, :]).then_inc(sg["neg_hi"], 1)
                        dve.wait_ge(*sg.at("neg_hi", un, k + 1))
                        dve.tensor_tensor(nmb[:, k, 1, :], nmx[:, k, :], nmb[:, k, 0, :], ALU.subtract)\
                           .then_inc(sg["neg_lo"], 1)
                    elif st == "NMS":
                        dve.wait_ge(*sg.at("nm_psum", un, k + 1))
                        if later:
                            dve.wait_ge(*sg.at("t_psum", un.step(-1), (k + 1) * NK))
                        dve.tensor_tensor(nmT[:, 8 * k:8 * k + 8, :],
                                          PS[0:16, BANK[f"NM{k}"], 0:S // 2].bitcast(BF16)
                                          .unsqueeze(1).broadcast_to([16, 8, S]),
                                          m["nmask"][0:16, :].unsqueeze(2).broadcast_to([16, 8, S]),
                                          ALU.mult).then_inc(sg["nm_sb"], 1)
                    elif st == "TM":
                        i, kt = k // NK, k % NK
                        dve.wait_ge(*sg.at("p_exp", un, k + 1))
                        if in_mask and k == 0:
                            dve.wait_ge(*sg.at("m_ready", un))
                        mT = m2[:, un.par, kt, :] if in_mask else m["causalT"][:, 0, :]
                        dve.tensor_tensor(P[:, i, kt, :, :], P[:, i, kt, :, :],
                                          mT.unsqueeze(1).broadcast_to([KS, 8, S]), ALU.min)\
                           .then_inc(sg["p_masked"], 1)
                    elif st == "QS":
                        dve.wait_ge(*sg.at("q_psum", un))
                        if in_mask:
                            dve.wait_ge(*sg.at("any_sb", un))
                        if later:
                            dve.wait_ge(*sg.at("qm_lo", un.step(-1)))
                        for c in range(C):
                            src = PS[:, BANK["Q0"], c * S:(c + 1) * S]
                            if in_mask:
                                ins = dve.scalar_tensor_tensor(qf[:, c, :], src, QK_SCALE, anyB[:, un.par, :],
                                                               ALU.mult, ALU.mult)
                            elif bias:
                                ins = dve.tensor_scalar(qf[:, c, :], src, col("bq", c), QK_SCALE, ALU.add, ALU.mult)
                            else:
                                ins = dve.tensor_scalar(qf[:, c, :], src, QK_SCALE, None, ALU.mult)
                        ins.then_inc(sg["q_sum"], 1)
                        dve.wait_ge(*sg.at("q_sum", un))
                        dve.tensor_copy(qH[:, :, :], qf[:, :, :]).then_inc(sg["q_hi"], 1)
                        dve.wait_ge(*sg.at("q_hi", un))
                        dve.tensor_tensor(qL[:, :, :], qf[:, :, :], qH[:, :, :].bitcast(F32), ALU.subtract)\
                           .then_inc(sg["q_lo"], 1)
                    elif st == "XL":
                        dve.wait_ge(*sg.at("xt_sb", un))
                        if later:
                            dve.wait_ge(*sg.at("q_psum", un.step(-1)))
                            if not cross:
                                dve.wait_ge(*sg.at("v_psum", un.step(-1)))
                        dve.tensor_tensor(xL[:, :, :], xT[:, :, :], xH[:, :, :].bitcast(F32), ALU.subtract)\
                           .then_inc(sg["xt_lo"], 1)
                    elif st == "OL":
                        dve.wait_ge(*sg.at("ot_sb", un))
                        if later:
                            dve.wait_ge(*sg.at("o_psum", un.step(-1)))
                        dve.tensor_tensor(oL[:, :, :], oT[:, :, :], oH[:, :, :].bitcast(F32), ALU.subtract)\
                           .then_inc(sg["ot_lo"], 1)
                    elif st == "KL":
                        dve.wait_ge(*sg.at("k_sb", un, k + 1))
                        n, w = (1, SCP) if cross else (C, S)
                        for c in range(n):
                            at = k + c
                            src = PS[:, BANK[f"K{k}"], c * S:c * S + w]
                            ins = dve.scalar_tensor_tensor(kL[:, un.par, at, :], src, col("bk", at),
                                                           kH[:, un.par, at, :].bitcast(F32), ALU.add, ALU.subtract)
                        ins.then_inc(sg["k_lo"], 1)
                    elif st == "VS":
                        dve.wait_ge(*sg.at("v_psum", un, k + 1))
                        dst = vA[:, un.par, k, :, 0:HD]
                        src = PS[0:KS, BANK[f"V{k}"], 0:D].rearrange("p (h d) -> p h d", h=H)
                        if bias:
                            dve.tensor_tensor(dst, src, row("bv", KS).rearrange("p (h d) -> p h d", h=H), ALU.add)\
                               .then_inc(sg["v_sb"], 1)
                        else:
                            dve.tensor_copy(dst, src).then_inc(sg["v_sb"], 1)
                    elif st == "BN":
                        dve.wait_ge(*sg.at("t1_psum", un))
                        dve.reciprocal(rden[:, :], PS[0:S, BANK["BT0"], :]
                                       .rearrange("p (h c) -> p h c", h=H)[:, :, HD])\
                           .then_inc(sg["rden"], 1)
                        dve.wait_ge(*sg.at("rden", un))
                        if later:
                            dve.wait_ge(*sg.at("ot_psum", un.step(-1)))
                        dve.tensor_tensor(on[:, :].rearrange("p (h d) -> p h d", h=H),
                                          PS[0:S, BANK["BT0"], :].rearrange("p (h c) -> p h c", h=H)[:, :, 0:HD],
                                          rden[:, :].unsqueeze(2).broadcast_to([S, H, HD]), ALU.mult)\
                           .then_inc(sg["o_norm"], 1)
                    elif st == "OX":
                        dve.wait_ge(*sg.at("o_psum", un))
                        if bias:
                            dve.wait_ge(*sg.at("xbias", un))
                        dve.tensor_tensor(x[:, un.n, :], PS[0:S, BANK["O0"], 0:D], x[:, un.n, :], ALU.add)\
                           .then_inc(sg["x_new"], 1)
                        if following:
                            wait_apart(dve, sg, sg.at("x_new", un))
                            if later:
                                wait_apart(dve, sg, sg.at("x_kept", un.step(-1)))
                            token_stats(dve, sg, m, un.n, un, 1)

            if rms:
                mean_square(dve, sg, m, sq[:, :])
            reciprocal_root(dve, None, sg, "rstd", sq[:, :] if rms else m["mv"][:, :, 1], root[:, :], m["rs"][:, :], vare[:, :])
            if ctx_ln:
                reciprocal_root(dve, None, sg, "c_rstd", m["cmv"][:, :, 1], croot[:, :], m["crs"][:, :], cvare[:, :])
            items(opening(Unit(0, 0)))
            units(dve, B, lambda un, prev, nxt: items(walk(un, prev, nxt)))
            items(closing(Unit(B // 2 - 1, 1)))

        @block.tensor
        def _(pe):
            user = {6: None, 7: None}

            def take(st, un):
                b = BANK[st]
                if user[b]:
                    was, w = user[b]
                    sem, k = READ_BY[was]
                    pe.wait_ge(*sg.at(sem, w, k))
                user[b] = (st, un)

            def items(seq):
                for st, k, un in seq:
                    if st == "XT":
                        pe.wait_ge(*sg.at("xn", un))
                        take("XT0", un)
                        for c in range(C):
                            ins = pe.transpose(PS[:, BANK["XT0"], c * S:(c + 1) * S], xn[:, c * 128:(c + 1) * 128],
                                               ident[0:S, 0:S])
                        ins.then_inc(sg["xt_psum"], 1)
                    elif st == "C":
                        pe.wait_ge(*sg.at("cxn", un, k + 1))
                        take(f"C{k}", un)
                        for c in range(C):
                            ins = pe.transpose(PS[:, BANK[f"C{k}"], c * KS:(c + 1) * KS],
                                               cxn[:, k, c * 128:(c + 1) * 128], ident[0:KS, 0:KS])
                        ins.then_inc(sg["ct_psum"], 1)
                    elif st == "ANY":
                        pe.wait_ge(*sg.at("m_two", un))
                        take("ANY0", un)
                        for kt in range(NK):
                            ins = pe.matmul(PS[:, BANK["ANY0"], 0:S], m["onesb"][0:KS, :], m2[:, un.par, kt, :],
                                            start=kt == 0, stop=kt == NK - 1)
                        ins.then_inc(sg["any_psum"], 1)
                    elif st == "K":
                        if cross:
                            if k == 0:
                                pe.wait_ge(*sg.at("c_lo", un))
                            take(f"K{k}", un)
                            for c in range(C):
                                ins = split_product(pe, PS[:, BANK[f"K{k}"], 0:SCP],
                                                    W(K_, c, slice(k * 128, (k + 1) * 128)),
                                                    (cH[:, c, :], cL[:, c, :]), c == 0, c == C - 1)
                        else:
                            pe.wait_ge(*sg.at("xt_lo", un))
                            take("K0", un)
                            for mo in range(C):
                                for c in range(C):
                                    ins = split_product(pe, PS[:, BANK["K0"], mo * S:(mo + 1) * S],
                                                        W(K_, c, slice(mo * 128, (mo + 1) * 128)),
                                                        (xH[:, c, :], xL[:, c, :]), c == 0, c == C - 1)
                        ins.then_inc(sg["k_psum"], 1)
                    elif st == "V":
                        take(f"V{k}", un)
                        hi, lo = (cH, cL) if cross else (xH, xL)
                        for c in range(C):
                            ks = slice(k * KS, (k + 1) * KS)
                            ins = split_product(pe, PS[0:KS, BANK[f"V{k}"], 0:D], (hi[:, c, ks], lo[:, c, ks]),
                                                W(V_, c), c == 0, c == C - 1)
                        ins.then_inc(sg["v_psum"], 1)
                    elif st == "Q":
                        pe.wait_ge(*sg.at("xt_lo", un))
                        take("Q0", un)
                        for mo in range(C):
                            for c in range(C):
                                ins = split_product(pe, PS[:, BANK["Q0"], mo * S:(mo + 1) * S],
                                                    W(Q_, c, slice(mo * 128, (mo + 1) * 128)),
                                                    (xH[:, c, :], xL[:, c, :]), c == 0, c == C - 1)
                        ins.then_inc(sg["q_psum"], 1)
                    elif st == "S":
                        i = k // 8
                        later = not (isinstance(un.pair, int) and un.pair * 2 + un.k == 0)
                        if k == 0:
                            pe.wait_ge(*sg.at("qm_hi", un))
                            pe.wait_ge(*sg.at("k_sb", un))
                        if k >= 2:
                            pe.wait_ge(*sg.at("s_max", un, k - 1))
                        elif later:
                            pe.wait_ge(*sg.at("s_max", un.step(-1), 15 + k))
                        pe.matmul(PS[0:S, 4 + k % 2, 0:KP], qmH[:, un.par, i, k % 8, :], kH[:, un.par, i, :],
                                  start=True, stop=True).then_inc(sg["s_psum"], 1)
                    elif st == "NM":
                        pe.wait_ge(*sg.at("neg_lo", un, k + 1))
                        take(f"NM{k}", un)
                        pe.transpose(PS[0:16, BANK[f"NM{k}"], 0:S // 2].bitcast(BF16),
                                     nmb[:, k, :, :].rearrange("p a b -> p (a b)"), identb[0:S, 0:S])\
                          .then_inc(sg["nm_psum"], 1)
                    elif st == "T":
                        i, kt = k // NK, k % NK
                        later = not (isinstance(un.pair, int) and un.pair * 2 + un.k == 0)
                        if kt == 0:
                            pe.wait_ge(*sg.at("nm_sb", un, i + 1))
                        if k == 0:
                            pe.wait_ge(*sg.at("qm_lo", un))
                            pe.wait_ge(*sg.at("k_lo", un))
                        if k >= 2:
                            pe.wait_ge(*sg.at("p_exp", un, k - 1))
                        elif later:
                            pe.wait_ge(*sg.at("p_exp", un.step(-1), NT - 1 + k))
                        ks = slice(kt * KS, (kt + 1) * KS)
                        for e in range(2):
                            o = PS[0:KS, 2 * (k % 2) + e, 0:4 * S]
                            split_product(pe, o, (kH[:, un.par, i, ks], kL[:, un.par, i, ks]),
                                          (qmH[:, un.par, i, 4 * e:4 * e + 4, :], qmL[:, un.par, i, 4 * e:4 * e + 4, :]),
                                          True, False)
                            ins = pe.matmul(o, m["onesb"][0:16, 0:KS],
                                            nmT[:, 8 * i + 4 * e:8 * i + 4 * e + 4, :], start=False, stop=True)
                        ins.then_inc(sg["t_psum"], 1)
                    elif st == "AV":
                        i = k
                        pe.wait_ge(*sg.at("p_masked" if masked else "p_exp", un, (i + 1) * NK))
                        if i == 0:
                            if not (isinstance(un.pair, int) and un.pair * 2 + un.k > 0):
                                pe.wait_ge(*sg.once("v_const", 2))
                            pe.wait_ge(*sg.at("v_sb", un))
                        take(f"AV{i}", un)
                        for e in range(2):
                            for kt in range(NK):
                                for j in range(4):
                                    ins = pe.matmul(PS[32 * j:32 * j + 32, BANK[f"AV{i}"], e * S:(e + 1) * S],
                                                    vA[:, un.par, kt, 8 * i + 4 * e + j, :], P[:, i, kt, 4 * e + j, :],
                                                    start=kt == 0, stop=kt == NK - 1)
                        ins.then_inc(sg["av_psum"], 1)
                    elif st == "BT":
                        pe.wait_ge(*sg.at("av_sb", un))
                        take("BT0", un)
                        for g in range(4):
                            ins = pe.transpose(PS[0:S, BANK["BT0"], g * 128:(g + 1) * 128], avT[:, g, :], ident[:, :])
                        ins.then_inc(sg["t1_psum"], 1)
                    elif st == "OT":
                        pe.wait_ge(*sg.at("o_norm", un))
                        take("OT0", un)
                        for c in range(C):
                            ins = pe.transpose(PS[:, BANK["OT0"], c * S:(c + 1) * S], on[:, c * 128:(c + 1) * 128],
                                               ident[0:S, 0:S])
                        ins.then_inc(sg["ot_psum"], 1)
                    elif st == "O":
                        pe.wait_ge(*sg.at("ot_lo", un))
                        take("O0", un)
                        for c in range(C):
                            ins = split_product(pe, PS[0:S, BANK["O0"], 0:D], (oH[:, c, :], oL[:, c, :]), W(O_, c),
                                                c == 0, c == C - 1)
                        ins.then_inc(sg["o_psum"], 1)

            def body(un, prev, nxt):
                if prev:
                    for b, (st, w) in list(user.items()):
                        user[b] = (st, un.step(w.k - body.at - 1))
                items(walk(un, prev, nxt))
                body.at = un.k

            pe.wait_ge(*sg.once("w_lo", 4))
            items(opening(Unit(0, 0)))
            body.at = 0
            units(pe, B, body)
            items(closing(Unit(B // 2 - 1, 1)))
    sg.end(B, w_hi=4, w_lo=4, w_next=16 if a + 1 < len(ATTN) else 0, ctx_pad=1 if cross else 0, v_const=2, **(dict(msq=2) if rms else {}), **({} if in_mask else dict(amb_zero=1)), rstd=6, rstd_root=1, **(dict(c_rstd=6, c_rstd_root=1) if ctx_ln else {}))


def ffn(nc, t, m, sg, name, following):
    moe = name == "MOE"
    npass = 1 + E if moe else 1
    w0 = {"MOE": 0, "F2": 1 + E, "F3": 2 + E}[name]
    PS, x, ident = m["psum"], m["x"], m["ident"]
    act_fn = ACT.Silu if moe else ACT.Gelu

    def col(p, c):
        at = COLS[name + p] + c
        return m["col"][:, at:at + 1]

    order = """XN0n H0u H1u HL0u XT0n XN1n H2u HL1u XS0n XT1n LG0n XN2n H3u HL2u H4u HL3u XS1n XT2n LG1n
        XN3n H5u HL4u H6u HL5u XS2n XT3n LG2n H7u HL6u Y0u HL7u XS3n LG3n Y1u YA0u CM0n Y2u YA1u CM1n Y3u YA2u
        CM2n YA3u CM3n GT0n"""
    steps = [(st[:-2], int(st[-2]), st[-1]) for st in order.split()]
    if not moe:
        steps = [st for st in steps if st[0] not in ("LG", "CM", "GT")]
    unit_steps = [(st, k) for st, k, whose in steps if whose == "u"]

    per_tile = dict(x_stats=TB, x_moments=TB, x_kept=TB, f_xn=TB, f_xbias=TB, f_xt_psum=TB, f_xt_sb=TB, f_hi=TB,
                    f_lo=TB)
    if moe:
        del per_tile["f_xbias"]
        per_tile.update(c_in0=32, c_in1=32, c_stats=3 * TB, c_moments=TB, c_kept=TB, lg_psum=TB, top=TB, topi=TB,
                        topf=TB, gdiff=1, gexp=1, gden=1, grec=1, gsec=1, lg_sb=1, gtwo=TB, gates_set=TB)
    per_step = dict(h_psum=HC, h_hi=HC, h_lo=HC, y_psum=TB, y_acc=TB)
    per_pass = dict(w1_in=16, w2_in=16, w1_hi=1, w1_lo=1, w2_hi=1, w2_lo=1)
    sg.phase(**per_tile, **per_step, **per_pass)
    for s in ("gates_in",):
        sg.once(s, 0)
    with ExitStack() as stk:
        def sb(nm, shape, dt=F32):
            return stk.enter_context(nc.sbuf_tensor(name + nm, shape, dt))
        w1f, w2f = sb("w1f", [128, C, HID]), sb("w2f", [128, HC, D])
        w1 = [sb("w1H", [128, C, HID], F32R), sb("w1L", [128, C, HID], F32R)]
        w2 = [sb("w2H", [128, HC, D], F32R), sb("w2L", [128, HC, D], F32R)]
        xn = sb("xn", [S, 2, D])
        root, vare, sq = sb("root", [S, B]), sb("vare", [S, B]), sb("sq", [S, B])
        hnf = sb("hnf", [128, 2, C, S])
        hn = [sb("hnH", [128, NTILES if moe else 2, C, TOK], F32R), sb("hnL", [128, NTILES if moe else 2, C, TOK], F32R)]
        hf = sb("hf", [128, 2, TOK])
        hT = [sb("hH", [128, HC, TOK], F32R), sb("hL", [128, HC, TOK], F32R)]
        if moe:
            gw = sb("gw", [128, C, E])
            gates = sb("gates", [S, B, E])
            top, topi, topf = sb("top", [S, TB, 8]), sb("topi", [S, TB, 8], U32), sb("topf", [S, TB, 2])
            gd, ge, gn, g1, g2 = (sb(f"g{k}", [S, TB]) for k in range(5))
            one, two = sb("one", [S, TB, E]), sb("two", [S, TB, E])
            lgs = sb("lgs", [S, TB, E])
            ctok, cst = sb("ctok", [KT_CTX, 2, 3, D]), sb("cst", [KT_CTX, 2, 3, 6])
            cmvs = sb("cmvs", [KT_CTX, 2, 3, 2])
        block = stk.enter_context(nc.Block())

        def kept(un):
            return un.n if moe else un.par

        def passed(sem, p):
            return sg[sem], p * per_pass[sem] + (sg.left[sem] + per_pass[sem])

        def is_first(un):
            return isinstance(un.pair, int) and un.pair * 2 + un.k == 0

        def run(eng, step_of, weights=None):
            def items(seq, un, renew=False):
                for st, k, whose in seq:
                    if renew and st == "YA" and k == 0:
                        weights("w1", 1, NTILES - 1)
                    if whose == "u":
                        step_of(st, k, un, un.n, un, 0, is_first(un), npass == 1)
                    else:
                        nxt = un.step(1)
                        step_of(st, k, None, None, nxt, None, False, None)
            if weights:
                weights("w1", 0, None)
                weights("w2", 0, None)
            for st, k, whose in steps:
                if whose == "n":
                    step_of(st, k, None, None, Unit(0, 0), None, True, None)
            with_next = steps
            alone = [st for st in steps if st[2] == "u"]

            def body(un, prev, nxt):
                items(with_next if nxt else alone, un, renew=not nxt and weights and moe)
            units(eng, NTILES, body)
            if not moe:
                return
            if weights:
                weights("w2", 1, NTILES - 1)

            def one_pass(pair, k, last):
                p = pair * 2 + k
                first_step = pair * (2 * NTILES) + k * NTILES

                def tile_steps(tile, renew=False):
                    for st, kk in unit_steps:
                        if renew and st == "YA" and kk == 0:
                            weights("w1", p + 1, first_step + (NTILES - 1))
                        step_of(st, kk, first_step + tile, tile, None, p, False, last)
                with eng.Fori(0, NTILES - 1) as tile:
                    tile_steps(tile)
                tile_steps(NTILES - 1, renew=weights and not last)
                if weights and not last:
                    weights("w2", p + 1, first_step + (NTILES - 1))
            with eng.Fori(0, E // 2 - 1) as pair:
                one_pass(pair, 1, False)
                one_pass(pair, 2, False)
            one_pass(E // 2 - 1, 1, False)
            one_pass(E // 2 - 1, 2, True)

        @block.sync
        def _(sp):
            for p in range(npass):
                if p:
                    sp.wait_ge(*passed("w1_lo", p - 1))
                sp.dma_start(w1f[:, :, :], t["ffn_w1"][w0 + p]).then_inc(sg["w1_in"], 16)
                if p:
                    sp.wait_ge(*passed("w2_lo", p - 1))
                sp.dma_start(w2f[:, :, :], t["ffn_w2"][w0 + p]).then_inc(sg["w2_in"], 16)
                if moe and p == 0:
                    sp.dma_start(gw[:, :, :], t["gate_w"]).then_inc(sg["gates_in"], 16)
                    for r in range(2):
                        sp.dma_start(ctok[:, r, :, :], t["ctx"][r].rearrange("(k p) d -> p k d", p=KT_CTX))\
                          .then_inc(sg[f"c_in{r}"], 16)
                    with sp.Fori(0, B // 2 - 1) as pair:
                        for r in range(2):
                            sp.wait_ge(sg["c_moments"], pair * 2 + (sg.left["c_moments"] + 1 + r))
                            sp.dma_start(ctok[:, r, :, :],
                                         t["ctx"][pair * 2 + (2 + r)].rearrange("(k p) d -> p k d", p=KT_CTX))\
                              .then_inc(sg[f"c_in{r}"], 16)

        @block.gpsimd
        def _(pool):
            if not moe:
                def step_of(st, k, step, tile, un, p, first, last):
                    if st == "XN":
                        pool.wait_ge(*sg.at("f_xn", un, k + 1))
                        b = un.n * TB + k
                        pool.tensor_tensor(x[:, b, :], x[:, b, :], m["row"][0:S, ROWS[name + "b2"], :], ALU.add)\
                            .then_inc(sg["f_xbias"], 1)
                run(pool, step_of)

        @block.scalar
        def _(act):
            def step_of(st, k, step, tile, un, p, first, last):
                if st == "XT":
                    act.wait_ge(*sg.at("f_xt_psum", un, k + 1))
                    if k >= 2 or not first:
                        act.wait_ge(*sg.at("f_lo", un, k - 1))
                        if moe:
                            act.wait_ge(*sg.at("lg_psum", un, k - 1))
                    for c in range(C):
                        ins = act.activation(hnf[:, k % 2, c, :], PS[:, 6, c * S:(c + 1) * S],
                                             ACT.Identity, bias=0.0 if moe else col("b", c), scale=col("g", c))
                    ins.then_inc(sg["f_xt_sb"], 1)
                elif st == "GT":
                    act.wait_ge(*sg.at("gdiff", un))
                    act.activation(ge[:, :], gd[:, :], ACT.Exp).then_inc(sg["gexp"], 1)
                elif st == "H":
                    act.wait_ge(*sg.at("h_psum", step, k + 1))
                    if k >= 2 or not first:
                        act.wait_ge(*sg.at("h_lo", step, k - 1))
                    for dst in (hf[:, k % 2, :], hT[0][:, k, :]):
                        ins = act.activation(dst, PS[:, k % 4, 0:TOK], act_fn,
                                             bias=0.0 if moe else m["fb1"][:, w0 - 1 - E, k:k + 1])
                    ins.then_inc(sg["h_hi"], 1)
            reciprocal_root(None, act, sg, "rstd", None, root[:, :], None, vare[:, :])
            run(act, step_of)

        @block.vector
        def _(dve):
            def moments(un, r, first):
                n = un.n * (TB * 3) + r * 3
                sem = sg.sems[f"c_in{r % 2}"]
                wait_apart(dve, sg, (sem, un.n * 32 + (sg.left[f"c_in{r % 2}"] + 16 * (r // 2 + 1))))
                if r >= 2 or not first:
                    wait_apart(dve, sg, sg.at("c_kept", un, r - 1))
                for kt in range(3):
                    dve.bn_stats(cst[:, r % 2, kt, :], ctok[:, r % 2, kt, :]).then_inc(sg["c_stats"], 1)
                for kt in range(3):
                    wait_apart(dve, sg, sg.at("c_stats", un, 3 * r + kt + 1))
                    ins = dve.bn_aggr(cmvs[:, r % 2, kt, :], cst[:, r % 2, kt, :])
                ins.then_inc(sg["c_moments"], 1)
                wait_apart(dve, sg, sg.at("c_moments", un, r + 1))
                dve.tensor_copy(m["cmv"][:, bass.ds(n, 3), :], cmvs[:, r % 2, :, :]).then_inc(sg["c_kept"], 1)

            def tile_gates(un):
                dve.wait_ge(*sg.at("lg_psum", un))
                dve.tensor_copy(lgs[:, :, :].rearrange("p r e -> p (r e)"), PS[0:S, 7, 0:TB * E])\
                   .then_inc(sg["lg_sb"], 1)
                wait_apart(dve, sg, sg.at("lg_sb", un))
                for r in range(TB):
                    dve.max(top[:, r, :], lgs[:, r, :]).then_inc(sg["top"], 1)
                for r in range(TB):
                    wait_apart(dve, sg, sg.at("top", un, r + 1))
                    dve.max_index(topi[:, r, :], top[:, r, :], lgs[:, r, :]).then_inc(sg["topi"], 1)
                dve.tensor_tensor(gd[:, :], top[:, :, 1], top[:, :, 0], ALU.subtract).then_inc(sg["gdiff"], 1)
                for r in range(TB):
                    dve.wait_ge(*sg.at("topi", un, r + 1))
                    dve.tensor_copy(topf[:, r, :], topi[:, r, 0:2]).then_inc(sg["topf"], 1)
                dve.wait_ge(*sg.at("gexp", un))
                dve.tensor_scalar(gn[:, :], ge[:, :], 1.0, None, ALU.add).then_inc(sg["gden"], 1)
                dve.wait_ge(*sg.at("gden", un))
                dve.reciprocal(g1[:, :], gn[:, :]).then_inc(sg["grec"], 1)
                dve.wait_ge(*sg.at("grec", un))
                dve.tensor_tensor(g2[:, :], ge[:, :], g1[:, :], ALU.mult).then_inc(sg["gsec"], 1)
                dve.wait_ge(*sg.at("gsec", un))
                dve.wait_ge(*sg.at("topf", un))
                for r in range(TB):
                    dve.tensor_scalar(one[:, r, :], m["iota"][0:S, :], topf[:, r, 0:1], g1[:, r:r + 1], ALU.is_equal,
                                      ALU.mult)
                    dve.tensor_scalar(two[:, r, :], m["iota"][0:S, :], topf[:, r, 1:2], g2[:, r:r + 1], ALU.is_equal,
                                      ALU.mult).then_inc(sg["gtwo"], 1)
                for r in range(TB):
                    dve.wait_ge(*sg.at("gtwo", un, r + 1))
                    dve.tensor_tensor(gates[:, un.n * TB + r, :], one[:, r, :], two[:, r, :], ALU.add)\
                       .then_inc(sg["gates_set"], 1)

            def stats_after(step, tile, r, b, very_first):
                wait_apart(dve, sg, sg.at("y_acc", step, r + 1))
                if not very_first:
                    wait_apart(dve, sg, sg.at("x_kept", tile, r))
                token_stats(dve, sg, m, b, tile, r + 1)

            def step_of(st, k, step, tile, un, p, first, last):
                if st == "XN":
                    if first and k == 0:
                        dve.wait_ge(*sg.once("rstd", 6))
                    if k >= 2 or not first:
                        dve.wait_ge(*sg.at("f_xt_psum", un, k - 1))
                    b = un.n * TB + k
                    if moe:
                        dve.tensor_scalar(xn[:, k % 2, :], x[:, b, :], m["rs"][:, bass.ds(b, 1)], None, ALU.mult)\
                           .then_inc(sg["f_xn"], 1)
                    else:
                        dve.tensor_scalar(xn[:, k % 2, :], x[:, b, :], m["mv"][:, b, 0:1],
                                          m["rs"][:, bass.ds(b, 1)], ALU.subtract, ALU.mult)\
                           .then_inc(sg["f_xn"], 1)
                elif st == "XS":
                    high, low = (hn[i][:, kept(un), :, k * S:(k + 1) * S] for i in range(2))
                    wait_apart(dve, sg, sg.at("f_xt_sb", un, k + 1))
                    if not moe and k == 0 and not first and not is_first(un.step(-1)):
                        wait_apart(dve, sg, sg.at("h_psum", un.step(-2)))
                    dve.tensor_copy(high, hnf[:, k % 2, :, :]).then_inc(sg["f_hi"], 1)
                    dve.wait_ge(*sg.at("f_hi", un, k + 1))
                    dve.tensor_tensor(low, hnf[:, k % 2, :, :], high.bitcast(F32), ALU.subtract)\
                       .then_inc(sg["f_lo"], 1)
                elif st == "CM":
                    moments(un, k, first)
                elif st == "GT":
                    tile_gates(un)
                elif st == "HL":
                    dve.wait_ge(*sg.at("h_hi", step, k + 1))
                    dve.tensor_tensor(hT[1][:, k, :], hf[:, k % 2, :], hT[0][:, k, :].bitcast(F32), ALU.subtract)\
                       .then_inc(sg["h_lo"], 1)
                elif st == "YA":
                    b = tile * TB + k
                    y = PS[0:S, 4 + k % 2, 0:D]
                    dve.wait_ge(*sg.at("y_psum", step, k + 1))
                    if un:
                        if not moe:
                            dve.wait_ge(*sg.at("f_xbias", un, k + 1))
                        dve.tensor_tensor(x[:, b, :], y, x[:, b, :], ALU.add).then_inc(sg["y_acc"], 1)
                        if following and not moe:
                            stats_after(un, un, k, b, first and k == 0)
                    else:
                        if k == 0:
                            dve.wait_ge(*sg.at("gates_set", NTILES - 1))
                        dve.wait_ge(*sg.at("y_acc", step, k + 1 - TB * NTILES))
                        dve.scalar_tensor_tensor(x[:, b, :], y, gates[:, b, bass.ds(p - 1, 1)], x[:, b, :],
                                                 ALU.mult, ALU.add).then_inc(sg["y_acc"], 1)
                        if following and last:
                            stats_after(step, tile, k, b, is_first_tile(tile) and k == 0)

            def is_first_tile(tile):
                return False

            def weights(which, p, last_step):
                staged, (high, low), reader = ((w1f, w1, "h_psum") if which == "w1" else (w2f, w2, "y_psum"))
                dve.wait_ge(*passed(which + "_in", p))
                if last_step is not None:
                    dve.wait_ge(*sg.at(reader, last_step))
                dve.tensor_copy(high[:, :, :], staged[:, :, :]).then_inc(sg[which + "_hi"], 1)
                dve.wait_ge(*passed(which + "_hi", p))
                dve.tensor_tensor(low[:, :, :], staged[:, :, :], high[:, :, :].bitcast(F32), ALU.subtract)\
                   .then_inc(sg[which + "_lo"], 1)
            if moe:
                mean_square(dve, sg, m, sq[:, :])
            reciprocal_root(dve, None, sg, "rstd", sq[:, :] if moe else m["mv"][:, :, 1], root[:, :], m["rs"][:, :], vare[:, :])
            run(dve, step_of, weights)

        @block.tensor
        def _(pe):
            def step_of(st, k, step, tile, un, p, first, last):
                if st == "XT":
                    pe.wait_ge(*sg.at("f_xn", un, k + 1))
                    if k or not first:
                        pe.wait_ge(*sg.at("f_xt_sb", un, k))
                    for c in range(C):
                        ins = pe.transpose(PS[:, 6, c * S:(c + 1) * S], xn[:, k % 2, c * 128:(c + 1) * 128],
                                           ident[0:S, 0:S])
                    ins.then_inc(sg["f_xt_psum"], 1)
                elif st == "LG":
                    if first and k == 0:
                        pe.wait_ge(sg["gates_in"], 16)
                    elif k == 0:
                        pe.wait_ge(*sg.at("lg_sb", un.step(-1)))
                    pe.wait_ge(*sg.at("f_xt_sb", un, k + 1))
                    for c in range(C):
                        ins = pe.matmul(PS[0:S, 7, k * E:(k + 1) * E], hnf[:, k % 2, c, :], gw[:, c, :],
                                        start=c == 0, stop=c == C - 1)
                    ins.then_inc(sg["lg_psum"], 1)
                elif st == "H":
                    if k == 0:
                        pe.wait_ge(*passed("w1_lo", p))
                        pe.wait_ge(*sg.at("f_lo", un if un else NTILES - 1))
                    if k >= 4 or not first:
                        pe.wait_ge(*sg.at("h_hi", step, k - 3))
                    place = kept(un) if un else tile
                    for c in range(C):
                        ws = [w[:, c, k * 128:(k + 1) * 128] for w in w1]
                        ins = split_product(pe, PS[:, k % 4, 0:TOK], ws, [h[:, place, c, :] for h in hn],
                                            c == 0, c == C - 1)
                    ins.then_inc(sg["h_psum"], 1)
                elif st == "Y":
                    if k == 0:
                        pe.wait_ge(*passed("w2_lo", p))
                    if k >= 2 or not first:
                        pe.wait_ge(*sg.at("y_acc", step, k - 1))
                    for hc in range(HC):
                        if k == 0:
                            pe.wait_ge(*sg.at("h_lo", step, hc + 1))
                        ins = split_product(pe, PS[0:S, 4 + k % 2, 0:D], [h[:, hc, k * S:(k + 1) * S] for h in hT],
                                            [w[:, hc, :] for w in w2], hc == 0, hc == HC - 1)
                    ins.then_inc(sg["y_psum"], 1)
            run(pe, step_of)
    if not following:
        for s in ("x_stats", "x_moments", "x_kept"):
            per_tile.pop(s)
    sg.per = per_tile
    sg.end(NTILES, rstd=6, rstd_root=1, **(dict(msq=2, gates_in=16) if moe else {}))
    sg.per = per_step
    sg.end(npass * NTILES)
    sg.per = per_pass
    sg.end(npass)


def build_inputs(inputs):
    g = {k: np.asarray(v) for k, v in inputs.items()}
    f = np.float32

    def chunks(w):
        return w.reshape(-1, 128, w.shape[-1]).transpose(1, 0, 2)

    def cols(v):
        return v.reshape(-1, 128).T

    wt = {"L0": [g[f"L0_xattn_W{p}"].T for p in "qkvo"],
          "L1S": [g[f"L1_xattn_sa_w{p}"].T for p in "qkvo"],
          "L1C": [g[f"L1_xattn_ca_w{p}"].T for p in "qkvo"],
          "L2": [g[f"L2_xattn_w{p}"] for p in "qkvo"],
          "L3S": [g["L3_xattn_attn_qkv_w"][i * D:(i + 1) * D].T for i in range(3)] + [g["L3_xattn_attn_proj_w"].T],
          "L3C": [g[f"L3_xattn_{p}_w"].T for p in ("q", "k", "v", "ca_proj")]}
    qkv_b = g["L3_xattn_attn_qkv_b"]
    zero, one = np.zeros(D, f), np.ones(D, f)
    vec = {"L0g": g["L0_xattn_ln_gamma"], "L0b": g["L0_xattn_ln_beta"], "L0bq": g["L0_xattn_bq"],
           "L0bk": g["L0_xattn_bk"], "L1Sg": g["L1_xattn_norm1_w"], "L1Cg": g["L1_xattn_norm2_w"],
           "MOEg": g["L1_xattn_norm3_w"],
           "L2g": g["L2_xattn_ln1_g"], "L2b": g["L2_xattn_ln1_b"], "L2bq": g["L2_xattn_bq"], "L2bk": g["L2_xattn_bk"],
           "F2g": g["L2_xattn_ln2_g"], "F2b": g["L2_xattn_ln2_b"],
           "L3Sg": g["L3_xattn_ln1_g"], "L3Sb": g["L3_xattn_ln1_b"], "L3Sbq": qkv_b[0:D], "L3Sbk": qkv_b[D:2 * D],
           "L3Cg": g["L3_xattn_ln2_g"], "L3Cb": g["L3_xattn_ln2_b"], "L3Cbq": g["L3_xattn_q_b"],
           "L3Cbk": g["L3_xattn_k_b"], "F3g": g["L3_xattn_ln3_g"], "F3b": g["L3_xattn_ln3_b"]}
    rows = {"L0bv": g["L0_xattn_bv"], "L0bo": g["L0_xattn_bo"], "L2bv": g["L2_xattn_bv"], "L2bo": g["L2_xattn_bo"],
            "L3Sbv": qkv_b[2 * D:], "L3Sbo": g["L3_xattn_attn_proj_b"], "L3Cbv": g["L3_xattn_v_b"],
            "L3Cbo": g["L3_xattn_ca_proj_b"], "F2b2": g["L2_xattn_b2"], "F3b2": g["L3_xattn_proj_b"]}
    w1 = [g["L1_xattn_sh_w1"].T] + [w.T for w in g["L1_xattn_exp_w1"]] + [g["L2_xattn_w1"], g["L3_xattn_fc_w"].T]
    w2 = [g["L1_xattn_sh_w2"].T] + [w.T for w in g["L1_xattn_exp_w2"]] + [g["L2_xattn_w2"], g["L3_xattn_proj_w"].T]
    p = np.arange(128)
    hmask = np.stack([(p // 16 == e) * 1.0 for e in range(8)], 1)
    nmask = np.stack([((p == e) | (p == 8 + e)) * 1.0 for e in range(8)], 1)
    tri = np.tril(np.ones((S, S)))
    a = {
        "x": g["x"],
        "ctx": g["ctx_1024"],
        "ctxT": g["ctx_1024"].transpose(0, 2, 1).reshape(B, C, 128, SC).transpose(0, 2, 1, 3),
        "maskL1S": g["mask_BxSxS_ik0"], "maskTL1S": g["mask_BxSxS_ik0"].transpose(0, 2, 1),
        "maskL1C": g["mask_BxSxS2_if1"], "maskTL1C": g["mask_BxSxS2_if1"].transpose(0, 2, 1),
        "attn_w": np.stack([np.stack([chunks(w) for w in wt[n]], 1) for n in ATTN_NAMES], 0),
        "col": np.concatenate([cols(vec.get(n, zero)) for n in COLS], 1),
        "fb1": np.stack([cols(g["L2_xattn_b1"]), cols(g["L3_xattn_fc_b"])], 1),
        "row": np.stack([rows.get(n, zero) for n in ROWS], 0),
        "ident": np.eye(128, dtype=f), "hmask": hmask.astype(f), "nmask": nmask.astype(f),
        "causal": ((1 - tri) * NEG).astype(f), "causalT": (tri.T * KEEP).astype(f),
        "gate_w": chunks(g["L1_xattn_gate_w"].T),
        "ffn_w1": np.stack([chunks(w) for w in w1], 0),
        "ffn_w2": np.stack([chunks(w) for w in w2], 0),
    }
    return {k: np.ascontiguousarray(v) for k, v in a.items()}


def kernel(**inputs):
    import concourse.bacc as bacc
    from concourse.bass_utils import run_bass_kernel_spmd

    nc = bacc.Bacc("TRN2", target_bir_lowering=False, num_devices=1)
    arrays = build_inputs(inputs)
    t = {k: nc.dram_tensor(k + "_dram", v.shape, mybir.dt.from_np(v.dtype), kind="ExternalInput").ap()
         for k, v in arrays.items()}
    out = nc.dram_tensor("out_dram", (B, S, D), F32, kind="ExternalOutput").ap()
    build(nc, t, out)
    r = run_bass_kernel_spmd(nc, [{k + "_dram": v for k, v in arrays.items()}], core_ids=[0])
    return r.results[0]["out_dram"]
```
